# Optimizing a Trainium2 kernel written in Bass

```python
import numpy as np
import jax
import jax.numpy as jnp

def _softmax(x, axis=-1):
    return jax.nn.softmax(x, axis=axis)

def _gelu(x):
    return jax.nn.gelu(x, approximate=True)

def _silu(x):
    return jax.nn.silu(x)

def _sigmoid(x):
    return jax.nn.sigmoid(x)

def _layernorm(x, axis=-1, eps=1e-05):
    m = jnp.mean(x, axis=axis, keepdims=True)
    v = jnp.var(x, axis=axis, keepdims=True)
    return (x - m) / jnp.sqrt(v + eps)

def _scatter_add(tgt, idx, src, axis=0):
    return tgt.at[idx].add(src)

def _segment_sum(src, seg, n):
    return jax.ops.segment_sum(src, seg, n)
kernel_name = 'mk_perceiver_d2_seqx_r2_b63b6f'

def setup_inputs(seed: int=0):
    np.random.seed(seed)
    _w = jnp.asarray

    def _rec_inputs():
        import jax
        import jax.numpy as jnp
        _rk = jax.random.key(seed)
        x = 7.22e-05 + 1 * jax.random.normal(jax.random.fold_in(_rk, 1), (2, 128, 512), jnp.float32)
        _lenS = 128 - jax.random.randint(jax.random.fold_in(_rk, 7), (2,), 0, max(1, 128 // 4) + 1, jnp.int32)
        _lenS2 = 2048 - jax.random.randint(jax.random.fold_in(_rk, 8), (2,), 0, max(1, 2048 // 4) + 1, jnp.int32)
        _ctx_1024P = jax.random.normal(jax.random.fold_in(_rk, 11), (2, 16, 512), jnp.float32)
        _ctx_1024c = jax.random.dirichlet(jax.random.fold_in(_rk, 511), 0.3 * jnp.ones((16,), jnp.float32), (2, 2048))
        _ctx_1024t = jnp.einsum('bsk,bkd->bsd', _ctx_1024c, _ctx_1024P)
        _ctx_1024t = _ctx_1024t * jax.lax.rsqrt(jnp.mean(jnp.square(_ctx_1024t)) + 1e-12) * 0.953939
        ctx_1024 = 4.13588e-05 + 0.999923 * (_ctx_1024t + 0.3 * jax.random.normal(jax.random.fold_in(_rk, 611), (2, 2048, 512), jnp.float32))
        return (x, ctx_1024)
    x, ctx_1024 = _rec_inputs()

    def _L0_xattn_setup():
        import jax, jax.numpy as jnp
        import numpy as np
        N_HEAD, MODEL_DIM, KEY_DIM, VALUE_DIM = (16, 512, 64, 64)
        B, S = (4, 1024)
        EPS = 1e-05
        TEMP = float(np.sqrt(KEY_DIM))
        key = jax.random.key(seed)
        ks = jax.random.split(key, 12)
        d = {'query': jax.random.normal(ks[0], (B, S, MODEL_DIM), jnp.float32), 'key': jax.random.normal(ks[1], (B, S, MODEL_DIM), jnp.float32), 'value': jax.random.normal(ks[2], (B, S, MODEL_DIM), jnp.float32), 'Wq': jax.random.normal(ks[3], (MODEL_DIM, N_HEAD * KEY_DIM), jnp.float32) * np.sqrt(2.0 / (MODEL_DIM + KEY_DIM)), 'bq': jnp.zeros((N_HEAD * KEY_DIM,), jnp.float32), 'Wk': jax.random.normal(ks[4], (MODEL_DIM, N_HEAD * KEY_DIM), jnp.float32) * np.sqrt(2.0 / (MODEL_DIM + KEY_DIM)), 'bk': jnp.zeros((N_HEAD * KEY_DIM,), jnp.float32), 'Wv': jax.random.normal(ks[5], (MODEL_DIM, N_HEAD * VALUE_DIM), jnp.float32) * np.sqrt(2.0 / (MODEL_DIM + VALUE_DIM)), 'bv': jnp.zeros((N_HEAD * VALUE_DIM,), jnp.float32), 'Wo': jax.random.normal(ks[6], (N_HEAD * VALUE_DIM, MODEL_DIM), jnp.float32) * np.sqrt(2.0 / (N_HEAD * VALUE_DIM + MODEL_DIM)), 'bo': jnp.zeros((MODEL_DIM,), jnp.float32), 'ln_gamma': jnp.ones((MODEL_DIM,), jnp.float32), 'ln_beta': jnp.zeros((MODEL_DIM,), jnp.float32)}
        return d
    _L0_xattn_all = _L0_xattn_setup()
    _L0_xattn_in = {k: v for k, v in _L0_xattn_all.items() if k in ('Wq', 'bq', 'Wk', 'bk', 'Wv', 'bv', 'Wo', 'bo', 'ln_gamma', 'ln_beta')}
    del _L0_xattn_all

    def _L0_attn_setup():
        import jax, jax.numpy as jnp
        import numpy as np
        B, T, C, H = (2, 1024, 512, 16)
        DK = DV = C // H
        CONV_K = 4
        EPS = 1e-05

        def _causal_depthwise_conv(x, w):
            K = w.shape[1]
            xp = jnp.pad(x, ((0, 0), (K - 1, 0), (0, 0)))
            y = jax.lax.conv_general_dilated(xp.transpose(0, 2, 1), w[:, None, :], window_strides=(1,), padding='VALID', feature_group_count=w.shape[0])
            return y.transpose(0, 2, 1)

        def _l2norm(x):
            return x * jax.lax.rsqrt(jnp.sum(x * x, axis=-1, keepdims=True) + 1e-06)

        def _rope(x, rot_dim, base=10000.0):
            t = x.shape[2]
            half = rot_dim // 2
            inv_freq = base ** (-jnp.arange(half, dtype=jnp.float32) / half)
            ang = jnp.arange(t, dtype=jnp.float32)[:, None] * inv_freq[None, :]
            cos, sin = (jnp.cos(ang), jnp.sin(ang))
            x1 = x[..., :half]
            x2 = x[..., half:rot_dim]
            xpass = x[..., rot_dim:]
            return jnp.concatenate([x1 * cos - x2 * sin, x2 * cos + x1 * sin, xpass], axis=-1)
        key = jax.random.key(seed)
        ks = jax.random.split(key, 16)
        s = 0.02
        inp = {'x': jax.random.normal(ks[0], (B, T, C), jnp.float32), 'Wq': jax.random.normal(ks[1], (C, H * DK), jnp.float32) * s, 'Wk': jax.random.normal(ks[2], (C, H * DK), jnp.float32) * s, 'Wv': jax.random.normal(ks[3], (C, H * DV), jnp.float32) * s, 'Wo': jax.random.normal(ks[4], (H * DV, C), jnp.float32) * s, 'Wg': jax.random.normal(ks[5], (C, H * DV), jnp.float32) * s, 'Wgk': jax.random.normal(ks[6], (C, H), jnp.float32) * s, 'Wb': jax.random.normal(ks[7], (C, H), jnp.float32) * s, 'bb': jnp.zeros((H,), jnp.float32), 'A_log': jnp.log(jax.random.uniform(ks[8], (H,), jnp.float32, 0.5, 8.0)), 'conv_q_w': jax.random.normal(ks[10], (H * DK, CONV_K), jnp.float32) * 0.2, 'conv_k_w': jax.random.normal(ks[11], (H * DK, CONV_K), jnp.float32) * 0.2, 'conv_v_w': jax.random.normal(ks[12], (H * DV, CONV_K), jnp.float32) * 0.2, 'gnorm_w': jnp.ones((DV,), jnp.float32)}
        dt = jnp.exp(jax.random.uniform(ks[9], (H,), jnp.float32) * (np.log(0.1) - np.log(0.001)) + np.log(0.001))
        dt = jnp.clip(dt, 0.0001, None)
        inp['dt_bias'] = dt + jnp.log(-jnp.expm1(-dt))
        return inp
    _L0_attn_all = _L0_attn_setup()
    _L0_attn_in = {k: v for k, v in _L0_attn_all.items() if k in ('Wq', 'Wk', 'Wv', 'Wo', 'Wg', 'Wgk', 'Wb', 'bb', 'A_log', 'conv_q_w', 'conv_k_w', 'conv_v_w', 'gnorm_w', 'dt_bias')}
    del _L0_attn_all

    def _L0_ffn_setup():
        import jax, jax.numpy as jnp
        import numpy as np
        B, S, H = (4, 1024, 512)
        F = 2048
        E = 8
        JITTER_EPS = 0.01

        def _sparse_mixer_top2(scores, jitter_eps):
            vals, idx = jax.lax.top_k(scores, 2)
            neg_inf = -jnp.inf
            m1 = vals[:, :1]
            factor1 = jnp.maximum(jnp.abs(scores), m1)
            mask1 = (m1 - scores) / factor1 > 2 * jitter_eps
            p1 = jax.nn.softmax(jnp.where(mask1, neg_inf, scores), axis=-1)
            mult1 = jnp.take_along_axis(p1, idx[:, :1], axis=-1)[:, 0]
            m2 = vals[:, 1:2]
            factor2 = jnp.maximum(jnp.abs(scores), m2)
            mask2 = (m2 - scores) / factor2 > 2 * jitter_eps
            top1_onehot = jnp.arange(scores.shape[-1])[None, :] == idx[:, :1]
            s2 = jnp.where(top1_onehot, neg_inf, scores)
            p2 = jax.nn.softmax(jnp.where(mask2, neg_inf, s2), axis=-1)
            mult2 = jnp.take_along_axis(p2, idx[:, 1:2], axis=-1)[:, 0]
            return (mult1, mult2, idx)
        key = jax.random.key(seed)
        k0, k1, k2, k3, k4 = jax.random.split(key, 5)
        hidden_states = jax.random.normal(k0, (B, S, H), dtype=jnp.float32)
        gate_w = jax.random.normal(k1, (E, H), dtype=jnp.float32) * 0.02
        w1 = jax.random.normal(k2, (E, F, H), dtype=jnp.float32) * 0.02
        w2 = jax.random.normal(k3, (E, H, F), dtype=jnp.float32) * 0.02
        w3 = jax.random.normal(k4, (E, F, H), dtype=jnp.float32) * 0.02
        return {'hidden_states': hidden_states, 'gate_w': gate_w, 'w1': w1, 'w2': w2, 'w3': w3}
    _L0_ffn_all = _L0_ffn_setup()
    _L0_ffn_in = {k: v for k, v in _L0_ffn_all.items() if k in ('gate_w', 'w1', 'w2', 'w3')}
    del _L0_ffn_all

    def _L1_xattn_setup():
        import jax, jax.numpy as jnp
        import numpy as np
        N_HEAD = 16
        key = jax.random.key(seed)
        ks = jax.random.split(key, 5)
        b, l, d = (4, 1024, 512)
        dh = d // N_HEAD
        return {'q': jax.random.normal(ks[0], (b, l, d), dtype=jnp.float32), 'kv': jax.random.normal(ks[1], (b, l, d), dtype=jnp.float32), 'Wq': jax.random.normal(ks[2], (d, d), dtype=jnp.float32) * 0.02, 'Wkv': jax.random.normal(ks[3], (2 * dh, d), dtype=jnp.float32) * 0.02, 'Wc': jax.random.normal(ks[4], (d, d), dtype=jnp.float32) * 0.02}
    _L1_xattn_all = _L1_xattn_setup()
    _L1_xattn_in = {k: v for k, v in _L1_xattn_all.items() if k in ('Wq', 'Wkv', 'Wc')}
    del _L1_xattn_all

    def _L1_attn_setup():
        import jax, jax.numpy as jnp
        import numpy as np
        D_IN = 512
        D_ATT = 512
        D_OUT = 512
        N, S = (8, 2048)
        key = jax.random.key(seed)
        ks = jax.random.split(key, 5)
        sc_in = 1.0 / np.sqrt(D_IN)
        sc_att = 1.0 / np.sqrt(D_ATT)
        return {'x': jax.random.normal(ks[0], (N, S, D_IN), dtype=jnp.float32), 'Wq': jax.random.normal(ks[1], (D_IN, D_ATT), dtype=jnp.float32) * sc_in, 'bq': jnp.zeros((D_ATT,), dtype=jnp.float32), 'Wk': jax.random.normal(ks[2], (D_IN, D_ATT), dtype=jnp.float32) * sc_in, 'bk': jnp.zeros((D_ATT,), dtype=jnp.float32), 'Wv': jax.random.normal(ks[3], (D_IN, D_ATT), dtype=jnp.float32) * sc_in, 'bv': jnp.zeros((D_ATT,), dtype=jnp.float32), 'Wo': jax.random.normal(ks[4], (D_ATT, D_OUT), dtype=jnp.float32) * sc_att, 'bo': jnp.zeros((D_OUT,), dtype=jnp.float32)}
    _L1_attn_all = _L1_attn_setup()
    _L1_attn_in = {k: v for k, v in _L1_attn_all.items() if k in ('Wq', 'bq', 'Wk', 'bk', 'Wv', 'bv', 'Wo', 'bo')}
    del _L1_attn_all

    def _L1_ffn_setup():
        import jax, jax.numpy as jnp
        import numpy as np
        D_IN, D_HID = (512, 2048)

        def _ternary(key, shape):
            return jax.random.randint(key, shape, -1, 2).astype(jnp.float32)

        def _tlin(x, w, s):
            return jnp.einsum('bsi,oi->bso', x, w) * s
        key = jax.random.key(seed)
        ks = jax.random.split(key, 12)
        inv = lambda fan: 1.0 / np.sqrt(fan).astype(np.float32)
        return {'x': jax.random.normal(ks[0], (4, 1024, D_IN), dtype=jnp.float32), 'w1_w': _ternary(ks[1], (D_HID, D_IN)), 'w1_s': jax.random.uniform(ks[2], (D_HID,), dtype=jnp.float32) * inv(D_IN), 'w2_w': _ternary(ks[3], (D_HID, D_IN)), 'w2_s': jax.random.uniform(ks[4], (D_HID,), dtype=jnp.float32) * inv(D_IN), 'h1_w': _ternary(ks[5], (D_HID, D_HID)), 'h1_s': jax.random.uniform(ks[6], (D_HID,), dtype=jnp.float32) * inv(D_HID), 'h2_w': _ternary(ks[7], (D_HID, D_HID)), 'h2_s': jax.random.uniform(ks[8], (D_HID,), dtype=jnp.float32) * inv(D_HID), 'w3_w': _ternary(ks[9], (D_IN, D_HID)), 'w3_s': jax.random.uniform(ks[10], (D_IN,), dtype=jnp.float32) * inv(D_HID)}
    _L1_ffn_all = _L1_ffn_setup()
    _L1_ffn_in = {k: v for k, v in _L1_ffn_all.items() if k in ('w1_w', 'w1_s', 'w2_w', 'w2_s', 'h1_w', 'h1_s', 'h2_w', 'h2_s', 'w3_w', 'w3_s')}
    del _L1_ffn_all
    return {'x': x, 'ctx_1024': ctx_1024, 'L0_xattn_Wq': _L0_xattn_in['Wq'], 'L0_xattn_bq': _L0_xattn_in['bq'], 'L0_xattn_Wk': _L0_xattn_in['Wk'], 'L0_xattn_bk': _L0_xattn_in['bk'], 'L0_xattn_Wv': _L0_xattn_in['Wv'], 'L0_xattn_bv': _L0_xattn_in['bv'], 'L0_xattn_Wo': _L0_xattn_in['Wo'], 'L0_xattn_bo': _L0_xattn_in['bo'], 'L0_xattn_ln_gamma': _L0_xattn_in['ln_gamma'], 'L0_xattn_ln_beta': _L0_xattn_in['ln_beta'], 'L0_attn_Wq': _L0_attn_in['Wq'], 'L0_attn_Wk': _L0_attn_in['Wk'], 'L0_attn_Wv': _L0_attn_in['Wv'], 'L0_attn_Wo': _L0_attn_in['Wo'], 'L0_attn_Wg': _L0_attn_in['Wg'], 'L0_attn_Wgk': _L0_attn_in['Wgk'], 'L0_attn_Wb': _L0_attn_in['Wb'], 'L0_attn_bb': _L0_attn_in['bb'], 'L0_attn_A_log': _L0_attn_in['A_log'], 'L0_attn_conv_q_w': _L0_attn_in['conv_q_w'], 'L0_attn_conv_k_w': _L0_attn_in['conv_k_w'], 'L0_attn_conv_v_w': _L0_attn_in['conv_v_w'], 'L0_attn_gnorm_w': _L0_attn_in['gnorm_w'], 'L0_attn_dt_bias': _L0_attn_in['dt_bias'], 'L0_ffn_gate_w': _L0_ffn_in['gate_w'], 'L0_ffn_w1': _L0_ffn_in['w1'], 'L0_ffn_w2': _L0_ffn_in['w2'], 'L0_ffn_w3': _L0_ffn_in['w3'], 'L1_xattn_Wq': _L1_xattn_in['Wq'], 'L1_xattn_Wkv': _L1_xattn_in['Wkv'], 'L1_xattn_Wc': _L1_xattn_in['Wc'], 'L1_attn_Wq': _L1_attn_in['Wq'], 'L1_attn_bq': _L1_attn_in['bq'], 'L1_attn_Wk': _L1_attn_in['Wk'], 'L1_attn_bk': _L1_attn_in['bk'], 'L1_attn_Wv': _L1_attn_in['Wv'], 'L1_attn_bv': _L1_attn_in['bv'], 'L1_attn_Wo': _L1_attn_in['Wo'], 'L1_attn_bo': _L1_attn_in['bo'], 'L1_ffn_w1_w': _L1_ffn_in['w1_w'], 'L1_ffn_w1_s': _L1_ffn_in['w1_s'], 'L1_ffn_w2_w': _L1_ffn_in['w2_w'], 'L1_ffn_w2_s': _L1_ffn_in['w2_s'], 'L1_ffn_h1_w': _L1_ffn_in['h1_w'], 'L1_ffn_h1_s': _L1_ffn_in['h1_s'], 'L1_ffn_h2_w': _L1_ffn_in['h2_w'], 'L1_ffn_h2_s': _L1_ffn_in['h2_s'], 'L1_ffn_w3_w': _L1_ffn_in['w3_w'], 'L1_ffn_w3_s': _L1_ffn_in['w3_s']}

def reference(x, ctx_1024, L0_xattn_Wq, L0_xattn_bq, L0_xattn_Wk, L0_xattn_bk, L0_xattn_Wv, L0_xattn_bv, L0_xattn_Wo, L0_xattn_bo, L0_xattn_ln_gamma, L0_xattn_ln_beta, L0_attn_Wq, L0_attn_Wk, L0_attn_Wv, L0_attn_Wo, L0_attn_Wg, L0_attn_Wgk, L0_attn_Wb, L0_attn_bb, L0_attn_A_log, L0_attn_conv_q_w, L0_attn_conv_k_w, L0_attn_conv_v_w, L0_attn_gnorm_w, L0_attn_dt_bias, L0_ffn_gate_w, L0_ffn_w1, L0_ffn_w2, L0_ffn_w3, L1_xattn_Wq, L1_xattn_Wkv, L1_xattn_Wc, L1_attn_Wq, L1_attn_bq, L1_attn_Wk, L1_attn_bk, L1_attn_Wv, L1_attn_bv, L1_attn_Wo, L1_attn_bo, L1_ffn_w1_w, L1_ffn_w1_s, L1_ffn_w2_w, L1_ffn_w2_s, L1_ffn_h1_w, L1_ffn_h1_s, L1_ffn_h2_w, L1_ffn_h2_s, L1_ffn_w3_w, L1_ffn_w3_s):
    import jax
    import jax.numpy as jnp

    def _L0_xattn_ref(query, key, value, Wq, bq, Wk, bk, Wv, bv, Wo, bo, ln_gamma, ln_beta):
        import jax, jax.numpy as jnp
        import numpy as np
        N_HEAD, MODEL_DIM, KEY_DIM, VALUE_DIM = (16, 512, 64, 64)
        B, S = (4, 1024)
        EPS = 1e-05
        TEMP = float(np.sqrt(KEY_DIM))
        b, sq, _ = query.shape
        residual = query
        q = (query @ Wq + bq).reshape(b, sq, N_HEAD, KEY_DIM)
        k = (key @ Wk + bk).reshape(b, key.shape[1], N_HEAD, KEY_DIM)
        v = (value @ Wv + bv).reshape(b, value.shape[1], N_HEAD, VALUE_DIM)
        scores = jnp.einsum('bqhd,bkhd->bhqk', q, k) / TEMP
        attn = jax.nn.softmax(scores, axis=-1)
        out = jnp.einsum('bhqk,bkhd->bqhd', attn, v).reshape(b, sq, N_HEAD * VALUE_DIM)
        out = out @ Wo + bo + residual
        mu = jnp.mean(out, axis=-1, keepdims=True)
        var = jnp.var(out, axis=-1, keepdims=True)
        return (out - mu) * jax.lax.rsqrt(var + EPS) * ln_gamma + ln_beta

    def _L0_attn_ref(x, Wq, Wk, Wv, Wo, Wg, Wgk, Wb, bb, A_log, conv_q_w, conv_k_w, conv_v_w, gnorm_w, dt_bias):
        import jax, jax.numpy as jnp
        import numpy as np
        B, T, C, H = (2, 1024, 512, 16)
        DK = DV = C // H
        CONV_K = 4
        EPS = 1e-05

        def _causal_depthwise_conv(x, w):
            K = w.shape[1]
            xp = jnp.pad(x, ((0, 0), (K - 1, 0), (0, 0)))
            y = jax.lax.conv_general_dilated(xp.transpose(0, 2, 1), w[:, None, :], window_strides=(1,), padding='VALID', feature_group_count=w.shape[0])
            return y.transpose(0, 2, 1)

        def _l2norm(x):
            return x * jax.lax.rsqrt(jnp.sum(x * x, axis=-1, keepdims=True) + 1e-06)

        def _rope(x, rot_dim, base=10000.0):
            t = x.shape[2]
            half = rot_dim // 2
            inv_freq = base ** (-jnp.arange(half, dtype=jnp.float32) / half)
            ang = jnp.arange(t, dtype=jnp.float32)[:, None] * inv_freq[None, :]
            cos, sin = (jnp.cos(ang), jnp.sin(ang))
            x1 = x[..., :half]
            x2 = x[..., half:rot_dim]
            xpass = x[..., rot_dim:]
            return jnp.concatenate([x1 * cos - x2 * sin, x2 * cos + x1 * sin, xpass], axis=-1)
        b, t, c = x.shape
        q = jax.nn.silu(_causal_depthwise_conv(x @ Wq, conv_q_w))
        k = jax.nn.silu(_causal_depthwise_conv(x @ Wk, conv_k_w))
        v = jax.nn.silu(_causal_depthwise_conv(x @ Wv, conv_v_w))
        gk = -jnp.exp(A_log) * jax.nn.softplus(x @ Wgk + dt_bias)
        beta = jax.nn.sigmoid(x @ Wb + bb)
        q = q.reshape(b, t, H, DK).transpose(0, 2, 1, 3)
        k = k.reshape(b, t, H, DK).transpose(0, 2, 1, 3)
        v = v.reshape(b, t, H, DV).transpose(0, 2, 1, 3)
        q = _rope(_l2norm(q), DK // 2)
        k = _rope(_l2norm(k), DK // 2)

        def step(S, ins):
            q_t, k_t, v_t, g_t, b_t = ins
            S = S * jnp.exp(g_t)[..., None, None]
            pred = jnp.einsum('bhk,bhkv->bhv', k_t, S)
            delta = b_t[..., None] * (v_t - pred)
            S = S + k_t[..., None] * delta[..., None, :]
            o_t = jnp.einsum('bhk,bhkv->bhv', q_t, S)
            return (S, o_t)
        S0 = jnp.zeros((b, H, DK, DV), jnp.float32)
        ins = (q.transpose(2, 0, 1, 3), k.transpose(2, 0, 1, 3), v.transpose(2, 0, 1, 3), gk.transpose(1, 0, 2), beta.transpose(1, 0, 2))
        _, o = jax.lax.scan(step, S0, ins)
        o = o.transpose(1, 0, 2, 3)
        g = (x @ Wg).reshape(b, t, H, DV)
        o = o * jax.lax.rsqrt(jnp.mean(o * o, axis=-1, keepdims=True) + EPS)
        o = o * gnorm_w * jax.nn.silu(g)
        return o.reshape(b, t, H * DV) @ Wo

    def _L0_ffn_ref(hidden_states, gate_w, w1, w2, w3):
        import jax, jax.numpy as jnp
        import numpy as np
        B, S, H = (4, 1024, 512)
        F = 2048
        E = 8
        JITTER_EPS = 0.01

        def _sparse_mixer_top2(scores, jitter_eps):
            vals, idx = jax.lax.top_k(scores, 2)
            neg_inf = -jnp.inf
            m1 = vals[:, :1]
            factor1 = jnp.maximum(jnp.abs(scores), m1)
            mask1 = (m1 - scores) / factor1 > 2 * jitter_eps
            p1 = jax.nn.softmax(jnp.where(mask1, neg_inf, scores), axis=-1)
            mult1 = jnp.take_along_axis(p1, idx[:, :1], axis=-1)[:, 0]
            m2 = vals[:, 1:2]
            factor2 = jnp.maximum(jnp.abs(scores), m2)
            mask2 = (m2 - scores) / factor2 > 2 * jitter_eps
            top1_onehot = jnp.arange(scores.shape[-1])[None, :] == idx[:, :1]
            s2 = jnp.where(top1_onehot, neg_inf, scores)
            p2 = jax.nn.softmax(jnp.where(mask2, neg_inf, s2), axis=-1)
            mult2 = jnp.take_along_axis(p2, idx[:, 1:2], axis=-1)[:, 0]
            return (mult1, mult2, idx)
        Bv, Sv, Hv = hidden_states.shape
        x = hidden_states.reshape(-1, Hv)
        scores = x @ gate_w.T
        mult1, mult2, idx = _sparse_mixer_top2(scores, JITTER_EPS)
        out = jnp.zeros_like(x)
        for e in range(E):
            w_tok = mult1 * (idx[:, 0] == e) + mult2 * (idx[:, 1] == e)
            h = jax.nn.silu(x @ w1[e].T) * (x @ w3[e].T)
            out = out + w_tok[:, None] * (h @ w2[e].T)
        return out.reshape(Bv, Sv, Hv)

    def _L1_xattn_ref(q, kv, Wq, Wkv, Wc):
        import jax, jax.numpy as jnp
        import numpy as np
        N_HEAD = 16
        b, l, d = q.shape
        h = N_HEAD
        dh = d // h
        qp = jnp.einsum('bld,ed->ble', q, Wq)
        scores = jnp.einsum('bld,bmd->blm', qp, kv)
        idx = jnp.argmax(scores, axis=-1)
        mem = jnp.take_along_axis(kv, idx[..., None], axis=1)
        mkv = jnp.einsum('bld,ed->ble', mem, Wkv)
        mk, mv = jnp.split(mkv, 2, axis=-1)
        qh = qp.reshape(b, l, h, dh).transpose(0, 2, 1, 3)
        scale = 1.0 / np.sqrt(dh).astype(np.float32)
        logits = jnp.einsum('bhld,bmd->bhlm', qh, mk) * scale
        attn = jax.nn.softmax(logits, axis=-1)
        out = jnp.einsum('bhlm,bmd->bhld', attn, mv)
        out = out.transpose(0, 2, 1, 3).reshape(b, l, d)
        return jnp.einsum('bld,ed->ble', out, Wc)

    def _L1_attn_ref(x, Wq, bq, Wk, bk, Wv, bv, Wo, bo):
        import jax, jax.numpy as jnp
        import numpy as np
        D_IN = 512
        D_ATT = 512
        D_OUT = 512
        N, S = (8, 2048)
        query = jnp.einsum('nsd,dh->nsh', x, Wq) + bq
        keyp = jnp.einsum('nsd,dh->nsh', x, Wk) + bk
        value = jnp.einsum('nsd,dh->nsh', x, Wv) + bv
        fmap = lambda t: jax.nn.elu(t) + 1.0
        Q = fmap(query)
        K = fmap(keyp)
        KV = jnp.sum(K * value, axis=1)
        Ksum = jnp.sum(K, axis=1)
        Z = 1.0 / (Q * Ksum[:, None, :] + 1e-06)
        V = Q * KV[:, None, :] * Z
        out = jnp.einsum('nsh,ho->nso', V, Wo) + bo
        return jax.nn.gelu(out)

    def _L1_ffn_ref(x, w1_w, w1_s, w2_w, w2_s, h1_w, h1_s, h2_w, h2_s, w3_w, w3_s):
        import jax, jax.numpy as jnp
        import numpy as np
        D_IN, D_HID = (512, 2048)

        def _ternary(key, shape):
            return jax.random.randint(key, shape, -1, 2).astype(jnp.float32)

        def _tlin(x, w, s):
            return jnp.einsum('bsi,oi->bso', x, w) * s
        h = jax.nn.silu(_tlin(x, w1_w, w1_s)) * _tlin(x, w2_w, w2_s)
        h = jax.nn.gelu(_tlin(h, h1_w, h1_s), approximate=False)
        h = jax.nn.gelu(_tlin(h, h2_w, h2_s), approximate=False)
        return _tlin(h, w3_w, w3_s)
    x = x + _L0_xattn_ref(_layernorm(x, axis=-1), ctx_1024, ctx_1024, L0_xattn_Wq, L0_xattn_bq, L0_xattn_Wk, L0_xattn_bk, L0_xattn_Wv, L0_xattn_bv, L0_xattn_Wo, L0_xattn_bo, L0_xattn_ln_gamma, L0_xattn_ln_beta)
    x = x + _L0_attn_ref(_layernorm(x, axis=-1), L0_attn_Wq, L0_attn_Wk, L0_attn_Wv, L0_attn_Wo, L0_attn_Wg, L0_attn_Wgk, L0_attn_Wb, L0_attn_bb, L0_attn_A_log, L0_attn_conv_q_w, L0_attn_conv_k_w, L0_attn_conv_v_w, L0_attn_gnorm_w, L0_attn_dt_bias)
    x = x + _L0_ffn_ref(_layernorm(x, axis=-1), L0_ffn_gate_w, L0_ffn_w1, L0_ffn_w2, L0_ffn_w3)
    x = x + _L1_xattn_ref(_layernorm(x, axis=-1), ctx_1024, L1_xattn_Wq, L1_xattn_Wkv, L1_xattn_Wc)
    x = x + _L1_attn_ref(_layernorm(x, axis=-1), L1_attn_Wq, L1_attn_bq, L1_attn_Wk, L1_attn_bk, L1_attn_Wv, L1_attn_bv, L1_attn_Wo, L1_attn_bo)
    x = x + _L1_ffn_ref(_layernorm(x, axis=-1), L1_ffn_w1_w, L1_ffn_w1_s, L1_ffn_w2_w, L1_ffn_w2_s, L1_ffn_h1_w, L1_ffn_h1_s, L1_ffn_h2_w, L1_ffn_h2_s, L1_ffn_w3_w, L1_ffn_w3_s)
    return x

_drawn_inputs = setup_inputs


def setup_inputs(seed=0):
    import zlib

    import numpy as np

    out = dict(_drawn_inputs(seed))
    spreads = {'L0_xattn_bq': (0.0, 0.1),
     'L0_xattn_bk': (0.0, 0.1),
     'L0_xattn_bv': (0.0, 0.1),
     'L0_xattn_bo': (0.0, 0.1),
     'L0_xattn_ln_gamma': (1.0, 0.2),
     'L0_xattn_ln_beta': (0.0, 0.1),
     'L0_attn_bb': (0.0, 0.1),
     'L0_attn_gnorm_w': (1.0, 0.2),
     'L1_attn_bq': (0.0, 0.1),
     'L1_attn_bk': (0.0, 0.1),
     'L1_attn_bv': (0.0, 0.1),
     'L1_attn_bo': (0.0, 0.1)}
    factors = {}
    for name, (base, spread) in spreads.items():
        noise = np.random.default_rng([zlib.crc32(name.encode()), seed]).standard_normal(out[name].shape)
        drawn = base * np.exp(spread * noise) if base else spread * noise
        out[name] = jnp.asarray(drawn.astype(out[name].dtype))
    for name, factor in factors.items():
        out[name] = (out[name] * factor).astype(out[name].dtype)
    return out
```

```python
from contextlib import ExitStack

import numpy as np

import concourse.bass as bass
from concourse import mybir

P = 128
B = 2
D = 512
C = D // P
T = B * P
CTX = 2048
KB = CTX // 512
KC = CTX // P
H = 16
PAIRS = H // 2
DK = D // H
TAPS = 4
E = 8
F = 2048
FQ = F // 512
FC = F // P
BLK = 2048
RING = 4
QKVW = 3 * C * P
LEVELS = 7
JITTER = 0.01
EPS = 1e-5

BLK_XO = 0
BLK_MIX = 2
BLK_MOE = 7
BLK_X1 = BLK_MOE + E * FQ * 3
BLK_LIN = BLK_X1 + 2
BLK_W12 = BLK_LIN + 4
BLK_H1 = BLK_W12 + 2 * FQ
BLK_H2 = BLK_H1 + FC
BLK_W3 = BLK_H2 + FC
NBLK = BLK_W3 + FQ

CONST_NAMES = ["ident", "le", "gt", "low0", "low1", "low2", "low3", "low4", "low5", "low6", "up0",
               "ropec", "ropes", "partner", "group", "iota"]
CONST = {n: P * i for i, n in enumerate(CONST_NAMES)}
NCONST = P * len(CONST_NAMES)
ROWS = {"x0_bo": (0, D), "x0_gamma": (D, D), "x0_beta": (2 * D, D), "mix_dt": (3 * D, H),
        "mix_bb": (3 * D + H, H), "mix_alog": (3 * D + 2 * H, H), "mix_gnorm": (3 * D + 3 * H, DK),
        "lin_bo": (3 * D + 3 * H + DK, D), "w3_s": (4 * D + 3 * H + DK, D)}
NROWS = 5 * D + 3 * H + DK
COLS = {"x0_bq": (0, PAIRS), "x0_bk": (8, PAIRS), "x0_bv": (16, PAIRS), "convw": (24, 3 * C * TAPS),
        "lin_b": (72, 3 * C), "w1_s": (84, FC), "w2_s": (100, FC), "h1_s": (116, FC), "h2_s": (132, FC),
        "headmask": (148, 4), "rank": (152, E)}
NCOLS = 152 + E
SMALL = {"mix_gb": (0, 2 * H), "gate": (C * 2 * H, E), "x1_k": (C * (2 * H + E), P), "x1_v": (C * (2 * H + E + P), DK)}
NSMALL = C * (2 * H + E + P + DK)

ARENA = 32768


def constants():
    r, c = np.indices((P, P))
    t = {"ident": r == c, "le": r <= c, "gt": r > c}
    for l in range(LEVELS):
        m = 1 << l
        pair = (r // (2 * m) == c // (2 * m)) & (r // m != c // m)
        t[f"low{l}"] = pair & (r > c)
        if l == 0:
            t["up0"] = pair & (r < c)
    half = DK // 4
    d = np.arange(P) % DK
    inv = (np.float32(10000.0) ** (-np.arange(half, dtype=np.float32) / np.float32(half))).astype(np.float32)
    ang = (np.arange(P, dtype=np.float32)[None, :] * inv[d % half][:, None]).astype(np.float32)
    rot = (d < 2 * half)[:, None]
    t["ropec"] = np.where(rot, np.cos(ang), 1.0)
    t["ropes"] = np.where(rot, np.sin(ang), 0.0)
    dm, dk = c % DK, r % DK
    t["partner"] = (r // DK == c // DK) * ((dm < half) * (dk == dm + half) * -1.0
                                           + ((dm >= half) & (dm < 2 * half)) * (dk == dm - half))
    t["group"] = r // DK == c // DK
    t["iota"] = c
    return np.concatenate([t[n].astype(np.float32) for n in CONST_NAMES], axis=1)


def build(nc, x, ctxT, ctx_rows, qkv, stream, small, cols, rows, consts, out):
    fp32, u32 = mybir.dt.float32, mybir.dt.uint32
    ALU = mybir.AluOpType
    ACT = mybir.ActivationFunctionType
    AX = mybir.AxisListType
    ds = bass.ds

    with ExitStack() as ctx:
        def sb(name, shape, dt=fp32):
            return ctx.enter_context(nc.sbuf_tensor(name, shape, dt))

        def sem(name):
            return ctx.enter_context(nc.semaphore(name))

        x_res = sb("x_res", [P, B, D])
        xn = sb("xn", [P, B, D])
        xnT = sb("xnT", [P, C, T])
        cst = sb("cst", [P, NCONST])
        row = sb("row", [P, NROWS])
        col = sb("col", [P, NCOLS])
        sml = sb("sml", [P, NSMALL])
        ring = [sb(f"ring{i}", [P, BLK]) for i in range(RING)]
        arena = sb("arena", [P, ARENA])
        stats = sb("stats", [P, B, 6])
        mv = sb("mv", [P, B, 2])
        std = sb("std", [P, B])
        rstd = sb("rstd", [P, B])
        epst = sb("epst", [P, 2])
        psum = ctx.enter_context(nc.psum_tensor("psum", [P, 8, 512], fp32))

        def C_(name, w=P):
            return cst[:, CONST[name]:CONST[name] + w]

        def R_(name):
            a, w = ROWS[name]
            return row[:, a:a + w]

        def K_(name, i=0, n=1):
            return col[:, COLS[name][0] + i:COLS[name][0] + i + n]

        def S_(name):
            a, w = SMALL[name]
            return sml[:, a:a + C * w].rearrange("p (c n) -> p c n", c=C)

        def view(at, *shape):
            n = int(np.prod(shape))
            assert at + n <= ARENA, (at, shape)
            v = arena[:, at:at + n]
            if len(shape) == 1:
                return v
            letters = "abcd"[:len(shape)]
            return v.rearrange(f"p ({' '.join(letters)}) -> p {' '.join(letters)}",
                               **dict(zip(letters[:-1], shape[:-1])))

        def block(k):
            return ring[k % RING][:, :].rearrange("p (c n) -> p c n", c=C)

        def per_row(ap, n):
            return ap.unsqueeze(1).to_broadcast([P, n, ap.shape[-1]])

        def per_elem(ap, n):
            return ap.unsqueeze(2).to_broadcast([P, ap.shape[-1], n])

        loaded = sem("loaded")
        pair_arrived = sem("pair_arrived")
        ctx_arrived = [sem(f"ctx_arrived{b}") for b in range(B)]
        blk_arrived = [sem(f"blk_arrived{i}") for i in range(RING)]
        blk_used = sem("blk_used")
        x_final = sem("x_final")
        stored = sem("stored")
        v_chain = sem("v_chain")
        a_chain = sem("a_chain")

        ln_var = sem("ln_var")
        ln_std = sem("ln_std")
        xn_ready = sem("xn_ready")
        xnT_filled = sem("xnT_filled")
        xnT_v = sem("xnT_v")
        xnT_a = sem("xnT_a")

        NLOADS = 5

        def dma_block(sp, k_dram, k_static, used=None):
            if used is not None:
                sp.wait_ge(blk_used, used)
            sp.dma_start(ring[k_static % RING][:, :], stream[k_dram] if isinstance(k_dram, int) else stream[k_dram].rearrange("a p n -> (a p) n")).then_inc(blk_arrived[k_static % RING], 16)

        def need(pe, k, more_rounds=None):
            turn = 16 * (k // RING + 1)
            pe.wait_ge(blk_arrived[k % RING], turn if more_rounds is None else more_rounds * 16 + turn)

        def link(dve, ins, count=[0]):
            count[0] += 1
            ins.then_inc(v_chain, 1)
            dve.wait_ge(v_chain, count[0])

        def link_a(act, ins, count=[0]):
            count[0] += 1
            ins.then_inc(a_chain, 1)
            act.wait_ge(a_chain, count[0])

        def norm_dve(dve, n):
            for b in range(B):
                ins = nc.vector.bn_stats(stats[:, b, :], x_res[:, b, :])
                if b == B - 1:
                    link(dve, ins)
            for b in range(B):
                nc.vector.bn_aggr(mv[:, b, :], stats[:, b, :]).then_inc(ln_var, 1)
            dve.wait_ge(ln_std, n + 1)
            link(dve, nc.vector.reciprocal(rstd[:, :], std[:, :]))
            for b in range(B):
                nc.vector.tensor_scalar(xn[:, b, :], x_res[:, b, :], mv[:, b, 0:1], rstd[:, b:b + 1],
                                        ALU.subtract, ALU.mult).then_inc(xn_ready, 1)
            dve.wait_ge(xnT_filled, 2 * n + 1)
            nc.vector.tensor_copy(xnT[:, :, 0:P], psum[:, 0, :].rearrange("p (c t) -> p c t", c=C)).then_inc(xnT_v, 1)

        def norm_act(act, n):
            act.wait_ge(ln_var, 2 * n + 2)
            nc.scalar.activation(std[:, :], mv[:, :, 1], ACT.Sqrt, bias=epst[:, 0:1]).then_inc(ln_std, 1)
            act.wait_ge(xnT_filled, 2 * n + 2)
            nc.scalar.copy(xnT[:, :, P:T], psum[:, 1, :].rearrange("p (c t) -> p c t", c=C)).then_inc(xnT_a, 1)

        def norm_pe(pe, n):
            for b in range(B):
                pe.wait_ge(xn_ready, 2 * n + b + 1)
                for c in range(C):
                    last = nc.tensor.transpose(psum[:, b, c * P:(c + 1) * P], xn[:, b, c * P:(c + 1) * P], C_("ident"))
                last.then_inc(xnT_filled, 1)
            pe.wait_ge(xnT_v, n + 1)
            pe.wait_ge(xnT_a, n + 1)

        ctxT_sb = [view(b * C * CTX, C, CTX) for b in range(B)]
        o = B * C * CTX
        kT = [view(o + b * CTX, CTX) for b in range(B)]
        o += B * CTX
        vv = [view(o + b * CTX, KC, P) for b in range(B)]
        o += B * CTX
        pbuf = view(o, CTX)
        o += CTX
        pT = view(o, KC, P)
        o += CTX
        qz = [view(o + b * 2 * P, 2, P) for b in range(B)]
        o += B * 2 * P
        attnT = view(o, PAIRS, T)
        o += PAIRS * T
        pairw = sb("pairw", [P, 3, C, P])
        nmax = sb("nmax", [P, 2])
        rsum = sb("rsum", [P, 1])
        rinv = sb("rinv", [P, 1])

        qz_clear = sem("qz_clear")
        kq_filled = sem("kq_filled")
        kq_evac = sem("kq_evac")
        v_filled = sem("v_filled")
        v_evac = sem("v_evac")
        scores_ready = sem("scores_ready")
        nmax_ready = sem("nmax_ready")
        rinv_ready = sem("rinv_ready")
        exp_ready = sem("exp_ready")
        p_ready = sem("p_ready")
        pT_filled = sem("pT_filled")
        pT_v = sem("pT_v")
        pT_a = sem("pT_a")
        pv_done = sem("pv_done")
        head_done = sem("head_done")
        attn_ready = sem("attn_ready")
        x0_filled = sem("x0_filled")
        x0_std = sem("x0_std")
        x0_var = sem("x0_var")

        def project_k(pe, b, j, kb, first=False):
            if not first:
                pe.wait_ge(kq_evac, 5 * j + kb)
            for c in range(C):
                last = nc.tensor.matmul(psum[:, 4, :], pairw[:, 1, c, :], ctxT_sb[b][:, c, kb * 512:(kb + 1) * 512],
                                        start=c == 0, stop=c == C - 1)
            last.then_inc(kq_filled, 1)

        def project_v(pe, b, j, kb, first=False):
            if not first:
                pe.wait_ge(v_evac, 4 * j + kb)
            for q in range(4):
                kc = 4 * kb + q
                for c in range(C):
                    last = nc.tensor.matmul(psum[:, 5, q * P:(q + 1) * P], ctxT_sb[b][:, c, kc * P:(kc + 1) * P],
                                            pairw[:, 2, c, :], start=c == 0, stop=c == C - 1)
            last.then_inc(v_filled, 1)

        def project_q(pe, b, j):
            pe.wait_ge(kq_evac, 5 * j + 4)
            for c in range(C):
                last = nc.tensor.matmul(psum[:, 4, 0:P], pairw[:, 0, c, :], xnT[:, c, b * P:(b + 1) * P],
                                        start=c == 0, stop=c == C - 1)
            last.then_inc(kq_filled, 1)

        def project_half(pe, b, j, half):
            for kb in (2 * half, 2 * half + 1):
                project_k(pe, b, j, kb)
                project_v(pe, b, j, kb)
            if half:
                project_q(pe, b, j)

        def attend_pe(pe, b, j, h, between):
            u = 2 * j + h
            pe.wait_ge(kq_evac, 5 * j + 5)
            for kb in range(KB):
                last = nc.tensor.matmul(psum[:, kb, :], qz[b][:, h, :], kT[b][:, kb * 512:(kb + 1) * 512],
                                        start=True, stop=True)
            last.then_inc(scores_ready, 1)
            between()
            pe.wait_ge(p_ready, u + 1)
            for kb in range(KB):
                for q in range(4):
                    kc = 4 * kb + q
                    last = nc.tensor.transpose(psum[:, kb, q * P:(q + 1) * P], pbuf[:, kc * P:(kc + 1) * P], C_("ident"))
                last.then_inc(pT_filled, 1)
            if h == 0:
                pe.wait_ge(v_evac, 4 * j + 4)
            for kb in range(KB):
                if kb == 0:
                    pe.wait_ge(pT_v, 2 * u + 2)
                if kb == 2:
                    pe.wait_ge(pT_a, 2 * u + 2)
                for q in range(4):
                    kc = 4 * kb + q
                    last = nc.tensor.matmul(psum[64 * h:64 * h + 64, 6 + h, 0:P], vv[b][:, kc, 64 * h:64 * h + 64],
                                            pT[:, kc, :], start=kc == 0, stop=kc == KC - 1)
            last.then_inc(pv_done, 1)

        def pair_pe(pe, hp, last_pair=False):
            j = hp * 2
            attend_pe(pe, 0, j, 0, lambda: project_half(pe, 1, j + 1, 0))
            attend_pe(pe, 0, j, 1, lambda: project_half(pe, 1, j + 1, 1))
            if last_pair:
                attend_pe(pe, 1, j + 1, 0, lambda: None)
                attend_pe(pe, 1, j + 1, 1, lambda: None)
                return
            def next_weights():
                pe.wait_ge(pair_arrived, hp * 16 + 32)
                project_half(pe, 0, j + 2, 0)
            attend_pe(pe, 1, j + 1, 0, next_weights)
            attend_pe(pe, 1, j + 1, 1, lambda: project_half(pe, 0, j + 2, 1))

        def cross0_pe(pe):
            norm_pe(pe, 0)
            pe.wait_ge(pair_arrived, 16)
            pe.wait_ge(ctx_arrived[0], 16)
            for kb in range(KB):
                project_k(pe, 0, 0, kb, first=kb == 0)
                project_v(pe, 0, 0, kb, first=kb == 0)
            project_q(pe, 0, 0)
            pe.wait_ge(ctx_arrived[1], 16)
            with pe.Fori(0, PAIRS - 1) as hp:
                pair_pe(pe, hp)
            pair_pe(pe, PAIRS - 1, last_pair=True)
            pe.wait_ge(attn_ready, 1)
            need(pe, BLK_XO)
            need(pe, BLK_XO + 1)
            for b in range(B):
                for hp in range(PAIRS):
                    last = nc.tensor.matmul(psum[:, b, :], attnT[:, hp, b * P:(b + 1) * P],
                                            block(BLK_XO + hp // C)[:, hp % C, :], start=hp == 0, stop=hp == PAIRS - 1)
                    if b == 1 and hp == C - 1:
                        last.then_inc(blk_used, 1)
                last.then_inc(x0_filled if b == 0 else blk_used, 1)

        def evac_k_dve(dve, b, j, kb, hp):
            dve.wait_ge(kq_filled, 5 * j + kb + 1)
            nc.vector.tensor_scalar(kT[b][:, kb * 512:(kb + 1) * 512], psum[:, 4, :], K_dyn("x0_bk", hp), None,
                                    ALU.add).then_inc(kq_evac, 1)

        def K_dyn(name, i):
            return col[:, ds(i + COLS[name][0], 1)]

        def evac_q_dve(dve, b, j, hp):
            dve.wait_ge(kq_filled, 5 * j + 5)
            for h in range(2):
                lo = 64 * h
                ins = nc.vector.tensor_scalar(qz[b][lo:lo + 64, h, :], psum[lo:lo + 64, 4, 0:P],
                                              col[lo:lo + 64, ds(hp + COLS["x0_bq"][0], 1)], None, ALU.add)
            ins.then_inc(kq_evac, 1)

        def evac_half_dve(dve, b, j, hp, half):
            for kb in (2 * half, 2 * half + 1):
                evac_k_dve(dve, b, j, kb, hp)
            if half:
                evac_q_dve(dve, b, j, hp)

        def attend_dve(dve, b, j, h, hp, between):
            u = 2 * j + h
            dve.wait_ge(scores_ready, u + 1)
            nc.vector.reduce_max(nmax[:, 0:1], psum[:, 0:KB, :].rearrange("p a n -> p (a n)"), AX.X).then_inc(nmax_ready, 1)
            dve.wait_ge(nmax_ready, 2 * u + 1)
            nc.vector.tensor_scalar(nmax[:, 1:2], nmax[:, 0:1], -0.125, None, ALU.mult).then_inc(nmax_ready, 1)
            dve.wait_ge(exp_ready, u + 1)
            nc.vector.reciprocal(rinv[:, :], rsum[:, :]).then_inc(rinv_ready, 1)
            dve.wait_ge(rinv_ready, u + 1)
            nc.vector.tensor_scalar(pbuf, pbuf, rinv[:, 0:1], None, ALU.mult).then_inc(p_ready, 1)
            between()
            for kb in range(2):
                dve.wait_ge(pT_filled, 4 * u + kb + 1)
                nc.vector.tensor_copy(pT[:, 4 * kb:4 * kb + 4, :], psum[:, kb, :].rearrange("p (q t) -> p q t", q=4)).then_inc(pT_v, 1)
            dve.wait_ge(pv_done, u + 1)
            nc.vector.tensor_copy(attnT[64 * h:64 * h + 64, ds(hp, 1), b * P:(b + 1) * P],
                                  psum[64 * h:64 * h + 64, 6 + h, 0:P].unsqueeze(1)).then_inc(head_done, 1)

        def pair_dve(dve, hp, last_pair=False):
            j = hp * 2
            attend_dve(dve, 0, j, 0, hp, lambda: evac_half_dve(dve, 1, j + 1, hp, 0))
            attend_dve(dve, 0, j, 1, hp, lambda: evac_half_dve(dve, 1, j + 1, hp, 1))
            attend_dve(dve, 1, j + 1, 0, hp, (lambda: None) if last_pair else lambda: evac_half_dve(dve, 0, j + 2, hp + 1, 0))
            attend_dve(dve, 1, j + 1, 1, hp, (lambda: None) if last_pair else lambda: evac_half_dve(dve, 0, j + 2, hp + 1, 1))

        def cross0_dve(dve):
            nc.vector.memset(epst[:, 0:1], EPS)
            nc.vector.memset(epst[:, 1:2], 1e-6)
            for b in range(B):
                link(dve, nc.vector.memset(qz[b], 0.0))
            dve.wait_ge(loaded, 16 * NLOADS)
            norm_dve(dve, 0)
            evac_half_dve(dve, 0, 0, 0, 0)
            evac_half_dve(dve, 0, 0, 0, 1)
            with dve.Fori(0, PAIRS - 1) as hp:
                pair_dve(dve, hp)
            pair_dve(dve, PAIRS - 1, last_pair=True)
            dve.wait_ge(head_done, 2 * H)
            for hp in range(PAIRS):
                ins = nc.vector.tensor_scalar(attnT[:, hp, :], attnT[:, hp, :], K_("x0_bv", hp), None, ALU.add)
            ins.then_inc(attn_ready, 1)
            y = pbuf[:, 0:B * D].rearrange("p (b n) -> p b n", b=B)
            for b in range(B):
                if b == 0:
                    dve.wait_ge(x0_filled, 1)
                else:
                    dve.wait_ge(blk_used, BLK_XO + 2)
                link(dve, nc.vector.tensor_tensor(y[:, b, :], psum[:, b, :], xn[:, b, :], ALU.add))
            link(dve, nc.vector.tensor_tensor(y, y, per_row(R_("x0_bo"), B), ALU.add))
            for b in range(B):
                link(dve, nc.vector.bn_stats(stats[:, b, :], y[:, b, :]))
                nc.vector.bn_aggr(mv[:, b, :], stats[:, b, :]).then_inc(x0_var, 1)
            dve.wait_ge(x0_std, 1)
            link(dve, nc.vector.reciprocal(rstd[:, :], std[:, :]))
            for b in range(B):
                link(dve, nc.vector.tensor_scalar(y[:, b, :], y[:, b, :], mv[:, b, 0:1], rstd[:, b:b + 1],
                                                  ALU.subtract, ALU.mult))
            link(dve, nc.vector.tensor_tensor(y, y, per_row(R_("x0_gamma"), B), ALU.mult))
            link(dve, nc.vector.tensor_tensor(y, y, per_row(R_("x0_beta"), B), ALU.add))
            link(dve, nc.vector.tensor_tensor(x_res[:, :, :], x_res[:, :, :], y, ALU.add))

        def evac_v_act(act, b, j, kb):
            act.wait_ge(v_filled, 4 * j + kb + 1)
            nc.scalar.copy(vv[b][:, 4 * kb:4 * kb + 4, :], psum[:, 5, :].rearrange("p (q t) -> p q t", q=4)).then_inc(v_evac, 1)

        def attend_act(act, b, j, h, between):
            u = 2 * j + h
            act.wait_ge(nmax_ready, 2 * u + 2)
            nc.scalar.activation(pbuf, psum[:, 0:KB, :].rearrange("p a n -> p (a n)"), ACT.Exp, bias=nmax[:, 1:2],
                                 scale=0.125, accum_out=rsum[:, 0:1]).then_inc(exp_ready, 1)
            between()
            for kb in range(2, 4):
                act.wait_ge(pT_filled, 4 * u + kb + 1)
                nc.scalar.copy(pT[:, 4 * kb:4 * kb + 4, :], psum[:, kb, :].rearrange("p (q t) -> p q t", q=4)).then_inc(pT_a, 1)

        def pair_act(act, hp, last_pair=False):
            j = hp * 2

            def values(b, jn, half):
                for kb in (2 * half, 2 * half + 1):
                    evac_v_act(act, b, jn, kb)
            attend_act(act, 0, j, 0, lambda: values(1, j + 1, 0))
            attend_act(act, 0, j, 1, lambda: values(1, j + 1, 1))
            attend_act(act, 1, j + 1, 0, lambda: None if last_pair else values(0, j + 2, 0))
            attend_act(act, 1, j + 1, 1, lambda: None if last_pair else values(0, j + 2, 1))

        def cross0_act(act):
            norm_act(act, 0)
            for kb in range(KB):
                evac_v_act(act, 0, 0, kb)
            with act.Fori(0, PAIRS - 1) as hp:
                pair_act(act, hp)
            pair_act(act, PAIRS - 1, last_pair=True)
            act.wait_ge(x0_var, 2)
            nc.scalar.activation(std[:, :], mv[:, :, 1], ACT.Sqrt, bias=epst[:, 0:1]).then_inc(x0_std, 1)

        BH = B * H
        G8 = BH // 4
        dec = view(0, BH, P)
        etm = dec
        gm = view(4096, BH, P)
        um = gm
        m1 = gm
        pm = view(8192, BH, P)
        at = view(12288, BH, P)
        xi = view(16384, BH, P)
        xt = view(20480, BH, P)
        xpad = view(24576, 3 * C, B, P + TAPS - 1)
        yc = view(24576 + 3 * C * B * (P + TAPS - 1), 3 * C, B, P)
        yc_flat = view(24576 + 3 * C * B * (P + TAPS - 1), 3 * C * B * P)
        vtok = view(24576 + 3 * C * B * (P + TAPS - 1) + 3 * C * T, B, D)
        sq = view(0, 4, 512)
        rn = view(4096, 4, 512)
        turn = view(8192, 2 * C * B, P)
        qk = view(12288, 2 * C, B, P)
        kz = view(16384, B, C, 4, P)
        qzm = view(20480, B, C, 4, P)
        wmix = view(24576, B, D)
        osb = view(24576 + B * D, B, D)
        osq = view(24576 + 2 * B * D, B, D)
        oT = view(24576 + 3 * B * D, C, T)
        gs = xn
        z = sb("z", [P, B, 2 * H])
        za = sb("za", [P, B, H])
        zl = sb("zl", [P, B, H])
        gdec = sb("gdec", [P, B, H])
        beta = sb("beta", [P, B, H])
        alog = sb("alog", [P, H])
        oss = sb("oss", [P, BH])
        orn = sb("orn", [P, BH])

        mix_proj = sem("mix_proj")
        mix_evac = sem("mix_evac")
        mix_gb = sem("mix_gb")
        mix_z = sem("mix_z")
        mix_za = sem("mix_za")
        mix_zl = sem("mix_zl")
        mix_beta = sem("mix_beta")
        mix_gs = sem("mix_gs")
        conv = sem("conv")
        pad_clear = sem("pad_clear")
        mix_silu = sem("mix_silu")
        sq_ready = sem("sq_ready")
        ss_filled = sem("ss_filled")
        ss_root = sem("ss_root")
        qkn_ready = sem("qkn_ready")
        turn_filled = sem("turn_filled")
        vtok_filled = sem("vtok_filled")
        vtok_ready = sem("vtok_ready")
        gm_ready = sem("gm_ready")
        dec_filled = sem("dec_filled")
        dec_exp = sem("dec_exp")
        masked_ready = sem("masked_ready")
        kk_filled = sem("kk_filled")
        u_ready = sem("u_ready")
        at_filled = sem("at_filled")
        at_ready = sem("at_ready")
        x_upd = sem("x_upd")
        et_ready = sem("et_ready")
        m1_filled = sem("m1_filled")
        m1_ready = sem("m1_ready")
        xx_filled = sem("xx_filled")
        w_filled = sem("w_filled")
        w_ready = sem("w_ready")
        o_filled = sem("o_filled")
        oss_ready = sem("oss_ready")
        oss_root = sem("oss_root")
        on_ready = sem("on_ready")
        oT_filled = sem("oT_filled")
        oT_ready = sem("oT_ready")

        def four(ap, g):
            return ap[:, 4 * g:4 * g + 4, :]

        def bank4(i):
            return psum[:, i, :].rearrange("p (a t) -> p a t", a=4)

        def mixer_pe(pe):
            norm_pe(pe, 1)
            for m in range(3):
                need(pe, BLK_MIX + m)
                for cc in range(C):
                    n = C * m + cc
                    for c in range(C):
                        last = nc.tensor.matmul(psum[:, 2 + n // 2, (n % 2) * T:(n % 2) * T + T],
                                                block(BLK_MIX + m)[:, c, cc * P:(cc + 1) * P], xnT[:, c, :],
                                                start=c == 0, stop=c == C - 1)
                    last.then_inc(blk_used if cc == C - 1 else mix_proj, 1)
            need(pe, BLK_MIX + 3)
            for b in range(B):
                for c in range(C):
                    last = nc.tensor.matmul(psum[:, b, :], xnT[:, c, b * P:(b + 1) * P], block(BLK_MIX + 3)[:, c, :],
                                            start=c == 0, stop=c == C - 1)
            last.then_inc(blk_used, 1)
            pe.wait_ge(mix_evac, 1)
            for b in range(B):
                for c in range(C):
                    last = nc.tensor.matmul(psum[:, 2, b * 2 * H:(b + 1) * 2 * H], xnT[:, c, b * P:(b + 1) * P],
                                            S_("mix_gb")[:, c, :], start=c == 0, stop=c == C - 1)
            last.then_inc(mix_gb, 1)
            pe.wait_ge(mix_silu, 1)
            for b in range(B):
                for cc in range(C):
                    last = nc.tensor.transpose(psum[:, 6 + b, cc * P:(cc + 1) * P], yc[:, 2 * C + cc, b, :], C_("ident"))
                last.then_inc(vtok_filled, 1)
            pe.wait_ge(sq_ready, 1)
            for i in range(4):
                last = nc.tensor.matmul(psum[:, 2 + i, :], C_("group"), sq[:, i, :], start=True, stop=True)
            last.then_inc(ss_filled, 1)
            pe.wait_ge(qkn_ready, 1)
            for i in range(4):
                last = nc.tensor.matmul(psum[:, 2 + i, :], C_("partner"), yc_flat[:, i * 512:(i + 1) * 512],
                                        start=True, stop=True)
            last.then_inc(turn_filled, 1)
            pe.wait_ge(gm_ready, 1)
            pe.wait_ge(vtok_ready, 2)
            pe.wait_ge(mix_gs, 1)
            for g in range(G8):
                nc.tensor.matmul(psum[:, g, :], C_("gt"), four(gm, g), start=True, stop=True).then_inc(dec_filled, 1)
            pe.wait_ge(masked_ready, 4)
            for g in range(G8):
                b, cc = g // C, g % C
                if g < 4:
                    pe.wait_ge(dec_exp, 2 * g + 2)
                else:
                    pe.wait_ge(u_ready, 2 * (g - 4) + 2)
                for i, src in enumerate((kz, qzm)):
                    nc.tensor.matmul(psum[:, 2 * (g % 4) + i, :], qk[:, C + cc, b, :], src[:, b, cc, :, :],
                                     start=True, stop=True).then_inc(kk_filled, 1)
            pe.wait_ge(u_ready, 2 * G8)
            for g in range(G8):
                for i in range(4):
                    last = nc.tensor.transpose(psum[:, g, i * P:(i + 1) * P], um[:, 4 * g + i, :], C_("ident"))
                last.then_inc(at_filled, 1)
            with pe.Fori(0, LEVELS - 1) as l:
                def merge_first(g):
                    pe.wait_ge(et_ready, l * G8 + (g + 1))
                    pe.wait_ge(x_upd, l * G8 + (g + 1))
                    if g >= 2:
                        pe.wait_ge(m1_ready, l * G8 + (g - 1))
                    for i in range(4):
                        last = nc.tensor.matmul(psum[:, g % 2, i * P:(i + 1) * P], etm[:, 4 * g + i, :],
                                                xi[:, 4 * g + i, :], start=True, stop=True)
                    last.then_inc(m1_filled, 1)

                def merge_second(g):
                    pe.wait_ge(m1_ready, l * G8 + (g + 1))
                    pe.wait_ge(x_upd, l * G8 + (G8 + g - 1 if g >= 2 else g + 7))
                    for i in range(4):
                        nc.tensor.matmul(psum[:, 2 + g % 2, i * P:(i + 1) * P], xt[:, 4 * g + i, :],
                                         m1[:, 4 * g + i, :], start=True, stop=True)
                    for i in range(4):
                        last = nc.tensor.matmul(psum[:, 4 + g % 2, i * P:(i + 1) * P], m1[:, 4 * g + i, :],
                                                xt[:, 4 * g + i, :], start=True, stop=True)
                    last.then_inc(xx_filled, 1)
                merge_first(0)
                merge_first(1)
                for g in range(G8):
                    merge_second(g)
                    if g + 2 < G8:
                        merge_first(g + 2)
            pe.wait_ge(x_upd, G8 * LEVELS)
            for b in range(B):
                for h in range(H):
                    last = nc.tensor.matmul(psum[:, b, h * DK:(h + 1) * DK], xi[:, b * H + h, :],
                                            vtok[:, b, h * DK:(h + 1) * DK], start=True, stop=True)
                last.then_inc(w_filled, 1)
            for b in range(B):
                pe.wait_ge(w_ready, b + 1)
                for h in range(H):
                    last = nc.tensor.matmul(psum[:, 2 + b, h * DK:(h + 1) * DK], pm[:, b * H + h, :],
                                            wmix[:, b, h * DK:(h + 1) * DK], start=True, stop=True)
                last.then_inc(o_filled, 1)
            pe.wait_ge(on_ready, 1)
            for b in range(B):
                for c in range(C):
                    last = nc.tensor.transpose(psum[:, 4 + b, c * P:(c + 1) * P], osb[:, b, c * P:(c + 1) * P], C_("ident"))
                last.then_inc(oT_filled, 1)
            need(pe, BLK_MIX + 4)
            pe.wait_ge(oT_ready, 2)
            for b in range(B):
                for c in range(C):
                    last = nc.tensor.matmul(psum[:, 6 + b, :], oT[:, c, b * P:(b + 1) * P], block(BLK_MIX + 4)[:, c, :],
                                            start=c == 0, stop=c == C - 1)
            last.then_inc(blk_used, 1)

        def mixer_act(act):
            norm_act(act, 1)
            act.wait_ge(pad_clear, 1)
            for i in range(3 * C // 2):
                m = i // 2
                if i % 2:
                    act.wait_ge(blk_used, BLK_MIX + m + 1)
                else:
                    act.wait_ge(mix_proj, 3 * m + 2)
                nc.scalar.copy(xpad[:, 2 * i:2 * i + 2, :, TAPS - 1:].rearrange("p n b t -> p (n b) t"),
                               bank4(2 + i)).then_inc(mix_evac, 1)
            act.wait_ge(blk_used, BLK_MIX + 4)
            nc.scalar.activation(gs[:, :, :], psum[:, 0:2, :], ACT.Silu).then_inc(mix_gs, 1)
            act.wait_ge(conv, 12 * TAPS)
            nc.scalar.activation(yc_flat, yc_flat, ACT.Silu).then_inc(mix_silu, 1)
            act.wait_ge(mix_z, 2)
            nc.scalar.activation(beta[:, :, :], z[:, :, H:], ACT.Sigmoid).then_inc(mix_beta, 1)
            link_a(act, nc.scalar.activation(zl[:, :, :], za[:, :, :], ACT.Exp, scale=-1.0))
            link_a(act, nc.scalar.activation(alog[:, :], R_("mix_alog"), ACT.Exp))
            nc.scalar.activation(zl[:, :, :], zl[:, :, :], ACT.Ln, bias=1.0).then_inc(mix_zl, 1)
            for b in range(B):
                act.wait_ge(vtok_filled, b + 1)
                nc.scalar.copy(vtok[:, b, :], psum[:, 6 + b, :]).then_inc(vtok_ready, 1)
            act.wait_ge(ss_filled, 1)
            nc.scalar.activation(rn, psum[:, 2:6, :], ACT.Sqrt, bias=epst[:, 1:2]).then_inc(ss_root, 1)
            for g in range(G8):
                act.wait_ge(dec_filled, g + 1)
                nc.scalar.activation(four(dec, g), bank4(g), ACT.Exp).then_inc(dec_exp, 1)
            for g in range(G8):
                act.wait_ge(at_filled, g + 1)
                nc.scalar.copy(four(at, g), bank4(g)).then_inc(at_ready, 1)
            with act.Fori(0, LEVELS - 1) as l:
                for g in range(G8):
                    act.wait_ge(m1_filled, l * G8 + (g + 1))
                    nc.scalar.copy(four(m1, g), bank4(g % 2)).then_inc(m1_ready, 1)
            for b in range(B):
                act.wait_ge(w_filled, b + 1)
                nc.scalar.copy(wmix[:, b, :], psum[:, b, :]).then_inc(w_ready, 1)
            act.wait_ge(oss_ready, 1)
            nc.scalar.activation(orn[:, :], oss[:, :], ACT.Sqrt, bias=epst[:, 0:1], scale=1.0 / DK).then_inc(oss_root, 1)
            for b in range(B):
                act.wait_ge(oT_filled, b + 1)
                nc.scalar.copy(oT[:, :, b * P:(b + 1) * P], psum[:, 4 + b, :].rearrange("p (c t) -> p c t", c=C)).then_inc(oT_ready, 1)

        def mixer_dve(dve):
            norm_dve(dve, 1)
            nc.vector.memset(xpad[:, :, :, 0:TAPS - 1], 0.0).then_inc(pad_clear, 1)
            for tap in range(TAPS):
                for n in range(3 * C):
                    w = K_("convw", n * TAPS + tap)
                    src = xpad[:, n, :, tap:tap + P]
                    if tap == 0:
                        dve.wait_ge(mix_evac, n // 2 + 1)
                        nc.vector.tensor_scalar(yc[:, n, :, :], src, w, None, ALU.mult).then_inc(conv, 1)
                    else:
                        dve.wait_ge(conv, 12 * (tap - 1) + n + 1)
                        nc.vector.scalar_tensor_tensor(yc[:, n, :, :], src, w, yc[:, n, :, :], ALU.mult, ALU.add).then_inc(conv, 1)
            dve.wait_ge(mix_gb, 1)
            dtbb = row[:, ROWS["mix_dt"][0]:ROWS["mix_dt"][0] + 2 * H]
            nc.vector.tensor_tensor(z[:, :, :], psum[:, 2, 0:B * 2 * H].rearrange("p (b n) -> p b n", b=B),
                                    per_row(dtbb, B), ALU.add).then_inc(mix_z, 1)
            dve.wait_ge(mix_z, 1)
            nc.vector.scalar_tensor_tensor(za[:, :, :], z[:, :, 0:H], -1.0, z[:, :, 0:H], ALU.mult, ALU.max).then_inc(mix_z, 1)
            dve.wait_ge(mix_silu, 1)
            qkflat = yc_flat[:, 0:2 * C * T].rearrange("p (a n) -> p a n", a=4)
            nc.vector.tensor_tensor(sq, qkflat, qkflat, ALU.mult).then_inc(sq_ready, 1)
            dve.wait_ge(mix_zl, 1)
            link(dve, nc.vector.scalar_tensor_tensor(gdec[:, :, :], z[:, :, 0:H], 0.0, zl[:, :, :], ALU.max, ALU.add))
            link(dve, nc.vector.scalar_tensor_tensor(gdec[:, :, :], gdec[:, :, :], -1.0, per_row(alog[:, :], B), ALU.mult, ALU.mult))
            dve.wait_ge(ss_root, 1)
            link(dve, nc.vector.reciprocal(rn, rn))
            nc.vector.tensor_tensor(qkflat, qkflat, rn, ALU.mult).then_inc(qkn_ready, 1)
            dve.wait_ge(qkn_ready, 1)
            qk16 = qk.rearrange("p n b t -> p (n b) t")
            y16 = yc_flat[:, 0:2 * C * T].rearrange("p (a n) -> p a n", a=2 * C * B)
            link(dve, nc.vector.tensor_tensor(qk16, y16, per_row(C_("ropec"), 2 * C * B), ALU.mult))
            dve.wait_ge(turn_filled, 1)
            link(dve, nc.vector.tensor_tensor(turn.rearrange("p (a n) t -> p a n t", a=4), psum[:, 2:6, :].rearrange("p a (n t) -> p a n t", n=4),
                                              C_("ropes").unsqueeze(1).unsqueeze(1).to_broadcast([P, 4, 4, P]), ALU.mult))
            link(dve, nc.vector.tensor_tensor(qk16, qk16, turn, ALU.add))
            gflat = gdec[:, :, :].rearrange("p b h -> p (b h)")
            bflat = beta[:, :, :].rearrange("p b h -> p (b h)")
            nc.vector.tensor_tensor(gm, per_row(C_("le"), BH), per_elem(gflat, P), ALU.mult).then_inc(gm_ready, 1)
            for b in range(B):
                for dst, n0 in ((kz, C), (qzm, 0)):
                    nc.vector.tensor_tensor(dst[:, b, :, :, :], qk[:, n0:n0 + C, b, :].unsqueeze(2).to_broadcast([P, C, 4, P]),
                                            K_("headmask", 0, 4).unsqueeze(1).unsqueeze(3).to_broadcast([P, C, 4, P]),
                                            ALU.mult).then_inc(masked_ready, 1)
            dve.wait_ge(mix_beta, 1)
            dve.wait_ge(dec_exp, G8)
            link(dve, nc.vector.tensor_tensor(dec, dec, per_elem(bflat, P), ALU.mult))
            link(dve, nc.vector.tensor_tensor(dec, dec, per_row(C_("le"), BH), ALU.mult))
            for g in range(G8):
                for i, dst in enumerate((um, pm)):
                    dve.wait_ge(kk_filled, 2 * g + i + 1)
                    nc.vector.tensor_tensor(four(dst, g), bank4(2 * (g % 4) + i), four(dec, g), ALU.mult).then_inc(u_ready, 1)
            dve.wait_ge(u_ready, 2 * G8)
            link(dve, nc.vector.tensor_tensor(xi, um, per_row(C_("up0"), BH), ALU.mult))
            link(dve, nc.vector.scalar_tensor_tensor(xi, xi, -1.0, per_row(C_("ident"), BH), ALU.mult, ALU.add))
            for g in range(G8):
                dve.wait_ge(at_ready, g + 1)
                link(dve, nc.vector.tensor_tensor(four(xt, g), four(at, g), per_row(C_("low0"), 4), ALU.mult))
                nc.vector.scalar_tensor_tensor(four(xt, g), four(xt, g), -1.0, per_row(C_("ident"), 4), ALU.mult, ALU.add).then_inc(x_upd, 1)
            with dve.Fori(0, LEVELS - 1) as l:
                mask = cst[:, ds(l * P + CONST["low1"], P)]
                for g in range(G8):
                    nc.vector.tensor_tensor(four(etm, g), four(at, g), per_row(mask, 4), ALU.mult).then_inc(et_ready, 1)
                for g in range(G8):
                    dve.wait_ge(xx_filled, l * G8 + (g + 1))
                    nc.vector.tensor_tensor(four(xi, g), four(xi, g), bank4(2 + g % 2), ALU.subtract)
                    nc.vector.tensor_tensor(four(xt, g), four(xt, g), bank4(4 + g % 2), ALU.subtract).then_inc(x_upd, 1)
            o32 = osb.rearrange("p b (h d) -> p (b h) d", h=H)
            q32 = osq.rearrange("p b (h d) -> p (b h) d", h=H)
            dve.wait_ge(o_filled, 2)
            link(dve, nc.vector.tensor_copy(osb, psum[:, 2:4, :]))
            link(dve, nc.vector.tensor_tensor(osq, osb, osb, ALU.mult))
            nc.vector.reduce_sum(oss[:, :], q32, AX.X).then_inc(oss_ready, 1)
            dve.wait_ge(oss_root, 1)
            link(dve, nc.vector.reciprocal(orn[:, :], orn[:, :]))
            link(dve, nc.vector.tensor_tensor(o32, o32, per_elem(orn[:, :], DK), ALU.mult))
            link(dve, nc.vector.tensor_tensor(o32, o32, per_row(R_("mix_gnorm"), BH), ALU.mult))
            nc.vector.tensor_tensor(osb, osb, gs[:, :, :], ALU.mult).then_inc(on_ready, 1)
            dve.wait_ge(blk_used, BLK_MIX + 5)
            link(dve, nc.vector.tensor_tensor(x_res[:, :, :], x_res[:, :, :], psum[:, 6:8, :], ALU.add))

        hid = [view(16384 + i * C * T, C, T) for i in range(2)]
        hsilu = view(16384 + 2 * C * T, C, T)
        acc = view(16384 + 3 * C * T, B, D)
        sc = sb("sc", [P, B, E])
        gt = {n: sb("gt_" + n, [P, B, E]) for n in ("abs", "rank", "top1", "top2", "rest", "weight")}
        gdist = sb("gdist", [P, 2, B, E])
        gkeep = sb("gkeep", [P, 2, B, E])
        gexp = sb("gexp", [P, 2, B, E])
        gm1 = sb("gm1", [P, B])
        gm2 = sb("gm2", [P, B])
        grm = sb("grm", [P, B])
        gsum = sb("gsum", [P, 2, B])
        wcur = sb("wcur", [P, B])
        posm = sb("posm", [P, B, E])
        overfull = sb("overfull", [P, 1], mybir.dt.int32)
        sel = view(16384, B, E, P)
        selw = view(18432, B, E, P)
        selT = view(20480, E, T)
        xgT = view(22528, C, E, P)
        shid = [view(26624 + i * C * P, C, P) for i in range(2)]
        ssilu = view(27648, C, P)
        yexp = view(28160, D)
        accT = view(28672, C, T)

        gate_filled = sem("gate_filled")
        gdist_ready = sem("gdist_ready")
        gexp_ready = sem("gexp_ready")
        up_filled = sem("up_filled")
        silu_ready = sem("silu_ready")
        hid_free = sem("hid_free")
        acc_upd = sem("acc_upd")
        wcur_ready = sem("wcur_ready")
        s_chain = sem("s_chain")
        chosen_ready = sem("chosen_ready")
        pos_filled = sem("pos_filled")
        overfull_known = sem("overfull_known")
        sel_ready = sem("sel_ready")
        xg_filled = sem("xg_filled")
        xg_ready = sem("xg_ready")
        selT_filled = sem("selT_filled")
        selT_ready = sem("selT_ready")
        scatter_filled = sem("scatter_filled")
        accT_filled = sem("accT_filled")
        moe_added = sem("moe_added")

        def experts_pe(pe):
            norm_pe(pe, 2)
            for b in range(B):
                for c in range(C):
                    last = nc.tensor.matmul(psum[:, 6, b * E:(b + 1) * E], xnT[:, c, b * P:(b + 1) * P],
                                            S_("gate")[:, c, :], start=c == 0, stop=c == C - 1)
            last.then_inc(gate_filled, 1)
            pe.wait_ge(chosen_ready, 1)
            chosen = gt["rest"]
            nc.tensor.matmul(psum[:, 7, 0:E], C_("le"), chosen[:, 0, :], start=True, stop=True)
            nc.tensor.matmul(psum[:, 7, E:2 * E], C_("le"), chosen[:, 1, :], start=True, stop=False)
            for o in (E, 2 * E):
                for i, w in enumerate(("le", "gt")):
                    last = nc.tensor.matmul(psum[:, 7, o:o + E], C_(w), chosen[:, 0, :],
                                            start=o == 2 * E and i == 0, stop=o == E and i == 1)
            for i, w in enumerate(("le", "gt")):
                last = nc.tensor.matmul(psum[:, 7, 2 * E:3 * E], C_(w), chosen[:, 1, :], start=False, stop=i == 1)
            last.then_inc(pos_filled, 1)
            pe.wait_ge(overfull_known, 1)
            most = pe.value_load(overfull[0:1, 0:1], min_val=0, max_val=T)
            with pe.If(most > P):
                dense_experts_pe(pe)
            with pe.Else():
                gathered_experts_pe(pe)

        def up_pe(pe, u, rounds, width, rhs, free):
            k = BLK_MOE + 3 * u
            need(pe, k, rounds)
            need(pe, k + 1, rounds)
            for f in range(4):
                pe.wait_ge(hid_free, free + (4 * u + f + 1))
                for i in range(2):
                    for c in range(C):
                        last = nc.tensor.matmul(psum[:, f, i * T:i * T + width], block(k + i)[:, c, f * P:(f + 1) * P],
                                                rhs(c), start=c == 0, stop=c == C - 1)
                    if f == 3:
                        last.then_inc(blk_used, 1)
                if f < 3:
                    last.then_inc(up_filled, 1)
            need(pe, k + 2, rounds)

        def dense_experts_pe(pe):
            with pe.Fori(0, E) as e:
                rounds = e * (3 * FQ // RING)
                for u in range(FQ):
                    up_pe(pe, u, rounds, T, lambda c: xnT[:, c, :], e * FC)
                    for f in range(4):
                        pe.wait_ge(hid_free, e * FC + (4 * u + f + 5))
                        if u == 0 and f == 0:
                            pe.wait_ge(acc_upd, e * B + 1)
                        for b in range(B):
                            last = nc.tensor.matmul(psum[:, 4 + b, :], hid[u % 2][:, f, b * P:(b + 1) * P],
                                                    block(BLK_MOE + 3 * u + 2)[:, f, :], start=u == 0 and f == 0,
                                                    stop=u == FQ - 1 and f == 3)
                    last.then_inc(blk_used, 1)

        def gathered_experts_pe(pe):
            pe.wait_ge(sel_ready, 1)
            for g in range(2):
                for c in range(C):
                    for b in range(B):
                        last = nc.tensor.matmul(psum[:, 4 * g + c, :], xn[:, b, c * P:(c + 1) * P],
                                                sel[:, b, 4 * g:4 * g + 4, :], start=b == 0, stop=b == B - 1)
                    last.then_inc(xg_filled, 1)
            pe.wait_ge(sel_ready, 2)
            pe.wait_ge(xg_ready, 4)
            for e in range(E):
                for b in range(B):
                    o = (e % 2) * T + b * P
                    last = nc.tensor.transpose(psum[:, e // 2, o:o + P], selw[:, b, e, :], C_("ident"))
                if e % 2:
                    last.then_inc(selT_filled, 1)
            pe.wait_ge(xg_ready, 8)
            pe.wait_ge(selT_ready, 4)
            with pe.Fori(0, E) as e:
                rounds = e * (3 * FQ // RING)
                for u in range(FQ):
                    up_pe(pe, u, rounds, P, lambda c: xgT[:, c, ds(e, 1), :], e * FC)
                    for f in range(4):
                        pe.wait_ge(hid_free, e * FC + (4 * u + f + 5))
                        if u == 0 and f == 0:
                            pe.wait_ge(acc_upd, e * 2 + 1)
                        last = nc.tensor.matmul(psum[:, 4, :], shid[u % 2][:, f, :], block(BLK_MOE + 3 * u + 2)[:, f, :],
                                                start=u == 0 and f == 0, stop=u == FQ - 1 and f == 3)
                    last.then_inc(blk_used, 1)
                pe.wait_ge(acc_upd, e * 2 + 2)
                for c in range(C):
                    last = nc.tensor.matmul(psum[:, 6 + c // 2, (c % 2) * T:(c % 2) * T + T], yexp[:, c * P:(c + 1) * P],
                                            selT[:, ds(e, 1), :], start=True, stop=True)
                last.then_inc(scatter_filled, 1)
            pe.wait_ge(acc_upd, 2 * E + 1)
            for b in range(B):
                for c in range(C):
                    last = nc.tensor.transpose(psum[:, b, c * P:(c + 1) * P], accT[:, c, b * P:(b + 1) * P], C_("ident"))
            last.then_inc(accT_filled, 1)

        def experts_act(act):
            norm_act(act, 2)
            act.wait_ge(gdist_ready, 1)
            nc.scalar.activation(gexp[:, :, :, :], gdist[:, :, :, :], ACT.Exp, scale=-1.0).then_inc(gexp_ready, 1)
            act.wait_ge(overfull_known, 1)
            most = act.value_load(overfull[0:1, 0:1], min_val=0, max_val=T)

            def silus(width, dst):
                with act.Fori(0, E) as e:
                    for u in range(FQ):
                        for f in range(4):
                            if f < 3:
                                act.wait_ge(up_filled, e * 12 + (3 * u + f + 1))
                            else:
                                act.wait_ge(blk_used, e * 12 + (BLK_MOE + 3 * u + 2))
                            nc.scalar.activation(dst[:, f, :], psum[:, f, 0:width], ACT.Silu).then_inc(silu_ready, 1)
            with act.If(most > P):
                silus(T, hsilu)
            with act.Else():
                for n in range(8):
                    act.wait_ge(xg_filled, n + 1)
                    nc.scalar.copy(xgT[:, n % 4, 4 * (n // 4):4 * (n // 4) + 4, :], bank4(n)).then_inc(xg_ready, 1)
                silus(P, ssilu)

        def gates_dve(dve):
            g = {k: v[:, :, :] for k, v in gt.items()}
            s = sc[:, :, :]
            tt = nc.vector.tensor_tensor
            stt = nc.vector.scalar_tensor_tensor
            rank = per_row(K_("rank", 0, E), B)
            dve.wait_ge(gate_filled, 1)
            link(dve, nc.vector.tensor_copy(s, psum[:, 6, 0:B * E].rearrange("p (b e) -> p b e", b=B)))
            link(dve, stt(g["abs"], s, -1.0, s, ALU.mult, ALU.max))
            m = (gm1[:, :], gm2[:, :])

            def choose(values, best, chosen):
                link(dve, nc.vector.reduce_max(best, values, AX.X))
                link(dve, tt(g["rank"], values, per_elem(best, E), ALU.is_equal))
                link(dve, tt(g["rank"], g["rank"], rank, ALU.mult))
                link(dve, nc.vector.reduce_max(grm[:, :], g["rank"], AX.X))
                link(dve, tt(chosen, g["rank"], per_elem(grm[:, :], E), ALU.is_equal))
            choose(s, m[0], g["top1"])
            link(dve, stt(g["rest"], g["top1"], -3.0e38, s, ALU.mult, ALU.add))
            choose(g["rest"], m[1], g["top2"])
            for i in range(2):
                link(dve, tt(gdist[:, i, :, :], per_elem(m[i], E), s, ALU.subtract))
                link(dve, tt(gkeep[:, i, :, :], per_elem(m[i], E), g["abs"], ALU.max))
                link(dve, stt(gkeep[:, i, :, :], gkeep[:, i, :, :], 2 * JITTER, gdist[:, i, :, :], ALU.mult, ALU.is_ge))
            link(dve, tt(g["rest"], gkeep[:, 1, :, :], g["top1"], ALU.mult))
            link(dve, tt(gkeep[:, 1, :, :], gkeep[:, 1, :, :], g["rest"], ALU.subtract))
            nc.vector.tensor_scalar(gdist[:, :, :, :], gdist[:, :, :, :], 0.0, None, ALU.max).then_inc(gdist_ready, 1)
            tt(g["rest"], g["top1"], g["top2"], ALU.add).then_inc(chosen_ready, 1)
            dve.wait_ge(gexp_ready, 1)
            link(dve, tt(gexp[:, :, :, :], gexp[:, :, :, :], gkeep[:, :, :, :], ALU.mult))
            link(dve, nc.vector.reduce_sum(gsum[:, :, :], gexp[:, :, :, :], AX.X))
            link(dve, nc.vector.reciprocal(gsum[:, :, :], gsum[:, :, :]))
            link(dve, tt(g["top1"], g["top1"], per_elem(gsum[:, 0, :], E), ALU.mult))
            link(dve, tt(g["top2"], g["top2"], per_elem(gsum[:, 1, :], E), ALU.mult))
            tt(g["weight"], g["top1"], g["top2"], ALU.add).then_inc(acc_upd, 1)
            dve.wait_ge(pos_filled, 1)
            link(dve, tt(posm[:, :, :], psum[:, 7, 0:2 * E].rearrange("p (b e) -> p b e", b=B), g["rest"], ALU.mult))
            link(dve, nc.vector.tensor_scalar(posm[:, :, :], posm[:, :, :], -1.0, None, ALU.add))
            nc.vector.reduce_max(overfull[:, :], psum[:, 7, 2 * E:3 * E], AX.X).then_inc(overfull_known, 1)

        def experts_dve(dve):
            norm_dve(dve, 2)
            for i in range(4):
                nc.vector.memset(acc[:, i // 2, (i % 2) * T:(i % 2) * T + T], 0.0).then_inc(hid_free, 1)
            gates_dve(dve)
            dve.wait_ge(overfull_known, 1)
            most = dve.value_load(overfull[0:1, 0:1], min_val=0, max_val=T)
            with dve.If(most > P):
                dense_experts_dve(dve)
            with dve.Else():
                gathered_experts_dve(dve)
            dve.wait_ge(moe_added, 1)

        def dense_experts_dve(dve):
            with dve.Fori(0, E) as e:
                dve.wait_ge(acc_upd, e * B + 1)
                nc.vector.tensor_copy(wcur[:, :].unsqueeze(2), gt["weight"][:, :, ds(e, 1)]).then_inc(wcur_ready, 1)
                for u in range(FQ):
                    for f in range(4):
                        dve.wait_ge(silu_ready, e * FC + (4 * u + f + 1))
                        nc.vector.tensor_tensor(hid[u % 2][:, f, :], hsilu[:, f, :], psum[:, f, T:2 * T], ALU.mult).then_inc(hid_free, 1)
                dve.wait_ge(wcur_ready, e + 1)
                dve.wait_ge(blk_used, e * 12 + (BLK_MOE + 12))
                for b in range(B):
                    nc.vector.scalar_tensor_tensor(acc[:, b, :], psum[:, 4 + b, :], wcur[:, b:b + 1], acc[:, b, :],
                                                   ALU.mult, ALU.add).then_inc(acc_upd, 1)
            dve.wait_ge(acc_upd, B * E + 1)
            nc.vector.tensor_tensor(x_res[:, :, :], x_res[:, :, :], acc, ALU.add).then_inc(moe_added, 1)

        def gathered_experts_dve(dve):
            flat = lambda v: v.rearrange("p b e s -> p (b e) s")
            nc.vector.tensor_tensor(flat(sel), per_row(C_("iota"), B * E),
                                    per_elem(posm[:, :, :].rearrange("p b e -> p (b e)"), P), ALU.is_equal).then_inc(sel_ready, 1)
            dve.wait_ge(sel_ready, 1)
            nc.vector.tensor_tensor(flat(selw), flat(sel), per_elem(gt["weight"][:, :, :].rearrange("p b e -> p (b e)"), P),
                                    ALU.mult).then_inc(sel_ready, 1)
            nc.vector.memset(accT, 0.0).then_inc(s_chain, 1)
            for n in range(4):
                dve.wait_ge(selT_filled, n + 1)
                nc.vector.tensor_copy(selT[:, 2 * n:2 * n + 2, :], psum[:, n, :].rearrange("p (e t) -> p e t", e=2)).then_inc(selT_ready, 1)
            dve.wait_ge(s_chain, 1)
            with dve.Fori(0, E) as e:
                for u in range(FQ):
                    for f in range(4):
                        dve.wait_ge(silu_ready, e * FC + (4 * u + f + 1))
                        nc.vector.tensor_tensor(shid[u % 2][:, f, :], ssilu[:, f, :], psum[:, f, T:T + P], ALU.mult).then_inc(hid_free, 1)
                dve.wait_ge(blk_used, e * 12 + (BLK_MOE + 12))
                nc.vector.tensor_copy(yexp, psum[:, 4, :]).then_inc(acc_upd, 1)
                dve.wait_ge(scatter_filled, e + 1)
                dve.wait_ge(acc_upd, e * 2 + 1)
                nc.vector.tensor_tensor(accT.rearrange("p (a c) t -> p a (c t)", a=2), accT.rearrange("p (a c) t -> p a (c t)", a=2),
                                        psum[:, 6:8, :], ALU.add).then_inc(acc_upd, 1)
            dve.wait_ge(accT_filled, 1)
            nc.vector.tensor_tensor(x_res[:, :, :], x_res[:, :, :], psum[:, 0:2, :], ALU.add).then_inc(moe_added, 1)

        qpT = view(16384, C, T)
        mem = view(17408, B, D)
        memT = view(18432, C, T)
        mkz = view(19456, B, 4, P)
        la = view(20480, B, H, P)
        laT = view(24576, B, H, P)
        x1oT = view(28672, C, T)
        mvt = sb("mvt", [P, B, DK])
        top8 = [sb(f"top8_{b}", [P, 8]) for b in range(B)]
        at8 = [sb(f"at8_{b}", [P, 8], u32) for b in range(B)]
        pick = [sb(f"pick{b}", [P, 1], u32) for b in range(B)]
        lm = sb("lm", [P, B, H])
        ls = sb("ls", [P, B, H])

        ctx_back = [sem(f"ctx_back{b}") for b in range(B)]
        qp_filled = sem("qp_filled")
        qp_ready = sem("qp_ready")
        pick_scores = sem("pick_scores")
        top_found = sem("top_found")
        at_found = sem("at_found")
        picked = sem("picked")
        mem_arrived = [sem(f"mem_arrived{b}") for b in range(B)]
        memT_filled = sem("memT_filled")
        memT_ready = sem("memT_ready")
        mk_filled = sem("mk_filled")
        mkz_ready = sem("mkz_ready")
        mv_filled = sem("mv_filled")
        mv_ready = sem("mv_ready")
        la_filled = sem("la_filled")
        la_shift = sem("la_shift")
        la_exp = sem("la_exp")
        la_ready = sem("la_ready")
        laT_filled = sem("laT_filled")
        laT_ready = sem("laT_ready")
        x1o_filled = sem("x1o_filled")
        x1o_ready = sem("x1o_ready")

        def cross1_pe(pe):
            norm_pe(pe, 3)
            need(pe, BLK_X1)
            for ec in range(C):
                for c in range(C):
                    last = nc.tensor.matmul(psum[:, 2 + ec // 2, (ec % 2) * T:(ec % 2) * T + T],
                                            block(BLK_X1)[:, c, ec * P:(ec + 1) * P], xnT[:, c, :],
                                            start=c == 0, stop=c == C - 1)
                if ec % 2:
                    last.then_inc(qp_filled if ec == 1 else blk_used, 1)
            pe.wait_ge(qp_ready, 2)
            for b in range(B):
                pe.wait_ge(ctx_back[b], 16)
                for kb in range(KB):
                    for c in range(C):
                        last = nc.tensor.matmul(psum[:, 4 - 4 * b + kb, :], qpT[:, c, b * P:(b + 1) * P],
                                                ctxT_sb[b][:, c, kb * 512:(kb + 1) * 512], start=c == 0, stop=c == C - 1)
                last.then_inc(pick_scores, 1)
            pe.wait_ge(at_found, 1)
            for b in range(B):
                pe.wait_ge(mem_arrived[b], 16)
                for c in range(C):
                    last = nc.tensor.transpose(psum[:, 4 + b, c * P:(c + 1) * P], mem[:, b, c * P:(c + 1) * P], C_("ident"))
                last.then_inc(memT_filled, 1)
            pe.wait_ge(memT_ready, 2)
            for c in range(C):
                last = nc.tensor.matmul(psum[:, 6, 0:T], S_("x1_k")[:, c, :], memT[:, c, :], start=c == 0, stop=c == C - 1)
            last.then_inc(mk_filled, 1)
            for b in range(B):
                for c in range(C):
                    last = nc.tensor.matmul(psum[:, 7, b * DK:(b + 1) * DK], memT[:, c, b * P:(b + 1) * P],
                                            S_("x1_v")[:, c, :], start=c == 0, stop=c == C - 1)
            last.then_inc(mv_filled, 1)
            pe.wait_ge(at_found, 2)
            for b in range(B):
                pe.wait_ge(mkz_ready, b + 1)
                if b == 1:
                    pe.wait_ge(mv_ready, 1)
                for j in range(C):
                    last = nc.tensor.matmul(psum[:, 4 * b + j, :], qpT[:, j, b * P:(b + 1) * P], mkz[:, b, :, :],
                                            start=True, stop=True)
                last.then_inc(la_filled, 1)
            for b in range(B):
                pe.wait_ge(la_ready, b + 1)
                for j in range(C):
                    for i in range(4):
                        last = nc.tensor.transpose(psum[:, 4 * b + j, i * P:(i + 1) * P], la[:, b, 4 * j + i, :], C_("ident"))
                    last.then_inc(laT_filled, 1)
            for b in range(B):
                pe.wait_ge(laT_ready, C * (b + 1))
                for i in range(4):
                    last = nc.tensor.matmul(psum[DK * i:DK * i + DK, b, :], mvt[:, b, :],
                                            laT[:, b, :, :].rearrange("p (j i) q -> p j i q", i=4)[:, :, i, :],
                                            start=True, stop=True)
                last.then_inc(x1o_filled, 1)
            need(pe, BLK_X1 + 1)
            for b in range(B):
                pe.wait_ge(x1o_ready, b + 1)
                for c in range(C):
                    last = nc.tensor.matmul(psum[:, 2 + b, :], x1oT[:, c, b * P:(b + 1) * P], block(BLK_X1 + 1)[:, c, :],
                                            start=c == 0, stop=c == C - 1)
            last.then_inc(blk_used, 1)

        def cross1_act(act):
            norm_act(act, 3)
            for i in range(2):
                if i == 0:
                    act.wait_ge(qp_filled, 1)
                else:
                    act.wait_ge(blk_used, BLK_X1 + 1)
                nc.scalar.copy(qpT[:, 2 * i:2 * i + 2, :], psum[:, 2 + i, :].rearrange("p (c t) -> p c t", c=2)).then_inc(qp_ready, 1)
            for b in range(B):
                act.wait_ge(memT_filled, b + 1)
                nc.scalar.copy(memT[:, :, b * P:(b + 1) * P], bank4(4 + b)).then_inc(memT_ready, 1)
            act.wait_ge(mv_filled, 1)
            nc.scalar.copy(mvt[:, :, :], psum[:, 7, 0:B * DK].rearrange("p (b d) -> p b d", b=B)).then_inc(mv_ready, 1)
            for b in range(B):
                act.wait_ge(la_shift, b + 1)
                nc.scalar.activation(la[:, b, :, :], la[:, b, :, :], ACT.Exp, scale=float(1.0 / np.sqrt(DK).astype(np.float32))).then_inc(la_exp, 1)
            for n in range(B * C):
                act.wait_ge(laT_filled, n + 1)
                nc.scalar.copy(laT[:, n // C, 4 * (n % C):4 * (n % C) + 4, :], bank4(n)).then_inc(laT_ready, 1)
            for b in range(B):
                act.wait_ge(x1o_filled, b + 1)
                nc.scalar.copy(x1oT[:, :, b * P:(b + 1) * P], bank4(b)).then_inc(x1o_ready, 1)

        def cross1_dve(dve):
            norm_dve(dve, 3)
            for b in range(B):
                dve.wait_ge(pick_scores, b + 1)
                scores = psum[:, 4 - 4 * b:8 - 4 * b, :].rearrange("p a n -> p (a n)")
                nc.vector.max(top8[b][:, :], scores).then_inc(top_found, 1)
                dve.wait_ge(top_found, b + 1)
                nc.vector.max_index(at8[b][:, :], top8[b][:, :], scores).then_inc(at_found, 1)
                dve.wait_ge(at_found, b + 1)
                nc.vector.tensor_scalar(pick[b][:, :], at8[b][:, 0:1], b * CTX, None, ALU.add).then_inc(picked, 1)
            dve.wait_ge(mk_filled, 1)
            for b in range(B):
                nc.vector.tensor_tensor(mkz[:, b, :, :], per_row(psum[:, 6, b * P:(b + 1) * P], 4),
                                        per_elem(K_("headmask", 0, 4), P), ALU.mult).then_inc(mkz_ready, 1)
            for b in range(B):
                dve.wait_ge(la_filled, b + 1)
                logits = psum[:, 4 * b:4 * b + 4, :].rearrange("p j (i m) -> p (j i) m", i=4)
                link(dve, nc.vector.reduce_max(lm[:, b, :], logits, AX.X))
                nc.vector.tensor_tensor(la[:, b, :, :], logits, per_elem(lm[:, b, :], P), ALU.subtract).then_inc(la_shift, 1)
            for b in range(B):
                dve.wait_ge(la_exp, b + 1)
                link(dve, nc.vector.reduce_sum(ls[:, b, :], la[:, b, :, :], AX.X))
                link(dve, nc.vector.reciprocal(ls[:, b, :], ls[:, b, :]))
                nc.vector.tensor_tensor(la[:, b, :, :], la[:, b, :, :], per_elem(ls[:, b, :], P), ALU.mult).then_inc(la_ready, 1)
            dve.wait_ge(blk_used, BLK_X1 + 2)
            link(dve, nc.vector.tensor_tensor(x_res[:, :, :], x_res[:, :, :], psum[:, 2:4, :], ALU.add))

        lz = view(0, 3, C, T)
        le = view(3 * C * T, 2, C, T)
        lqk = view(5 * C * T, 2, C, T)
        lkv = view(7 * C * T, C * B, P)
        lden = view(8 * C * T, C * B, P)
        lvT = view(9 * C * T, C, T)
        ly = view(10 * C * T, B, D)
        lkvs = sb("lkvs", [P, C * B])
        lks = sb("lks", [P, C * B])

        lin_filled = sem("lin_filled")
        lmin_ready = sem("lmin_ready")
        lexp_ready = sem("lexp_ready")
        lv_ready = sem("lv_ready")
        ly_ready = sem("ly_ready")
        lgelu = sem("lgelu")

        def linear_pe(pe):
            norm_pe(pe, 4)
            for m in range(3):
                need(pe, BLK_LIN + m)
                for cc in range(C):
                    for c in range(C):
                        last = nc.tensor.matmul(psum[:, 2 + 2 * m + cc // 2, (cc % 2) * T:(cc % 2) * T + T],
                                                block(BLK_LIN + m)[:, c, cc * P:(cc + 1) * P], xnT[:, c, :],
                                                start=c == 0, stop=c == C - 1)
                    if cc % 2:
                        last.then_inc(lin_filled if cc == 1 else blk_used, 1)
            need(pe, BLK_LIN + 3)
            pe.wait_ge(lv_ready, 1)
            for b in range(B):
                for c in range(C):
                    last = nc.tensor.matmul(psum[:, b, :], lvT[:, c, b * P:(b + 1) * P], block(BLK_LIN + 3)[:, c, :],
                                            start=c == 0, stop=c == C - 1)
            last.then_inc(blk_used, 1)

        def linear_act(act):
            norm_act(act, 4)
            act.wait_ge(lmin_ready, 1)
            nc.scalar.activation(le, le, ACT.Exp).then_inc(lexp_ready, 1)
            act.wait_ge(ly_ready, 1)
            nc.scalar.activation(ly, ly, ACT.Gelu_apprx_tanh).then_inc(lgelu, 1)

        def linear_dve(dve):
            norm_dve(dve, 4)
            for m in range(3):
                for cc in range(C):
                    if cc == 0:
                        dve.wait_ge(lin_filled, m + 1)
                    if cc == 2:
                        dve.wait_ge(blk_used, BLK_LIN + m + 1)
                    ins = nc.vector.tensor_scalar(lz[:, m, cc, :], psum[:, 2 + 2 * m + cc // 2, (cc % 2) * T:(cc % 2) * T + T],
                                                  K_("lin_b", m * C + cc), None, ALU.add)
                if m == 1:
                    link(dve, ins)
                    nc.vector.tensor_scalar(le, lz[:, 0:2, :, :], 0.0, None, ALU.min).then_inc(lmin_ready, 1)
            dve.wait_ge(lexp_ready, 1)
            flat = lambda v: v.rearrange("p m c t -> p (m c t)")
            link(dve, nc.vector.scalar_tensor_tensor(flat(lqk), flat(lz[:, 0:2, :, :]), 0.0, flat(le), ALU.max, ALU.add))
            q8 = lqk[:, 0, :, :].rearrange("p c (b t) -> p (c b) t", b=B)
            k8 = lqk[:, 1, :, :].rearrange("p c (b t) -> p (c b) t", b=B)
            v8 = lz[:, 2, :, :].rearrange("p c (b t) -> p (c b) t", b=B)
            link(dve, nc.vector.tensor_tensor(lkv, k8, v8, ALU.mult))
            link(dve, nc.vector.reduce_sum(lkvs[:, :], lkv, AX.X))
            link(dve, nc.vector.reduce_sum(lks[:, :], k8, AX.X))
            link(dve, nc.vector.tensor_tensor(lden, q8, per_elem(lks[:, :], P), ALU.mult))
            link(dve, nc.vector.tensor_scalar(lden, lden, 1e-6, None, ALU.add))
            link(dve, nc.vector.reciprocal(lden, lden))
            link(dve, nc.vector.tensor_tensor(lkv, q8, per_elem(lkvs[:, :], P), ALU.mult))
            nc.vector.tensor_tensor(lvT.rearrange("p c (b t) -> p (c b) t", b=B), lkv, lden, ALU.mult).then_inc(lv_ready, 1)
            dve.wait_ge(blk_used, BLK_LIN + 4)
            nc.vector.tensor_tensor(ly, psum[:, 0:2, :], per_row(R_("lin_bo"), B), ALU.add).then_inc(ly_ready, 1)
            dve.wait_ge(lgelu, 1)
            link(dve, nc.vector.tensor_tensor(x_res[:, :, :], x_res[:, :, :], ly, ALU.add))

        h_even = view(0, FC, T)
        h_odd = view(FC * T, FC, T)
        fsilu = view(2 * FC * T, 4, T)
        fy = view(2 * FC * T + 4 * T, B, D)
        ffn_filled = sem("ffn_filled")
        ffn_act = sem("ffn_act")
        ffn_hid = sem("ffn_hid")

        def ffn_pe(pe):
            norm_pe(pe, 5)
            for n in range(FC):
                k, f = BLK_W12 + 2 * (n // 4), n % 4
                if f == 0:
                    need(pe, k)
                    need(pe, k + 1)
                if n >= 4:
                    pe.wait_ge(ffn_hid, n - 3)
                for i in range(2):
                    for c in range(C):
                        last = nc.tensor.matmul(psum[:, f, i * T:(i + 1) * T], block(k + i)[:, c, f * P:(f + 1) * P],
                                                xnT[:, c, :], start=c == 0, stop=c == C - 1)
                    if f == 3:
                        last.then_inc(blk_used, 1)
                if f < 3:
                    last.then_inc(ffn_filled, 1)
            for layer, (k0, src) in enumerate(((BLK_H1, h_even), (BLK_H2, h_odd))):
                if layer == 0:
                    pe.wait_ge(ffn_hid, FC)
                else:
                    pe.wait_ge(ffn_act, 2 * FC)
                with pe.Fori(0, FC // RING) as it:
                    for s in range(RING):
                        need(pe, k0 + s, it)
                        pe.wait_ge(ffn_act, it * RING + (FC * (layer + 1) + s - 3))
                        w = ring[(k0 + s) % RING][:, :].rearrange("p (c n) -> p c n", c=FC)
                        for c in range(FC):
                            last = nc.tensor.matmul(psum[:, 4 + s, 0:T], w[:, c, :], src[:, c, :],
                                                    start=c == 0, stop=c == FC - 1)
                        last.then_inc(blk_used, 1)
            pe.wait_ge(ffn_act, 3 * FC)
            for n in range(FC):
                if n % 4 == 0:
                    need(pe, BLK_W3 + n // 4)
                for b in range(B):
                    last = nc.tensor.matmul(psum[:, b, :], h_even[:, n, b * P:(b + 1) * P], block(BLK_W3 + n // 4)[:, n % 4, :],
                                            start=n == 0, stop=n == FC - 1)
                if n % 4 == 3:
                    last.then_inc(blk_used, 1)

        def ffn_scalar(act):
            norm_act(act, 5)
            for n in range(FC):
                f = n % 4
                if f < 3:
                    act.wait_ge(ffn_filled, 3 * (n // 4) + f + 1)
                else:
                    act.wait_ge(blk_used, BLK_W12 + 2 * (n // 4) + 2)
                nc.scalar.activation(fsilu[:, f, :], psum[:, f, 0:T], ACT.Silu, scale=K_("w1_s", n)).then_inc(ffn_act, 1)
            for k0, dst, name in ((BLK_H1, h_odd, "h1_s"), (BLK_H2, h_even, "h2_s")):
                with act.Fori(0, FC // RING) as it:
                    for s in range(RING):
                        act.wait_ge(blk_used, it * RING + (k0 + s + 1))
                        nc.scalar.activation(dst[:, ds(it * RING + s, 1), :], psum[:, 4 + s, 0:T].unsqueeze(1), ACT.Gelu,
                                             scale=col[:, ds(it * RING + (COLS[name][0] + s), 1)]).then_inc(ffn_act, 1)

        def ffn_dve(dve):
            norm_dve(dve, 5)
            for n in range(FC):
                f = n % 4
                dve.wait_ge(ffn_act, n + 1)
                nc.vector.scalar_tensor_tensor(h_even[:, n, :], psum[:, f, T:2 * T], K_("w2_s", n), fsilu[:, f, :],
                                               ALU.mult, ALU.mult).then_inc(ffn_hid, 1)
            dve.wait_ge(blk_used, NBLK)
            link(dve, nc.vector.tensor_tensor(fy, psum[:, 0:2, :], per_row(R_("w3_s"), B), ALU.mult))
            nc.vector.tensor_tensor(x_res[:, :, :], x_res[:, :, :], fy, ALU.add).then_inc(x_final, 1)

        block_ = ctx.enter_context(nc.Block())

        @block_.sync
        def _(sp):
            sp.dma_start(x_res[:, :, :], x).then_inc(loaded, 16)
            sp.dma_start(cst[:, :], consts).then_inc(loaded, 16)
            sp.dma_start(row[:, :], rows.partition_broadcast(P)).then_inc(loaded, 16)
            sp.dma_start(col[:, :], cols).then_inc(loaded, 16)
            sp.dma_start(sml[:, :], small).then_inc(loaded, 16)
            sp.dma_start(pairw[:, :, :, :], qkv[0].rearrange("p (m c n) -> p m c n", m=3, c=C)).then_inc(pair_arrived, 16)
            sp.dma_start(ctxT_sb[0], ctxT[0]).then_inc(ctx_arrived[0], 16)
            sp.dma_start(ctxT_sb[1], ctxT[1]).then_inc(ctx_arrived[1], 16)
            for k in range(RING):
                dma_block(sp, k, k)
            with sp.Fori(1, PAIRS) as hp:
                sp.wait_ge(kq_evac, hp * 10)
                sp.dma_start(pairw[:, :, :, :], qkv[ds(hp, 1)].rearrange("a p (m c n) -> p (a m) c n", m=3, c=C)).then_inc(pair_arrived, 16)
            for k in range(RING, 7):
                dma_block(sp, k, k, used=k - RING + 1)
            with sp.Fori(0, E) as e:
                for i in range(3 * FQ):
                    dma_block(sp, ds(e * 12 + (BLK_MOE + i), 1), BLK_MOE + i, used=e * 12 + (BLK_MOE + i - RING + 1))
            turns = (NBLK - BLK_X1) // RING
            with sp.Fori(0, turns) as i:
                for s in range(RING):
                    dma_block(sp, ds(i * RING + (BLK_X1 + s), 1), BLK_X1 + s, used=i * RING + (BLK_X1 + s - RING + 1))
            for k in range(BLK_X1 + turns * RING, NBLK):
                dma_block(sp, k, k, used=k - RING + 1)
            sp.wait_ge(x_final, 1)
            sp.dma_start(out, x_res[:, :, :]).then_inc(stored, 16)
            sp.wait_ge(stored, 16)

        @block_.gpsimd
        def _(gp):
            gp.wait_ge(blk_used, BLK_MOE + 3 * FQ)
            for b in range(B):
                gp.dma_start(ctxT_sb[b], ctxT[b]).then_inc(ctx_back[b], 16)
            for b in range(B):
                gp.wait_ge(picked, b + 1)
                gp.indirect_dma_start(out=mem[:, b, :], out_offset=None, in_=ctx_rows,
                                      in_offset=bass.IndirectOffsetOnAxis(ap=pick[b][:, :], axis=0)).then_inc(mem_arrived[b], 16)

        @block_.scalar
        def _(act):
            cross0_act(act)
            mixer_act(act)
            experts_act(act)
            cross1_act(act)
            linear_act(act)
            ffn_scalar(act)

        @block_.vector
        def _(dve):
            cross0_dve(dve)
            mixer_dve(dve)
            experts_dve(dve)
            cross1_dve(dve)
            linear_dve(dve)
            ffn_dve(dve)

        @block_.tensor
        def _(pe):
            pe.wait_ge(loaded, 16 * NLOADS)
            cross0_pe(pe)
            mixer_pe(pe)
            experts_pe(pe)
            cross1_pe(pe)
            linear_pe(pe)
            ffn_pe(pe)


def _rows_to_partitions(w):
    n = w.shape[0] // P
    return w.reshape(n, P, w.shape[1]).transpose(1, 0, 2).reshape(P, n * w.shape[1])


def _columns(v):
    return v.reshape(-1, P).T


def _stream_blocks(a):
    def quarters(w):
        return [w[:, q * 512:(q + 1) * 512] for q in range(w.shape[1] // 512)]

    def row_quarters(w):
        return [w[q * 512:(q + 1) * 512] for q in range(w.shape[0] // 512)]

    mats = row_quarters(a["L0_xattn_Wo"])
    mats += [a["L0_attn_" + n] for n in ("Wq", "Wk", "Wv", "Wg", "Wo")]
    for e in range(E):
        for w1, w3, w2 in zip(quarters(a["L0_ffn_w1"][e].T), quarters(a["L0_ffn_w3"][e].T),
                              row_quarters(a["L0_ffn_w2"][e].T)):
            mats += [w1, w3, w2]
    mats += [a["L1_xattn_Wq"].T, a["L1_xattn_Wc"].T]
    mats += [a["L1_attn_" + n] for n in ("Wq", "Wk", "Wv", "Wo")]
    for w1, w2 in zip(quarters(a["L1_ffn_w1_w"].T), quarters(a["L1_ffn_w2_w"].T)):
        mats += [w1, w2]
    for n in ("h1", "h2"):
        w = a[f"L1_ffn_{n}_w"].T
        mats += [w[:, f * P:(f + 1) * P] for f in range(FC)]
    mats += row_quarters(a["L1_ffn_w3_w"].T)
    return np.stack([_rows_to_partitions(m) for m in mats])


def kernel(**inputs):
    import concourse.bacc as _bacc
    from concourse.bass_utils import run_bass_kernel_spmd as _run

    a = {k: np.asarray(v) for k, v in inputs.items()}
    f32 = np.float32
    qkv = np.stack([np.concatenate([_rows_to_partitions(a["L0_xattn_W" + m][:, hp * P:(hp + 1) * P]) for m in "qkv"],
                                   axis=1) for hp in range(PAIRS)])
    convw = np.stack([a[f"L0_attn_conv_{m}_w"].reshape(C, P, TAPS) for m in "qkv"]).transpose(2, 0, 1, 3).reshape(P, -1)
    headmask = (np.arange(P)[:, None] // DK == np.arange(4)[None, :]).astype(f32)
    rank = np.broadcast_to(np.arange(E, 0, -1).astype(f32), (P, E))
    cols = np.concatenate([_columns(a["L0_xattn_bq"]), _columns(a["L0_xattn_bk"]), _columns(a["L0_xattn_bv"]), convw,
                           _columns(a["L1_attn_bq"]), _columns(a["L1_attn_bk"]), _columns(a["L1_attn_bv"])]
                          + [_columns(a[f"L1_ffn_{n}_s"]) for n in ("w1", "w2", "h1", "h2")] + [headmask, rank], axis=1)
    rows = np.concatenate([a[n] for n in ("L0_xattn_bo", "L0_xattn_ln_gamma", "L0_xattn_ln_beta", "L0_attn_dt_bias",
                                          "L0_attn_bb", "L0_attn_A_log", "L0_attn_gnorm_w", "L1_attn_bo",
                                          "L1_ffn_w3_s")])
    wkv = a["L1_xattn_Wkv"]
    small = np.concatenate([_rows_to_partitions(m) for m in (
        np.concatenate([a["L0_attn_Wgk"], a["L0_attn_Wb"]], axis=1), a["L0_ffn_gate_w"].T,
        np.concatenate([wkv[:DK].T] * 4, axis=1), wkv[DK:].T)], axis=1)
    ctx = a["ctx_1024"]
    arrays = {
        "x": a["x"].transpose(1, 0, 2),
        "ctxT": ctx.transpose(0, 2, 1).reshape(B, C, P, CTX).transpose(0, 2, 1, 3),
        "ctx_rows": ctx.reshape(B * CTX, D),
        "qkv": qkv, "stream": _stream_blocks(a), "small": small, "cols": cols, "rows": rows, "consts": constants(),
    }
    nc = _bacc.Bacc("TRN2", target_bir_lowering=False, num_devices=1)
    arrays = {f"in_{n}": np.ascontiguousarray(v) for n, v in arrays.items()}
    args = [nc.dram_tensor(n, v.shape, mybir.dt.from_np(v.dtype), kind="ExternalInput").ap() for n, v in arrays.items()]
    out = nc.dram_tensor("out", (P, B, D), mybir.dt.float32, kind="ExternalOutput").ap()
    build(nc, *args, out)
    r = _run(nc, [arrays], core_ids=[0])
    return r.results[0]["out"].transpose(1, 0, 2)
```

```python
from contextlib import ExitStack

import numpy as np

import concourse.bass as bass
from concourse import mybir

P = 128
B = 2
D = 512
C = D // P
T = B * P
CTX = 2048
KB = CTX // 512
KC = CTX // P
H = 16
PAIRS = H // 2
DK = D // H
TAPS = 4
E = 8
F = 2048
FQ = F // 512
FC = F // P
BLK = 2048
RING = 4
LEVELS = 7
JITTER = 0.01
EPS = 1e-5

BLK_XO = 0
BLK_MIX = 2
BLK_MOE = 7
BLK_X1 = BLK_MOE + E * FQ * 3
BLK_LIN = BLK_X1 + 2
BLK_W12 = BLK_LIN + 4
BLK_H1 = BLK_W12 + 2 * FQ
BLK_H2 = BLK_H1 + FC
BLK_W3 = BLK_H2 + FC
NBLK = BLK_W3 + FQ

CONST_NAMES = ["ident", "le", "gt", "low0", "low1", "low2", "low3", "low4", "low5", "low6", "up0",
               "ropec", "ropes", "partner", "group", "iota"]
CONST = {n: P * i for i, n in enumerate(CONST_NAMES)}
NCONST = P * len(CONST_NAMES)
ROWS = {"x0_bo": (0, D), "x0_gamma": (D, D), "x0_beta": (2 * D, D), "mix_dt": (3 * D, H),
        "mix_bb": (3 * D + H, H), "mix_alog": (3 * D + 2 * H, H), "mix_gnorm": (3 * D + 3 * H, DK),
        "lin_bo": (3 * D + 3 * H + DK, D), "w3_s": (4 * D + 3 * H + DK, D)}
NROWS = 5 * D + 3 * H + DK
COLS = {"x0_bq": (0, PAIRS), "x0_bk": (8, PAIRS), "x0_bv": (16, PAIRS), "convw": (24, 3 * C * TAPS),
        "lin_b": (72, 3 * C), "w1_s": (84, FC), "w2_s": (100, FC), "h1_s": (116, FC), "h2_s": (132, FC),
        "headmask": (148, 4), "rank": (152, E)}
NCOLS = 152 + E
SMALL = {"mix_gb": (0, 2 * H), "gate": (C * 2 * H, E), "x1_k": (C * (2 * H + E), P), "x1_v": (C * (2 * H + E + P), DK)}
NSMALL = C * (2 * H + E + P + DK)

ARENA = 32768
ARENA_R = 8192


def constants():
    r, c = np.indices((P, P))
    t = {"ident": r == c, "le": r <= c, "gt": r > c}
    for l in range(LEVELS):
        m = 1 << l
        pair = (r // (2 * m) == c // (2 * m)) & (r // m != c // m)
        t[f"low{l}"] = pair & (r > c)
        if l == 0:
            t["up0"] = pair & (r < c)
    half = DK // 4
    d = np.arange(P) % DK
    inv = (np.float32(10000.0) ** (-np.arange(half, dtype=np.float32) / np.float32(half))).astype(np.float32)
    ang = (np.arange(P, dtype=np.float32)[None, :] * inv[d % half][:, None]).astype(np.float32)
    rot = (d < 2 * half)[:, None]
    t["ropec"] = np.where(rot, np.cos(ang), 1.0)
    t["ropes"] = np.where(rot, np.sin(ang), 0.0)
    dm, dk = c % DK, r % DK
    t["partner"] = (r // DK == c // DK) * ((dm < half) * (dk == dm + half) * -1.0
                                           + ((dm >= half) & (dm < 2 * half)) * (dk == dm - half))
    t["group"] = r // DK == c // DK
    t["iota"] = c
    return np.concatenate([t[n].astype(np.float32) for n in CONST_NAMES], axis=1)


def build(nc, x, ctxT, ctx_rows, wq, wk, wv, stream, small, cols, rows, consts, out):
    fp32, f32r, u32 = mybir.dt.float32, mybir.dt.float32r, mybir.dt.uint32
    ALU = mybir.AluOpType
    ACT = mybir.ActivationFunctionType
    AX = mybir.AxisListType
    ds = bass.ds

    with ExitStack() as ctx:
        def sb(name, shape, dt=fp32):
            return ctx.enter_context(nc.sbuf_tensor(name, shape, dt))

        def sem(name):
            return ctx.enter_context(nc.semaphore(name))

        x_res = sb("x_res", [P, B, D])
        xn = sb("xn", [P, B, D])
        xnT = sb("xnT", [P, C, T])
        cst = sb("cst", [P, NCONST])
        row = sb("row", [P, NROWS])
        col = sb("col", [P, NCOLS])
        sml = sb("sml", [P, NSMALL])
        ring = [sb(f"ring{i}", [P, BLK]) for i in range(RING)]
        with nc.sbuf_tensor("arena", [P, ARENA], fp32) as arena_memory:
            arena = arena_memory
        arena_r = [sb(f"arena_r{i}", [P, ARENA_R], f32r) for i in range(ARENA // ARENA_R)]
        stats = sb("stats", [P, B, 6])
        mv = sb("mv", [P, B, 2])
        std = sb("std", [P, B])
        rstd = sb("rstd", [P, B])
        epst = sb("epst", [P, 2])
        psum = ctx.enter_context(nc.psum_tensor("psum", [P, 8, 512], fp32))

        def C_(name, w=P):
            return cst[:, CONST[name]:CONST[name] + w]

        def R_(name):
            a, w = ROWS[name]
            return row[:, a:a + w]

        def K_(name, i=0, n=1):
            return col[:, COLS[name][0] + i:COLS[name][0] + i + n]

        def S_(name):
            a, w = SMALL[name]
            return sml[:, a:a + C * w].rearrange("p (c n) -> p c n", c=C)

        def view(at, *shape, one_pass=False):
            n = int(np.prod(shape))
            assert at + n <= ARENA, (at, shape)
            if one_pass:
                assert at // ARENA_R == (at + n - 1) // ARENA_R, (at, shape)
                v = arena_r[at // ARENA_R][:, at % ARENA_R:at % ARENA_R + n]
            else:
                v = arena[:, at:at + n]
            if len(shape) == 1:
                return v
            letters = "abcd"[:len(shape)]
            return v.rearrange(f"p ({' '.join(letters)}) -> p {' '.join(letters)}",
                               **dict(zip(letters[:-1], shape[:-1])))

        def block(k):
            return ring[k % RING][:, :].rearrange("p (c n) -> p c n", c=C)

        def per_row(ap, n):
            return ap.unsqueeze(1).to_broadcast([P, n, ap.shape[-1]])

        def per_elem(ap, n):
            return ap.unsqueeze(2).to_broadcast([P, ap.shape[-1], n])

        x_loaded = sem("x_loaded")
        loaded = sem("loaded")
        wq_arrived = sem("wq_arrived")
        wk_arrived = sem("wk_arrived")
        wv_arrived = sem("wv_arrived")
        ctx_arrived = [sem(f"ctx_arrived{kb}") for kb in range(KB)]
        blk_arrived = [sem(f"blk_arrived{i}") for i in range(RING)]
        blk_used = sem("blk_used")
        x_final = sem("x_final")
        stored = sem("stored")
        v_chain = sem("v_chain")
        a_chain = sem("a_chain")

        ln_var = sem("ln_var")
        ln_std = sem("ln_std")
        xn_ready = sem("xn_ready")
        xnT_filled = sem("xnT_filled")
        xnT_v = sem("xnT_v")
        xnT_a = sem("xnT_a")

        NLOADS = 4

        def dma_block(sp, k_dram, k_static, used=None):
            if used is not None:
                sp.wait_ge(blk_used, used)
            sp.dma_start(ring[k_static % RING][:, :], stream[k_dram] if isinstance(k_dram, int) else stream[k_dram].rearrange("a p n -> (a p) n")).then_inc(blk_arrived[k_static % RING], 16)

        def need(pe, k, more_rounds=None):
            turn = 16 * (k // RING + 1)
            pe.wait_ge(blk_arrived[k % RING], turn if more_rounds is None else more_rounds * 16 + turn)

        def link(dve, ins, count=[0]):
            count[0] += 1
            ins.then_inc(v_chain, 1)
            dve.wait_ge(v_chain, count[0])

        def link_a(act, ins, count=[0]):
            count[0] += 1
            ins.then_inc(a_chain, 1)
            act.wait_ge(a_chain, count[0])

        def norm_stats_dve(dve, n):
            for b in range(B):
                ins = nc.vector.bn_stats(stats[:, b, :], x_res[:, b, :])
                if b == B - 1:
                    link(dve, ins)
            for b in range(B):
                nc.vector.bn_aggr(mv[:, b, :], stats[:, b, :]).then_inc(ln_var, 1)
            dve.wait_ge(ln_std, n + 1)
            link(dve, nc.vector.reciprocal(rstd[:, :], std[:, :]))
            for b in range(B):
                nc.vector.tensor_scalar(xn[:, b, :], x_res[:, b, :], mv[:, b, 0:1], rstd[:, b:b + 1],
                                        ALU.subtract, ALU.mult).then_inc(xn_ready, 1)

        def norm_dve(dve, n):
            norm_stats_dve(dve, n)
            norm_turned_dve(dve, n)

        def norm_turned_dve(dve, n):
            dve.wait_ge(xnT_filled, 2 * n + 1)
            nc.vector.tensor_copy(xnT[:, :, 0:P], psum[:, 0, :].rearrange("p (c t) -> p c t", c=C)).then_inc(xnT_v, 1)

        def norm_std_act(act, n):
            act.wait_ge(ln_var, 2 * n + 2)
            nc.scalar.activation(std[:, :], mv[:, :, 1], ACT.Sqrt, bias=epst[:, 0:1]).then_inc(ln_std, 1)

        def norm_act(act, n):
            norm_std_act(act, n)
            norm_turned_act(act, n)

        def norm_turned_act(act, n):
            act.wait_ge(xnT_filled, 2 * n + 2)
            nc.scalar.copy(xnT[:, :, P:T], psum[:, 1, :].rearrange("p (c t) -> p c t", c=C)).then_inc(xnT_a, 1)

        def norm_pe(pe, n):
            for b in range(B):
                pe.wait_ge(xn_ready, 2 * n + b + 1)
                for c in range(C):
                    last = nc.tensor.transpose(psum[:, b, c * P:(c + 1) * P], xn[:, b, c * P:(c + 1) * P], C_("ident"))
                last.then_inc(xnT_filled, 1)
            pe.wait_ge(xnT_v, n + 1)
            pe.wait_ge(xnT_a, n + 1)

        PARTS = ((0, 0), (0, 1), (1, 0))

        def lo_part(out, v, hi):
            return nc.vector.tensor_tensor(out, v, hi.bitcast(fp32), ALU.subtract)

        ctxT_sb = [view(b * C * CTX, C, CTX) for b in range(B)]
        cx = [view(i * C * CTX, C, CTX, one_pass=True) for i in range(2)]
        cx_in = view(C * CTX, C, CTX)
        o = B * C * CTX
        kT = [view(o + i * CTX, CTX) for i in range(2)]
        o += 2 * CTX
        pbuf = view(o, CTX)
        o += CTX
        pT = [view(o + h * CTX, KC, P) for h in range(2)]
        o += 2 * CTX
        qz = [view(o + i * 2 * P, 2, P) for i in range(2)]
        o += 2 * 2 * P
        attnT = view(o, PAIRS, T)
        o += PAIRS * T
        wq_sb = view(o, C, P)
        o += C * P
        wk_sb = [view(o + i * C * P, C, P, one_pass=True) for i in range(2)]
        wk_in = view(o + C * P, C, P)
        o += 2 * C * P
        wv_sb = [view(o + i * C * T, C, T, one_pass=True) for i in range(2)]
        wv_in = view(o + C * T, C, T)
        vv = [ring[2 + i][:, :].rearrange("p (k n) -> p k n", n=2 * P) for i in range(2)]
        nmax = sb("nmax", [P, 2])
        rsum = sb("rsum", [P, 1])
        rinv = sb("rinv", [P, 1])

        ctx_hi = sem("ctx_hi")
        ctx_lo = sem("ctx_lo")
        wk_hi = sem("wk_hi")
        wk_lo = sem("wk_lo")
        wv_hi = sem("wv_hi")
        wv_lo = sem("wv_lo")
        kq_filled = sem("kq_filled")
        kq_evac = sem("kq_evac")
        v_filled = sem("v_filled")
        v_evac = sem("v_evac")
        scores_ready = sem("scores_ready")
        nmax_ready = sem("nmax_ready")
        rinv_ready = sem("rinv_ready")
        exp_ready = sem("exp_ready")
        p_ready = sem("p_ready")
        pT_filled = sem("pT_filled")
        pT_v = sem("pT_v")
        pT_a = sem("pT_a")
        pv_done = sem("pv_done")
        head_done = sem("head_done")
        attn_ready = sem("attn_ready")
        x0_filled = sem("x0_filled")
        x0_std = sem("x0_std")
        x0_var = sem("x0_var")

        FIRST = (("k0", "v0", "k1", "v1"), ("v2", "v3"), ("k2", "v4", "k3", "v5"), ("v6", "v7", "q"))
        SECOND = (("k0", "k1"), (), ("k2", "k3"), ("q",))
        NOTHING = ((), (), (), ())

        def project_k(pe, bn, n, kb, own_bank):
            bank = 4 if own_bank else 4 + kb % 2
            if not isinstance(n, int):
                pe.wait_ge(kq_evac, n * 5 + (kb if own_bank or kb == 0 else kb - 1))
            elif n * 5 + kb > 1:
                pe.wait_ge(kq_evac, n * 5 + (kb if own_bank or kb == 0 else kb - 1))
            if kb == 0:
                pe.wait_ge(wk_lo, n + 1)
            pe.wait_ge(ctx_lo, bn * KB + kb + 1)
            for c in range(C):
                for wp, xp in PARTS:
                    last = nc.tensor.matmul(psum[:, bank, :], wk_sb[wp][:, c, :], cx[xp][:, c, kb * 512:(kb + 1) * 512],
                                            start=c == wp == xp == 0, stop=c == C - 1 and wp == 1)
            last.then_inc(kq_filled, 1)

        def project_v(pe, m, i):
            if i == 0:
                pe.wait_ge(wv_lo, m + 1)
                pe.wait_ge(nmax_ready, m * 8 + 2)
            if i >= 2:
                pe.wait_ge(v_evac, m * 8 + (i - 1))
            for q in range(2):
                kc = 2 * i + q
                for c in range(C):
                    for wp, xp in PARTS:
                        last = nc.tensor.matmul(psum[:, 7 - i % 2 * 2, q * T:(q + 1) * T], cx[xp][:, c, kc * P:(kc + 1) * P],
                                                wv_sb[wp][:, c, :], start=c == wp == xp == 0, stop=c == C - 1 and wp == 1)
            last.then_inc(v_filled, 1)

        def project_q(pe, bn, n):
            pe.wait_ge(kq_evac, n * 5 + 4)
            pe.wait_ge(wq_arrived, n * 16 + 16)
            for c in range(C):
                last = nc.tensor.matmul(psum[:, 4, 0:P], wq_sb[:, c, :], xnT[:, c, bn * P:(bn + 1) * P],
                                        start=c == 0, stop=c == C - 1)
            last.then_inc(kq_filled, 1)

        def project(pe, pause, bn, n, m, second):
            for item in pause:
                if item[0] == "k":
                    project_k(pe, bn, n, int(item[1]), own_bank=not second)
                elif item[0] == "v":
                    project_v(pe, m, int(item[1]))
                else:
                    project_q(pe, bn, n)

        def unit_pe(pe, bn, j, m, second, pauses):
            n = j + 1
            pe.wait_ge(kq_evac, j * 5 + 5)
            for h in range(2):
                for kb in range(KB):
                    if h == 1:
                        pe.wait_ge(pT_v if kb < 2 else pT_a, j * 4 + (kb % 2 + 1))
                    last = nc.tensor.matmul(psum[:, kb, :], qz[second][:, h, :], kT[second][:, kb * 512:(kb + 1) * 512],
                                            start=True, stop=True)
                last.then_inc(scores_ready, 1)
                project(pe, pauses[2 * h], bn, n, m, second)
                pe.wait_ge(p_ready, j * 2 + (h + 1))
                for kb in range(KB):
                    for q in range(4):
                        kc = 4 * kb + q
                        last = nc.tensor.transpose(psum[:, kb, q * P:(q + 1) * P], pbuf[:, kc * P:(kc + 1) * P], C_("ident"))
                    last.then_inc(pT_filled, 1)
                project(pe, pauses[2 * h + 1], bn, n, m, second)
            for kc in range(KC):
                if kc == 0:
                    pe.wait_ge(pT_v, j * 4 + 4)
                if kc == KC // 2:
                    pe.wait_ge(pT_a, j * 4 + 4)
                if not second and kc in (0, 14):
                    pe.wait_ge(v_evac, m * 8 + 7 + kc // 14)
                for h in range(2):
                    last = nc.tensor.matmul(psum[64 * h:64 * h + 64, 6 + h, 0:P],
                                            vv[kc // 8][:, kc % 8, second * P + 64 * h:second * P + 64 * h + 64],
                                            pT[h][:, kc, :], start=kc == 0, stop=kc == KC - 1)
            last.then_inc(pv_done, 1)

        def cross0_pe(pe):
            for kb in range(KB):
                project_k(pe, 0, 0, kb, own_bank=False)
            pe.wait_ge(loaded, 16 * NLOADS)
            norm_pe(pe, 0)
            project_q(pe, 0, 0)
            for b in range(B):
                with pe.Fori(0, PAIRS // 2 - 1) as g:
                    unit_pe(pe, b, g * 2 + PAIRS * b, g + PAIRS // 2 * b, 0, FIRST)
                    unit_pe(pe, b, g * 2 + (PAIRS * b + 1), g + PAIRS // 2 * b, 1, SECOND)
                j, m = PAIRS * (b + 1) - 2, PAIRS // 2 * (b + 1) - 1
                unit_pe(pe, b, j, m, 0, FIRST)
                unit_pe(pe, b + 1, j + 1, m, 1, SECOND if b == 0 else NOTHING)
            pe.wait_ge(attn_ready, 1)
            need(pe, BLK_XO)
            need(pe, BLK_XO + 1)
            for b in range(B):
                for hp in range(PAIRS):
                    last = nc.tensor.matmul(psum[:, b, :], attnT[:, hp, b * P:(b + 1) * P],
                                            block(BLK_XO + hp // C)[:, hp % C, :], start=hp == 0, stop=hp == PAIRS - 1)
                    if b == 1 and hp == C - 1:
                        last.then_inc(blk_used, 1)
                last.then_inc(x0_filled if b == 0 else blk_used, 1)

        def split_wk_dve(dve, n):
            dve.wait_ge(wk_hi, n + 1)
            lo_part(wk_sb[1], wk_in, wk_sb[0]).then_inc(wk_lo, 1)

        def split_wv_dve(dve, m):
            dve.wait_ge(wv_hi, m + 1)
            lo_part(wv_sb[1], wv_in, wv_sb[0]).then_inc(wv_lo, 1)

        def split_ctx_dve(dve, b, kb):
            dve.wait_ge(ctx_hi, b * KB + kb + 1)
            k = slice(kb * 512, (kb + 1) * 512)
            lo_part(cx[1][:, :, k], cx_in[:, :, k], cx[0][:, :, k]).then_inc(ctx_lo, 1)

        def evac_k_dve(dve, n, hp, kb, place, own_bank):
            dve.wait_ge(kq_filled, n * 5 + (kb + 1))
            nc.vector.tensor_scalar(kT[place][:, kb * 512:(kb + 1) * 512], psum[:, 4 if own_bank else 4 + kb % 2, :],
                                    col[:, ds(hp + COLS["x0_bk"][0], 1)], None, ALU.add).then_inc(kq_evac, 1)

        def evac_q_dve(dve, n, hp, place):
            dve.wait_ge(kq_filled, n * 5 + 5)
            for h in range(2):
                lo = 64 * h
                ins = nc.vector.tensor_scalar(qz[place][lo:lo + 64, h, :], psum[lo:lo + 64, 4, 0:P],
                                              col[lo:lo + 64, ds(hp + COLS["x0_bq"][0], 1)], None, ALU.add)
            ins.then_inc(kq_evac, 1)

        def evac_dve(dve, items, n, hpn, second):
            for item in items:
                if item[0] == "k":
                    evac_k_dve(dve, n, hpn, int(item[1]), 1 - second, own_bank=not second)
                elif item == "q":
                    evac_q_dve(dve, n, hpn, 1 - second)

        def unit_dve(dve, b, j, hp, m, second, pauses, hpn, switch=False):
            n = j + 1
            if pauses is not NOTHING:
                split_wk_dve(dve, n)
            if not second:
                split_wv_dve(dve, m)
            if switch:
                split_ctx_dve(dve, 1, 0)
            for h in range(2):
                u = j * 2 + h
                keys = [item for item in pauses[2 * h] if item[0] == "k"]
                dve.wait_ge(scores_ready, u + 1)
                nc.vector.reduce_max(nmax[:, 0:1], psum[:, 0:KB, :].rearrange("p a n -> p (a n)"), AX.X).then_inc(nmax_ready, 1)
                dve.wait_ge(nmax_ready, u * 2 + 1)
                nc.vector.tensor_scalar(nmax[:, 1:2], nmax[:, 0:1], -0.125, None, ALU.mult).then_inc(nmax_ready, 1)
                if switch and h == 0:
                    split_ctx_dve(dve, 1, 1)
                evac_dve(dve, keys[:1], n, hpn, second)
                dve.wait_ge(exp_ready, u + 1)
                nc.vector.reciprocal(rinv[:, :], rsum[:, :]).then_inc(rinv_ready, 1)
                dve.wait_ge(rinv_ready, u + 1)
                nc.vector.tensor_scalar(pbuf, pbuf, rinv[:, 0:1], None, ALU.mult).then_inc(p_ready, 1)
                evac_dve(dve, keys[1:], n, hpn, second)
                for kb in range(2):
                    dve.wait_ge(pT_filled, u * 4 + (kb + 1))
                    nc.vector.tensor_copy(pT[h][:, 4 * kb:4 * kb + 4, :], psum[:, kb, :].rearrange("p (q t) -> p q t", q=4)).then_inc(pT_v, 1)
                if switch and h == 0:
                    split_ctx_dve(dve, 1, 2)
                    split_ctx_dve(dve, 1, 3)
                evac_dve(dve, pauses[2 * h + 1], n, hpn, second)
            dve.wait_ge(pv_done, j + 1)
            for h in range(2):
                nc.vector.tensor_copy(attnT[64 * h:64 * h + 64, ds(hp, 1), b * P:(b + 1) * P],
                                      psum[64 * h:64 * h + 64, 6 + h, 0:P].unsqueeze(1)).then_inc(head_done, 1)

        def cross0_dve(dve):
            nc.vector.memset(epst[:, 0:1], EPS)
            nc.vector.memset(epst[:, 1:2], 1e-6)
            for i in range(2):
                link(dve, nc.vector.memset(qz[i], 0.0))
            dve.wait_ge(x_loaded, 16)
            norm_stats_dve(dve, 0)
            split_wk_dve(dve, 0)
            split_ctx_dve(dve, 0, 0)
            for kb in range(KB):
                if kb < KB - 1:
                    split_ctx_dve(dve, 0, kb + 1)
                if kb == 0:
                    dve.wait_ge(loaded, 16 * NLOADS)
                evac_k_dve(dve, 0, 0, kb, 0, own_bank=False)
            norm_turned_dve(dve, 0)
            evac_q_dve(dve, 0, 0, 0)
            for b in range(B):
                with dve.Fori(0, PAIRS // 2 - 1) as g:
                    j, m = g * 2 + PAIRS * b, g + PAIRS // 2 * b
                    unit_dve(dve, b, j, g * 2, m, 0, FIRST, g * 2 + 1)
                    unit_dve(dve, b, j + 1, g * 2 + 1, m, 1, SECOND, g * 2 + 2)
                j, m = PAIRS * (b + 1) - 2, PAIRS // 2 * (b + 1) - 1
                unit_dve(dve, b, j, PAIRS - 2, m, 0, FIRST, PAIRS - 1)
                unit_dve(dve, b, j + 1, PAIRS - 1, m, 1, SECOND if b == 0 else NOTHING, 0, switch=b == 0)
            dve.wait_ge(head_done, 2 * H)
            for hp in range(PAIRS):
                ins = nc.vector.tensor_scalar(attnT[:, hp, :], attnT[:, hp, :], K_("x0_bv", hp), None, ALU.add)
            ins.then_inc(attn_ready, 1)
            y = pbuf[:, 0:B * D].rearrange("p (b n) -> p b n", b=B)
            for b in range(B):
                if b == 0:
                    dve.wait_ge(x0_filled, 1)
                else:
                    dve.wait_ge(blk_used, BLK_XO + 2)
                link(dve, nc.vector.tensor_tensor(y[:, b, :], psum[:, b, :], xn[:, b, :], ALU.add))
            link(dve, nc.vector.tensor_tensor(y, y, per_row(R_("x0_bo"), B), ALU.add))
            for b in range(B):
                link(dve, nc.vector.bn_stats(stats[:, b, :], y[:, b, :]))
                nc.vector.bn_aggr(mv[:, b, :], stats[:, b, :]).then_inc(x0_var, 1)
            dve.wait_ge(x0_std, 1)
            link(dve, nc.vector.reciprocal(rstd[:, :], std[:, :]))
            for b in range(B):
                link(dve, nc.vector.tensor_scalar(y[:, b, :], y[:, b, :], mv[:, b, 0:1], rstd[:, b:b + 1],
                                                  ALU.subtract, ALU.mult))
            link(dve, nc.vector.tensor_tensor(y, y, per_row(R_("x0_gamma"), B), ALU.mult))
            link(dve, nc.vector.tensor_tensor(y, y, per_row(R_("x0_beta"), B), ALU.add))
            link(dve, nc.vector.tensor_tensor(x_res[:, :, :], x_res[:, :, :], y, ALU.add))

        def split_wk_act(act, n):
            act.wait_ge(wk_arrived, n * 16 + 16)
            nc.scalar.copy(wk_sb[0], wk_in).then_inc(wk_hi, 1)

        def split_wv_act(act, m):
            act.wait_ge(wv_arrived, m * 16 + 16)
            nc.scalar.copy(wv_sb[0], wv_in).then_inc(wv_hi, 1)

        def split_ctx_act(act, b, kb):
            act.wait_ge(ctx_arrived[kb], b * 16 + 16)
            k = slice(kb * 512, (kb + 1) * 512)
            nc.scalar.copy(cx[0][:, :, k], cx_in[:, :, k]).then_inc(ctx_hi, 1)

        def evac_v_act(act, items, m):
            for item in items:
                if item[0] == "v":
                    i = int(item[1])
                    act.wait_ge(v_filled, m * 8 + (i + 1))
                    nc.scalar.copy(vv[i // 4][:, i % 4 * 2:i % 4 * 2 + 2, :],
                                   psum[:, 7 - i % 2 * 2, :].rearrange("p (q n) -> p q n", q=2)).then_inc(v_evac, 1)

        def unit_act(act, j, m, second, pauses, switch=False):
            if pauses is not NOTHING:
                split_wk_act(act, j + 1)
            if not second:
                split_wv_act(act, m)
            if switch:
                split_ctx_act(act, 1, 0)
                split_ctx_act(act, 1, 1)
            for h in range(2):
                u = j * 2 + h
                act.wait_ge(nmax_ready, u * 2 + 2)
                nc.scalar.activation(pbuf, psum[:, 0:KB, :].rearrange("p a n -> p (a n)"), ACT.Exp, bias=nmax[:, 1:2],
                                     scale=0.125, accum_out=rsum[:, 0:1]).then_inc(exp_ready, 1)
                if switch and h == 0:
                    split_ctx_act(act, 1, 2)
                    split_ctx_act(act, 1, 3)
                evac_v_act(act, pauses[2 * h], m)
                for kb in range(2, 4):
                    act.wait_ge(pT_filled, u * 4 + (kb + 1))
                    nc.scalar.copy(pT[h][:, 4 * kb:4 * kb + 4, :], psum[:, kb, :].rearrange("p (q t) -> p q t", q=4)).then_inc(pT_a, 1)
                evac_v_act(act, pauses[2 * h + 1], m)

        def cross0_act(act):
            norm_std_act(act, 0)
            split_wk_act(act, 0)
            for kb in range(KB):
                split_ctx_act(act, 0, kb)
            norm_turned_act(act, 0)
            for b in range(B):
                with act.Fori(0, PAIRS // 2 - 1) as g:
                    j, m = g * 2 + PAIRS * b, g + PAIRS // 2 * b
                    unit_act(act, j, m, 0, FIRST)
                    unit_act(act, j + 1, m, 1, SECOND)
                j, m = PAIRS * (b + 1) - 2, PAIRS // 2 * (b + 1) - 1
                unit_act(act, j, m, 0, FIRST)
                unit_act(act, j + 1, m, 1, SECOND if b == 0 else NOTHING, switch=b == 0)
            act.wait_ge(x0_var, 2)
            nc.scalar.activation(std[:, :], mv[:, :, 1], ACT.Sqrt, bias=epst[:, 0:1]).then_inc(x0_std, 1)

        BH = B * H
        G8 = BH // 4
        dec = view(0, BH, P)
        etm = dec
        gm = view(4096, BH, P)
        um = gm
        m1 = gm
        pm = view(8192, BH, P)
        at = view(12288, BH, P)
        xi = view(16384, BH, P)
        xt = view(20480, BH, P)
        xpad = view(24576, 3 * C, B, P + TAPS - 1)
        yc = view(24576 + 3 * C * B * (P + TAPS - 1), 3 * C, B, P)
        yc_flat = view(24576 + 3 * C * B * (P + TAPS - 1), 3 * C * B * P)
        vtok = view(24576 + 3 * C * B * (P + TAPS - 1) + 3 * C * T, B, D)
        sq = view(0, 4, 512)
        rn = view(4096, 4, 512)
        turn = view(8192, 2 * C * B, P)
        qk = view(12288, 2 * C, B, P)
        kz = view(16384, B, C, 4, P)
        qzm = view(20480, B, C, 4, P)
        wmix = view(24576, B, D)
        osb = view(24576 + B * D, B, D)
        osq = view(24576 + 2 * B * D, B, D)
        oT = view(24576 + 3 * B * D, C, T)
        gs = xn
        z = sb("z", [P, B, 2 * H])
        za = sb("za", [P, B, H])
        zl = sb("zl", [P, B, H])
        gdec = sb("gdec", [P, B, H])
        beta = sb("beta", [P, B, H])
        alog = sb("alog", [P, H])
        oss = sb("oss", [P, BH])
        orn = sb("orn", [P, BH])

        mix_proj = sem("mix_proj")
        mix_evac = sem("mix_evac")
        mix_gb = sem("mix_gb")
        mix_z = sem("mix_z")
        mix_za = sem("mix_za")
        mix_zl = sem("mix_zl")
        mix_beta = sem("mix_beta")
        mix_gs = sem("mix_gs")
        conv = sem("conv")
        pad_clear = sem("pad_clear")
        mix_silu = sem("mix_silu")
        sq_ready = sem("sq_ready")
        ss_filled = sem("ss_filled")
        ss_root = sem("ss_root")
        qkn_ready = sem("qkn_ready")
        turn_filled = sem("turn_filled")
        vtok_filled = sem("vtok_filled")
        vtok_ready = sem("vtok_ready")
        gm_ready = sem("gm_ready")
        dec_filled = sem("dec_filled")
        dec_exp = sem("dec_exp")
        masked_ready = sem("masked_ready")
        kk_filled = sem("kk_filled")
        u_ready = sem("u_ready")
        at_filled = sem("at_filled")
        at_ready = sem("at_ready")
        x_upd = sem("x_upd")
        et_ready = sem("et_ready")
        m1_filled = sem("m1_filled")
        m1_ready = sem("m1_ready")
        xx_filled = sem("xx_filled")
        w_filled = sem("w_filled")
        w_ready = sem("w_ready")
        o_filled = sem("o_filled")
        oss_ready = sem("oss_ready")
        oss_root = sem("oss_root")
        on_ready = sem("on_ready")
        oT_filled = sem("oT_filled")
        oT_ready = sem("oT_ready")

        def four(ap, g):
            return ap[:, 4 * g:4 * g + 4, :]

        def bank4(i):
            return psum[:, i, :].rearrange("p (a t) -> p a t", a=4)

        def mixer_pe(pe):
            norm_pe(pe, 1)
            for m in range(3):
                need(pe, BLK_MIX + m)
                for cc in range(C):
                    n = C * m + cc
                    for c in range(C):
                        last = nc.tensor.matmul(psum[:, 2 + n // 2, (n % 2) * T:(n % 2) * T + T],
                                                block(BLK_MIX + m)[:, c, cc * P:(cc + 1) * P], xnT[:, c, :],
                                                start=c == 0, stop=c == C - 1)
                    last.then_inc(blk_used if cc == C - 1 else mix_proj, 1)
            need(pe, BLK_MIX + 3)
            for b in range(B):
                for c in range(C):
                    last = nc.tensor.matmul(psum[:, b, :], xnT[:, c, b * P:(b + 1) * P], block(BLK_MIX + 3)[:, c, :],
                                            start=c == 0, stop=c == C - 1)
            last.then_inc(blk_used, 1)
            pe.wait_ge(mix_evac, 1)
            for b in range(B):
                for c in range(C):
                    last = nc.tensor.matmul(psum[:, 2, b * 2 * H:(b + 1) * 2 * H], xnT[:, c, b * P:(b + 1) * P],
                                            S_("mix_gb")[:, c, :], start=c == 0, stop=c == C - 1)
            last.then_inc(mix_gb, 1)
            pe.wait_ge(mix_silu, 1)
            for b in range(B):
                for cc in range(C):
                    last = nc.tensor.transpose(psum[:, 6 + b, cc * P:(cc + 1) * P], yc[:, 2 * C + cc, b, :], C_("ident"))
                last.then_inc(vtok_filled, 1)
            pe.wait_ge(sq_ready, 1)
            for i in range(4):
                last = nc.tensor.matmul(psum[:, 2 + i, :], C_("group"), sq[:, i, :], start=True, stop=True)
            last.then_inc(ss_filled, 1)
            pe.wait_ge(qkn_ready, 1)
            for i in range(4):
                last = nc.tensor.matmul(psum[:, 2 + i, :], C_("partner"), yc_flat[:, i * 512:(i + 1) * 512],
                                        start=True, stop=True)
            last.then_inc(turn_filled, 1)
            pe.wait_ge(gm_ready, 1)
            pe.wait_ge(vtok_ready, 2)
            pe.wait_ge(mix_gs, 1)
            for g in range(G8):
                nc.tensor.matmul(psum[:, g, :], C_("gt"), four(gm, g), start=True, stop=True).then_inc(dec_filled, 1)
            pe.wait_ge(masked_ready, 4)
            for g in range(G8):
                b, cc = g // C, g % C
                if g < 4:
                    pe.wait_ge(dec_exp, 2 * g + 2)
                else:
                    pe.wait_ge(u_ready, 2 * (g - 4) + 2)
                for i, src in enumerate((kz, qzm)):
                    nc.tensor.matmul(psum[:, 2 * (g % 4) + i, :], qk[:, C + cc, b, :], src[:, b, cc, :, :],
                                     start=True, stop=True).then_inc(kk_filled, 1)
            pe.wait_ge(u_ready, 2 * G8)
            for g in range(G8):
                for i in range(4):
                    last = nc.tensor.transpose(psum[:, g, i * P:(i + 1) * P], um[:, 4 * g + i, :], C_("ident"))
                last.then_inc(at_filled, 1)
            with pe.Fori(0, LEVELS - 1) as l:
                def merge_first(g):
                    pe.wait_ge(et_ready, l * G8 + (g + 1))
                    pe.wait_ge(x_upd, l * G8 + (g + 1))
                    if g >= 2:
                        pe.wait_ge(m1_ready, l * G8 + (g - 1))
                    for i in range(4):
                        last = nc.tensor.matmul(psum[:, g % 2, i * P:(i + 1) * P], etm[:, 4 * g + i, :],
                                                xi[:, 4 * g + i, :], start=True, stop=True)
                    last.then_inc(m1_filled, 1)

                def merge_second(g):
                    pe.wait_ge(m1_ready, l * G8 + (g + 1))
                    pe.wait_ge(x_upd, l * G8 + (G8 + g - 1 if g >= 2 else g + 7))
                    for i in range(4):
                        nc.tensor.matmul(psum[:, 2 + g % 2, i * P:(i + 1) * P], xt[:, 4 * g + i, :],
                                         m1[:, 4 * g + i, :], start=True, stop=True)
                    for i in range(4):
                        last = nc.tensor.matmul(psum[:, 4 + g % 2, i * P:(i + 1) * P], m1[:, 4 * g + i, :],
                                                xt[:, 4 * g + i, :], start=True, stop=True)
                    last.then_inc(xx_filled, 1)
                merge_first(0)
                merge_first(1)
                for g in range(G8):
                    merge_second(g)
                    if g + 2 < G8:
                        merge_first(g + 2)
            pe.wait_ge(x_upd, G8 * LEVELS)
            for b in range(B):
                for h in range(H):
                    last = nc.tensor.matmul(psum[:, b, h * DK:(h + 1) * DK], xi[:, b * H + h, :],
                                            vtok[:, b, h * DK:(h + 1) * DK], start=True, stop=True)
                last.then_inc(w_filled, 1)
            for b in range(B):
                pe.wait_ge(w_ready, b + 1)
                for h in range(H):
                    last = nc.tensor.matmul(psum[:, 2 + b, h * DK:(h + 1) * DK], pm[:, b * H + h, :],
                                            wmix[:, b, h * DK:(h + 1) * DK], start=True, stop=True)
                last.then_inc(o_filled, 1)
            pe.wait_ge(on_ready, 1)
            for b in range(B):
                for c in range(C):
                    last = nc.tensor.transpose(psum[:, 4 + b, c * P:(c + 1) * P], osb[:, b, c * P:(c + 1) * P], C_("ident"))
                last.then_inc(oT_filled, 1)
            need(pe, BLK_MIX + 4)
            pe.wait_ge(oT_ready, 2)
            for b in range(B):
                for c in range(C):
                    last = nc.tensor.matmul(psum[:, 6 + b, :], oT[:, c, b * P:(b + 1) * P], block(BLK_MIX + 4)[:, c, :],
                                            start=c == 0, stop=c == C - 1)
            last.then_inc(blk_used, 1)

        def mixer_act(act):
            norm_act(act, 1)
            act.wait_ge(pad_clear, 1)
            for i in range(3 * C // 2):
                m = i // 2
                if i % 2:
                    act.wait_ge(blk_used, BLK_MIX + m + 1)
                else:
                    act.wait_ge(mix_proj, 3 * m + 2)
                nc.scalar.copy(xpad[:, 2 * i:2 * i + 2, :, TAPS - 1:].rearrange("p n b t -> p (n b) t"),
                               bank4(2 + i)).then_inc(mix_evac, 1)
            act.wait_ge(blk_used, BLK_MIX + 4)
            nc.scalar.activation(gs[:, :, :], psum[:, 0:2, :], ACT.Silu).then_inc(mix_gs, 1)
            act.wait_ge(conv, 12 * TAPS)
            nc.scalar.activation(yc_flat, yc_flat, ACT.Silu).then_inc(mix_silu, 1)
            act.wait_ge(mix_z, 2)
            nc.scalar.activation(beta[:, :, :], z[:, :, H:], ACT.Sigmoid).then_inc(mix_beta, 1)
            link_a(act, nc.scalar.activation(zl[:, :, :], za[:, :, :], ACT.Exp, scale=-1.0))
            link_a(act, nc.scalar.activation(alog[:, :], R_("mix_alog"), ACT.Exp))
            nc.scalar.activation(zl[:, :, :], zl[:, :, :], ACT.Ln, bias=1.0).then_inc(mix_zl, 1)
            for b in range(B):
                act.wait_ge(vtok_filled, b + 1)
                nc.scalar.copy(vtok[:, b, :], psum[:, 6 + b, :]).then_inc(vtok_ready, 1)
            act.wait_ge(ss_filled, 1)
            nc.scalar.activation(rn, psum[:, 2:6, :], ACT.Sqrt, bias=epst[:, 1:2]).then_inc(ss_root, 1)
            for g in range(G8):
                act.wait_ge(dec_filled, g + 1)
                nc.scalar.activation(four(dec, g), bank4(g), ACT.Exp).then_inc(dec_exp, 1)
            for g in range(G8):
                act.wait_ge(at_filled, g + 1)
                nc.scalar.copy(four(at, g), bank4(g)).then_inc(at_ready, 1)
            with act.Fori(0, LEVELS - 1) as l:
                for g in range(G8):
                    act.wait_ge(m1_filled, l * G8 + (g + 1))
                    nc.scalar.copy(four(m1, g), bank4(g % 2)).then_inc(m1_ready, 1)
            for b in range(B):
                act.wait_ge(w_filled, b + 1)
                nc.scalar.copy(wmix[:, b, :], psum[:, b, :]).then_inc(w_ready, 1)
            act.wait_ge(oss_ready, 1)
            nc.scalar.activation(orn[:, :], oss[:, :], ACT.Sqrt, bias=epst[:, 0:1], scale=1.0 / DK).then_inc(oss_root, 1)
            for b in range(B):
                act.wait_ge(oT_filled, b + 1)
                nc.scalar.copy(oT[:, :, b * P:(b + 1) * P], psum[:, 4 + b, :].rearrange("p (c t) -> p c t", c=C)).then_inc(oT_ready, 1)

        def mixer_dve(dve):
            norm_dve(dve, 1)
            nc.vector.memset(xpad[:, :, :, 0:TAPS - 1], 0.0).then_inc(pad_clear, 1)
            for tap in range(TAPS):
                for n in range(3 * C):
                    w = K_("convw", n * TAPS + tap)
                    src = xpad[:, n, :, tap:tap + P]
                    if tap == 0:
                        dve.wait_ge(mix_evac, n // 2 + 1)
                        nc.vector.tensor_scalar(yc[:, n, :, :], src, w, None, ALU.mult).then_inc(conv, 1)
                    else:
                        dve.wait_ge(conv, 12 * (tap - 1) + n + 1)
                        nc.vector.scalar_tensor_tensor(yc[:, n, :, :], src, w, yc[:, n, :, :], ALU.mult, ALU.add).then_inc(conv, 1)
            dve.wait_ge(mix_gb, 1)
            dtbb = row[:, ROWS["mix_dt"][0]:ROWS["mix_dt"][0] + 2 * H]
            nc.vector.tensor_tensor(z[:, :, :], psum[:, 2, 0:B * 2 * H].rearrange("p (b n) -> p b n", b=B),
                                    per_row(dtbb, B), ALU.add).then_inc(mix_z, 1)
            dve.wait_ge(mix_z, 1)
            nc.vector.scalar_tensor_tensor(za[:, :, :], z[:, :, 0:H], -1.0, z[:, :, 0:H], ALU.mult, ALU.max).then_inc(mix_z, 1)
            dve.wait_ge(mix_silu, 1)
            qkflat = yc_flat[:, 0:2 * C * T].rearrange("p (a n) -> p a n", a=4)
            nc.vector.tensor_tensor(sq, qkflat, qkflat, ALU.mult).then_inc(sq_ready, 1)
            dve.wait_ge(mix_zl, 1)
            link(dve, nc.vector.scalar_tensor_tensor(gdec[:, :, :], z[:, :, 0:H], 0.0, zl[:, :, :], ALU.max, ALU.add))
            link(dve, nc.vector.scalar_tensor_tensor(gdec[:, :, :], gdec[:, :, :], -1.0, per_row(alog[:, :], B), ALU.mult, ALU.mult))
            dve.wait_ge(ss_root, 1)
            link(dve, nc.vector.reciprocal(rn, rn))
            nc.vector.tensor_tensor(qkflat, qkflat, rn, ALU.mult).then_inc(qkn_ready, 1)
            dve.wait_ge(qkn_ready, 1)
            qk16 = qk.rearrange("p n b t -> p (n b) t")
            y16 = yc_flat[:, 0:2 * C * T].rearrange("p (a n) -> p a n", a=2 * C * B)
            link(dve, nc.vector.tensor_tensor(qk16, y16, per_row(C_("ropec"), 2 * C * B), ALU.mult))
            dve.wait_ge(turn_filled, 1)
            link(dve, nc.vector.tensor_tensor(turn.rearrange("p (a n) t -> p a n t", a=4), psum[:, 2:6, :].rearrange("p a (n t) -> p a n t", n=4),
                                              C_("ropes").unsqueeze(1).unsqueeze(1).to_broadcast([P, 4, 4, P]), ALU.mult))
            link(dve, nc.vector.tensor_tensor(qk16, qk16, turn, ALU.add))
            gflat = gdec[:, :, :].rearrange("p b h -> p (b h)")
            bflat = beta[:, :, :].rearrange("p b h -> p (b h)")
            nc.vector.tensor_tensor(gm, per_row(C_("le"), BH), per_elem(gflat, P), ALU.mult).then_inc(gm_ready, 1)
            for b in range(B):
                for dst, n0 in ((kz, C), (qzm, 0)):
                    nc.vector.tensor_tensor(dst[:, b, :, :, :], qk[:, n0:n0 + C, b, :].unsqueeze(2).to_broadcast([P, C, 4, P]),
                                            K_("headmask", 0, 4).unsqueeze(1).unsqueeze(3).to_broadcast([P, C, 4, P]),
                                            ALU.mult).then_inc(masked_ready, 1)
            dve.wait_ge(mix_beta, 1)
            dve.wait_ge(dec_exp, G8)
            link(dve, nc.vector.tensor_tensor(dec, dec, per_elem(bflat, P), ALU.mult))
            link(dve, nc.vector.tensor_tensor(dec, dec, per_row(C_("le"), BH), ALU.mult))
            for g in range(G8):
                for i, dst in enumerate((um, pm)):
                    dve.wait_ge(kk_filled, 2 * g + i + 1)
                    nc.vector.tensor_tensor(four(dst, g), bank4(2 * (g % 4) + i), four(dec, g), ALU.mult).then_inc(u_ready, 1)
            dve.wait_ge(u_ready, 2 * G8)
            link(dve, nc.vector.tensor_tensor(xi, um, per_row(C_("up0"), BH), ALU.mult))
            link(dve, nc.vector.scalar_tensor_tensor(xi, xi, -1.0, per_row(C_("ident"), BH), ALU.mult, ALU.add))
            for g in range(G8):
                dve.wait_ge(at_ready, g + 1)
                link(dve, nc.vector.tensor_tensor(four(xt, g), four(at, g), per_row(C_("low0"), 4), ALU.mult))
                nc.vector.scalar_tensor_tensor(four(xt, g), four(xt, g), -1.0, per_row(C_("ident"), 4), ALU.mult, ALU.add).then_inc(x_upd, 1)
            with dve.Fori(0, LEVELS - 1) as l:
                mask = cst[:, ds(l * P + CONST["low1"], P)]
                for g in range(G8):
                    nc.vector.tensor_tensor(four(etm, g), four(at, g), per_row(mask, 4), ALU.mult).then_inc(et_ready, 1)
                for g in range(G8):
                    dve.wait_ge(xx_filled, l * G8 + (g + 1))
                    nc.vector.tensor_tensor(four(xi, g), four(xi, g), bank4(2 + g % 2), ALU.subtract)
                    nc.vector.tensor_tensor(four(xt, g), four(xt, g), bank4(4 + g % 2), ALU.subtract).then_inc(x_upd, 1)
            o32 = osb.rearrange("p b (h d) -> p (b h) d", h=H)
            q32 = osq.rearrange("p b (h d) -> p (b h) d", h=H)
            dve.wait_ge(o_filled, 2)
            link(dve, nc.vector.tensor_copy(osb, psum[:, 2:4, :]))
            link(dve, nc.vector.tensor_tensor(osq, osb, osb, ALU.mult))
            nc.vector.reduce_sum(oss[:, :], q32, AX.X).then_inc(oss_ready, 1)
            dve.wait_ge(oss_root, 1)
            link(dve, nc.vector.reciprocal(orn[:, :], orn[:, :]))
            link(dve, nc.vector.tensor_tensor(o32, o32, per_elem(orn[:, :], DK), ALU.mult))
            link(dve, nc.vector.tensor_tensor(o32, o32, per_row(R_("mix_gnorm"), BH), ALU.mult))
            nc.vector.tensor_tensor(osb, osb, gs[:, :, :], ALU.mult).then_inc(on_ready, 1)
            dve.wait_ge(blk_used, BLK_MIX + 5)
            link(dve, nc.vector.tensor_tensor(x_res[:, :, :], x_res[:, :, :], psum[:, 6:8, :], ALU.add))

        hid = [view(16384 + i * C * T, C, T) for i in range(2)]
        hsilu = view(16384 + 2 * C * T, C, T)
        acc = view(16384 + 3 * C * T, B, D)
        sc = sb("sc", [P, B, E])
        gt = {n: sb("gt_" + n, [P, B, E]) for n in ("abs", "rank", "top1", "top2", "rest", "weight")}
        gdist = sb("gdist", [P, 2, B, E])
        gkeep = sb("gkeep", [P, 2, B, E])
        gexp = sb("gexp", [P, 2, B, E])
        gm1 = sb("gm1", [P, B])
        gm2 = sb("gm2", [P, B])
        grm = sb("grm", [P, B])
        gsum = sb("gsum", [P, 2, B])
        wcur = sb("wcur", [P, B])
        posm = sb("posm", [P, B, E])
        overfull = sb("overfull", [P, 1], mybir.dt.int32)
        sel = view(16384, B, E, P)
        selw = view(18432, B, E, P)
        selT = view(20480, E, T)
        xgT = view(22528, C, E, P)
        shid = [view(26624 + i * C * P, C, P) for i in range(2)]
        ssilu = view(27648, C, P)
        yexp = view(28160, D)
        accT = view(28672, C, T)

        gate_filled = sem("gate_filled")
        gdist_ready = sem("gdist_ready")
        gexp_ready = sem("gexp_ready")
        up_filled = sem("up_filled")
        silu_ready = sem("silu_ready")
        hid_free = sem("hid_free")
        acc_upd = sem("acc_upd")
        wcur_ready = sem("wcur_ready")
        s_chain = sem("s_chain")
        chosen_ready = sem("chosen_ready")
        pos_filled = sem("pos_filled")
        overfull_known = sem("overfull_known")
        sel_ready = sem("sel_ready")
        xg_filled = sem("xg_filled")
        xg_ready = sem("xg_ready")
        selT_filled = sem("selT_filled")
        selT_ready = sem("selT_ready")
        scatter_filled = sem("scatter_filled")
        accT_filled = sem("accT_filled")
        moe_added = sem("moe_added")

        def experts_pe(pe):
            norm_pe(pe, 2)
            for b in range(B):
                for c in range(C):
                    last = nc.tensor.matmul(psum[:, 6, b * E:(b + 1) * E], xnT[:, c, b * P:(b + 1) * P],
                                            S_("gate")[:, c, :], start=c == 0, stop=c == C - 1)
            last.then_inc(gate_filled, 1)
            pe.wait_ge(chosen_ready, 1)
            chosen = gt["rest"]
            nc.tensor.matmul(psum[:, 7, 0:E], C_("le"), chosen[:, 0, :], start=True, stop=True)
            nc.tensor.matmul(psum[:, 7, E:2 * E], C_("le"), chosen[:, 1, :], start=True, stop=False)
            for o in (E, 2 * E):
                for i, w in enumerate(("le", "gt")):
                    last = nc.tensor.matmul(psum[:, 7, o:o + E], C_(w), chosen[:, 0, :],
                                            start=o == 2 * E and i == 0, stop=o == E and i == 1)
            for i, w in enumerate(("le", "gt")):
                last = nc.tensor.matmul(psum[:, 7, 2 * E:3 * E], C_(w), chosen[:, 1, :], start=False, stop=i == 1)
            last.then_inc(pos_filled, 1)
            pe.wait_ge(overfull_known, 1)
            most = pe.value_load(overfull[0:1, 0:1], min_val=0, max_val=T)
            with pe.If(most > P):
                dense_experts_pe(pe)
            with pe.Else():
                gathered_experts_pe(pe)

        def up_pe(pe, u, rounds, width, rhs, free):
            k = BLK_MOE + 3 * u
            need(pe, k, rounds)
            need(pe, k + 1, rounds)
            for f in range(4):
                pe.wait_ge(hid_free, free + (4 * u + f + 1))
                for i in range(2):
                    for c in range(C):
                        last = nc.tensor.matmul(psum[:, f, i * T:i * T + width], block(k + i)[:, c, f * P:(f + 1) * P],
                                                rhs(c), start=c == 0, stop=c == C - 1)
                    if f == 3:
                        last.then_inc(blk_used, 1)
                if f < 3:
                    last.then_inc(up_filled, 1)
            need(pe, k + 2, rounds)

        def dense_experts_pe(pe):
            with pe.Fori(0, E) as e:
                rounds = e * (3 * FQ // RING)
                for u in range(FQ):
                    up_pe(pe, u, rounds, T, lambda c: xnT[:, c, :], e * FC)
                    for f in range(4):
                        pe.wait_ge(hid_free, e * FC + (4 * u + f + 5))
                        if u == 0 and f == 0:
                            pe.wait_ge(acc_upd, e * B + 1)
                        for b in range(B):
                            last = nc.tensor.matmul(psum[:, 4 + b, :], hid[u % 2][:, f, b * P:(b + 1) * P],
                                                    block(BLK_MOE + 3 * u + 2)[:, f, :], start=u == 0 and f == 0,
                                                    stop=u == FQ - 1 and f == 3)
                    last.then_inc(blk_used, 1)

        def gathered_experts_pe(pe):
            pe.wait_ge(sel_ready, 1)
            for g in range(2):
                for c in range(C):
                    for b in range(B):
                        last = nc.tensor.matmul(psum[:, 4 * g + c, :], xn[:, b, c * P:(c + 1) * P],
                                                sel[:, b, 4 * g:4 * g + 4, :], start=b == 0, stop=b == B - 1)
                    last.then_inc(xg_filled, 1)
            pe.wait_ge(sel_ready, 2)
            pe.wait_ge(xg_ready, 4)
            for e in range(E):
                for b in range(B):
                    o = (e % 2) * T + b * P
                    last = nc.tensor.transpose(psum[:, e // 2, o:o + P], selw[:, b, e, :], C_("ident"))
                if e % 2:
                    last.then_inc(selT_filled, 1)
            pe.wait_ge(xg_ready, 8)
            pe.wait_ge(selT_ready, 4)
            with pe.Fori(0, E) as e:
                rounds = e * (3 * FQ // RING)
                for u in range(FQ):
                    up_pe(pe, u, rounds, P, lambda c: xgT[:, c, ds(e, 1), :], e * FC)
                    for f in range(4):
                        pe.wait_ge(hid_free, e * FC + (4 * u + f + 5))
                        if u == 0 and f == 0:
                            pe.wait_ge(acc_upd, e * 2 + 1)
                        last = nc.tensor.matmul(psum[:, 4, :], shid[u % 2][:, f, :], block(BLK_MOE + 3 * u + 2)[:, f, :],
                                                start=u == 0 and f == 0, stop=u == FQ - 1 and f == 3)
                    last.then_inc(blk_used, 1)
                pe.wait_ge(acc_upd, e * 2 + 2)
                for c in range(C):
                    last = nc.tensor.matmul(psum[:, 6 + c // 2, (c % 2) * T:(c % 2) * T + T], yexp[:, c * P:(c + 1) * P],
                                            selT[:, ds(e, 1), :], start=True, stop=True)
                last.then_inc(scatter_filled, 1)
            pe.wait_ge(acc_upd, 2 * E + 1)
            for b in range(B):
                for c in range(C):
                    last = nc.tensor.transpose(psum[:, b, c * P:(c + 1) * P], accT[:, c, b * P:(b + 1) * P], C_("ident"))
            last.then_inc(accT_filled, 1)

        def experts_act(act):
            norm_act(act, 2)
            act.wait_ge(gdist_ready, 1)
            nc.scalar.activation(gexp[:, :, :, :], gdist[:, :, :, :], ACT.Exp, scale=-1.0).then_inc(gexp_ready, 1)
            act.wait_ge(overfull_known, 1)
            most = act.value_load(overfull[0:1, 0:1], min_val=0, max_val=T)

            def silus(width, dst):
                with act.Fori(0, E) as e:
                    for u in range(FQ):
                        for f in range(4):
                            if f < 3:
                                act.wait_ge(up_filled, e * 12 + (3 * u + f + 1))
                            else:
                                act.wait_ge(blk_used, e * 12 + (BLK_MOE + 3 * u + 2))
                            nc.scalar.activation(dst[:, f, :], psum[:, f, 0:width], ACT.Silu).then_inc(silu_ready, 1)
            with act.If(most > P):
                silus(T, hsilu)
            with act.Else():
                for n in range(8):
                    act.wait_ge(xg_filled, n + 1)
                    nc.scalar.copy(xgT[:, n % 4, 4 * (n // 4):4 * (n // 4) + 4, :], bank4(n)).then_inc(xg_ready, 1)
                silus(P, ssilu)

        def gates_dve(dve):
            g = {k: v[:, :, :] for k, v in gt.items()}
            s = sc[:, :, :]
            tt = nc.vector.tensor_tensor
            stt = nc.vector.scalar_tensor_tensor
            rank = per_row(K_("rank", 0, E), B)
            dve.wait_ge(gate_filled, 1)
            link(dve, nc.vector.tensor_copy(s, psum[:, 6, 0:B * E].rearrange("p (b e) -> p b e", b=B)))
            link(dve, stt(g["abs"], s, -1.0, s, ALU.mult, ALU.max))
            m = (gm1[:, :], gm2[:, :])

            def choose(values, best, chosen):
                link(dve, nc.vector.reduce_max(best, values, AX.X))
                link(dve, tt(g["rank"], values, per_elem(best, E), ALU.is_equal))
                link(dve, tt(g["rank"], g["rank"], rank, ALU.mult))
                link(dve, nc.vector.reduce_max(grm[:, :], g["rank"], AX.X))
                link(dve, tt(chosen, g["rank"], per_elem(grm[:, :], E), ALU.is_equal))
            choose(s, m[0], g["top1"])
            link(dve, stt(g["rest"], g["top1"], -3.0e38, s, ALU.mult, ALU.add))
            choose(g["rest"], m[1], g["top2"])
            for i in range(2):
                link(dve, tt(gdist[:, i, :, :], per_elem(m[i], E), s, ALU.subtract))
                link(dve, tt(gkeep[:, i, :, :], per_elem(m[i], E), g["abs"], ALU.max))
                link(dve, stt(gkeep[:, i, :, :], gkeep[:, i, :, :], 2 * JITTER, gdist[:, i, :, :], ALU.mult, ALU.is_ge))
            link(dve, tt(g["rest"], gkeep[:, 1, :, :], g["top1"], ALU.mult))
            link(dve, tt(gkeep[:, 1, :, :], gkeep[:, 1, :, :], g["rest"], ALU.subtract))
            nc.vector.tensor_scalar(gdist[:, :, :, :], gdist[:, :, :, :], 0.0, None, ALU.max).then_inc(gdist_ready, 1)
            tt(g["rest"], g["top1"], g["top2"], ALU.add).then_inc(chosen_ready, 1)
            dve.wait_ge(gexp_ready, 1)
            link(dve, tt(gexp[:, :, :, :], gexp[:, :, :, :], gkeep[:, :, :, :], ALU.mult))
            link(dve, nc.vector.reduce_sum(gsum[:, :, :], gexp[:, :, :, :], AX.X))
            link(dve, nc.vector.reciprocal(gsum[:, :, :], gsum[:, :, :]))
            link(dve, tt(g["top1"], g["top1"], per_elem(gsum[:, 0, :], E), ALU.mult))
            link(dve, tt(g["top2"], g["top2"], per_elem(gsum[:, 1, :], E), ALU.mult))
            tt(g["weight"], g["top1"], g["top2"], ALU.add).then_inc(acc_upd, 1)
            dve.wait_ge(pos_filled, 1)
            link(dve, tt(posm[:, :, :], psum[:, 7, 0:2 * E].rearrange("p (b e) -> p b e", b=B), g["rest"], ALU.mult))
            link(dve, nc.vector.tensor_scalar(posm[:, :, :], posm[:, :, :], -1.0, None, ALU.add))
            nc.vector.reduce_max(overfull[:, :], psum[:, 7, 2 * E:3 * E], AX.X).then_inc(overfull_known, 1)

        def experts_dve(dve):
            norm_dve(dve, 2)
            for i in range(4):
                nc.vector.memset(acc[:, i // 2, (i % 2) * T:(i % 2) * T + T], 0.0).then_inc(hid_free, 1)
            gates_dve(dve)
            dve.wait_ge(overfull_known, 1)
            most = dve.value_load(overfull[0:1, 0:1], min_val=0, max_val=T)
            with dve.If(most > P):
                dense_experts_dve(dve)
            with dve.Else():
                gathered_experts_dve(dve)
            dve.wait_ge(moe_added, 1)

        def dense_experts_dve(dve):
            with dve.Fori(0, E) as e:
                dve.wait_ge(acc_upd, e * B + 1)
                nc.vector.tensor_copy(wcur[:, :].unsqueeze(2), gt["weight"][:, :, ds(e, 1)]).then_inc(wcur_ready, 1)
                for u in range(FQ):
                    for f in range(4):
                        dve.wait_ge(silu_ready, e * FC + (4 * u + f + 1))
                        nc.vector.tensor_tensor(hid[u % 2][:, f, :], hsilu[:, f, :], psum[:, f, T:2 * T], ALU.mult).then_inc(hid_free, 1)
                dve.wait_ge(wcur_ready, e + 1)
                dve.wait_ge(blk_used, e * 12 + (BLK_MOE + 12))
                for b in range(B):
                    nc.vector.scalar_tensor_tensor(acc[:, b, :], psum[:, 4 + b, :], wcur[:, b:b + 1], acc[:, b, :],
                                                   ALU.mult, ALU.add).then_inc(acc_upd, 1)
            dve.wait_ge(acc_upd, B * E + 1)
            nc.vector.tensor_tensor(x_res[:, :, :], x_res[:, :, :], acc, ALU.add).then_inc(moe_added, 1)

        def gathered_experts_dve(dve):
            flat = lambda v: v.rearrange("p b e s -> p (b e) s")
            nc.vector.tensor_tensor(flat(sel), per_row(C_("iota"), B * E),
                                    per_elem(posm[:, :, :].rearrange("p b e -> p (b e)"), P), ALU.is_equal).then_inc(sel_ready, 1)
            dve.wait_ge(sel_ready, 1)
            nc.vector.tensor_tensor(flat(selw), flat(sel), per_elem(gt["weight"][:, :, :].rearrange("p b e -> p (b e)"), P),
                                    ALU.mult).then_inc(sel_ready, 1)
            nc.vector.memset(accT, 0.0).then_inc(s_chain, 1)
            for n in range(4):
                dve.wait_ge(selT_filled, n + 1)
                nc.vector.tensor_copy(selT[:, 2 * n:2 * n + 2, :], psum[:, n, :].rearrange("p (e t) -> p e t", e=2)).then_inc(selT_ready, 1)
            dve.wait_ge(s_chain, 1)
            with dve.Fori(0, E) as e:
                for u in range(FQ):
                    for f in range(4):
                        dve.wait_ge(silu_ready, e * FC + (4 * u + f + 1))
                        nc.vector.tensor_tensor(shid[u % 2][:, f, :], ssilu[:, f, :], psum[:, f, T:T + P], ALU.mult).then_inc(hid_free, 1)
                dve.wait_ge(blk_used, e * 12 + (BLK_MOE + 12))
                nc.vector.tensor_copy(yexp, psum[:, 4, :]).then_inc(acc_upd, 1)
                dve.wait_ge(scatter_filled, e + 1)
                dve.wait_ge(acc_upd, e * 2 + 1)
                nc.vector.tensor_tensor(accT.rearrange("p (a c) t -> p a (c t)", a=2), accT.rearrange("p (a c) t -> p a (c t)", a=2),
                                        psum[:, 6:8, :], ALU.add).then_inc(acc_upd, 1)
            dve.wait_ge(accT_filled, 1)
            nc.vector.tensor_tensor(x_res[:, :, :], x_res[:, :, :], psum[:, 0:2, :], ALU.add).then_inc(moe_added, 1)

        qpT = view(16384, C, T)
        mem = view(17408, B, D)
        memT = view(18432, C, T)
        mkz = view(19456, B, 4, P)
        la = view(20480, B, H, P)
        laT = view(24576, B, H, P)
        x1oT = view(28672, C, T)
        mvt = sb("mvt", [P, B, DK])
        top8 = [sb(f"top8_{b}", [P, 8]) for b in range(B)]
        at8 = [sb(f"at8_{b}", [P, 8], u32) for b in range(B)]
        pick = [sb(f"pick{b}", [P, 1], u32) for b in range(B)]
        lm = sb("lm", [P, B, H])
        ls = sb("ls", [P, B, H])

        ctx_back = [sem(f"ctx_back{b}") for b in range(B)]
        qp_filled = sem("qp_filled")
        qp_ready = sem("qp_ready")
        pick_scores = sem("pick_scores")
        top_found = sem("top_found")
        at_found = sem("at_found")
        picked = sem("picked")
        mem_arrived = [sem(f"mem_arrived{b}") for b in range(B)]
        memT_filled = sem("memT_filled")
        memT_ready = sem("memT_ready")
        mk_filled = sem("mk_filled")
        mkz_ready = sem("mkz_ready")
        mv_filled = sem("mv_filled")
        mv_ready = sem("mv_ready")
        la_filled = sem("la_filled")
        la_shift = sem("la_shift")
        la_exp = sem("la_exp")
        la_ready = sem("la_ready")
        laT_filled = sem("laT_filled")
        laT_ready = sem("laT_ready")
        x1o_filled = sem("x1o_filled")
        x1o_ready = sem("x1o_ready")

        def cross1_pe(pe):
            norm_pe(pe, 3)
            need(pe, BLK_X1)
            for ec in range(C):
                for c in range(C):
                    last = nc.tensor.matmul(psum[:, 2 + ec // 2, (ec % 2) * T:(ec % 2) * T + T],
                                            block(BLK_X1)[:, c, ec * P:(ec + 1) * P], xnT[:, c, :],
                                            start=c == 0, stop=c == C - 1)
                if ec % 2:
                    last.then_inc(qp_filled if ec == 1 else blk_used, 1)
            pe.wait_ge(qp_ready, 2)
            for b in range(B):
                pe.wait_ge(ctx_back[b], 16)
                for kb in range(KB):
                    for c in range(C):
                        last = nc.tensor.matmul(psum[:, 4 - 4 * b + kb, :], qpT[:, c, b * P:(b + 1) * P],
                                                ctxT_sb[b][:, c, kb * 512:(kb + 1) * 512], start=c == 0, stop=c == C - 1)
                last.then_inc(pick_scores, 1)
            pe.wait_ge(at_found, 1)
            for b in range(B):
                pe.wait_ge(mem_arrived[b], 16)
                for c in range(C):
                    last = nc.tensor.transpose(psum[:, 4 + b, c * P:(c + 1) * P], mem[:, b, c * P:(c + 1) * P], C_("ident"))
                last.then_inc(memT_filled, 1)
            pe.wait_ge(memT_ready, 2)
            for c in range(C):
                last = nc.tensor.matmul(psum[:, 6, 0:T], S_("x1_k")[:, c, :], memT[:, c, :], start=c == 0, stop=c == C - 1)
            last.then_inc(mk_filled, 1)
            for b in range(B):
                for c in range(C):
                    last = nc.tensor.matmul(psum[:, 7, b * DK:(b + 1) * DK], memT[:, c, b * P:(b + 1) * P],
                                            S_("x1_v")[:, c, :], start=c == 0, stop=c == C - 1)
            last.then_inc(mv_filled, 1)
            pe.wait_ge(at_found, 2)
            for b in range(B):
                pe.wait_ge(mkz_ready, b + 1)
                if b == 1:
                    pe.wait_ge(mv_ready, 1)
                for j in range(C):
                    last = nc.tensor.matmul(psum[:, 4 * b + j, :], qpT[:, j, b * P:(b + 1) * P], mkz[:, b, :, :],
                                            start=True, stop=True)
                last.then_inc(la_filled, 1)
            for b in range(B):
                pe.wait_ge(la_ready, b + 1)
                for j in range(C):
                    for i in range(4):
                        last = nc.tensor.transpose(psum[:, 4 * b + j, i * P:(i + 1) * P], la[:, b, 4 * j + i, :], C_("ident"))
                    last.then_inc(laT_filled, 1)
            for b in range(B):
                pe.wait_ge(laT_ready, C * (b + 1))
                for i in range(4):
                    last = nc.tensor.matmul(psum[DK * i:DK * i + DK, b, :], mvt[:, b, :],
                                            laT[:, b, :, :].rearrange("p (j i) q -> p j i q", i=4)[:, :, i, :],
                                            start=True, stop=True)
                last.then_inc(x1o_filled, 1)
            need(pe, BLK_X1 + 1)
            for b in range(B):
                pe.wait_ge(x1o_ready, b + 1)
                for c in range(C):
                    last = nc.tensor.matmul(psum[:, 2 + b, :], x1oT[:, c, b * P:(b + 1) * P], block(BLK_X1 + 1)[:, c, :],
                                            start=c == 0, stop=c == C - 1)
            last.then_inc(blk_used, 1)

        def cross1_act(act):
            norm_act(act, 3)
            for i in range(2):
                if i == 0:
                    act.wait_ge(qp_filled, 1)
                else:
                    act.wait_ge(blk_used, BLK_X1 + 1)
                nc.scalar.copy(qpT[:, 2 * i:2 * i + 2, :], psum[:, 2 + i, :].rearrange("p (c t) -> p c t", c=2)).then_inc(qp_ready, 1)
            for b in range(B):
                act.wait_ge(memT_filled, b + 1)
                nc.scalar.copy(memT[:, :, b * P:(b + 1) * P], bank4(4 + b)).then_inc(memT_ready, 1)
            act.wait_ge(mv_filled, 1)
            nc.scalar.copy(mvt[:, :, :], psum[:, 7, 0:B * DK].rearrange("p (b d) -> p b d", b=B)).then_inc(mv_ready, 1)
            for b in range(B):
                act.wait_ge(la_shift, b + 1)
                nc.scalar.activation(la[:, b, :, :], la[:, b, :, :], ACT.Exp, scale=float(1.0 / np.sqrt(DK).astype(np.float32))).then_inc(la_exp, 1)
            for n in range(B * C):
                act.wait_ge(laT_filled, n + 1)
                nc.scalar.copy(laT[:, n // C, 4 * (n % C):4 * (n % C) + 4, :], bank4(n)).then_inc(laT_ready, 1)
            for b in range(B):
                act.wait_ge(x1o_filled, b + 1)
                nc.scalar.copy(x1oT[:, :, b * P:(b + 1) * P], bank4(b)).then_inc(x1o_ready, 1)

        def cross1_dve(dve):
            norm_dve(dve, 3)
            for b in range(B):
                dve.wait_ge(pick_scores, b + 1)
                scores = psum[:, 4 - 4 * b:8 - 4 * b, :].rearrange("p a n -> p (a n)")
                nc.vector.max(top8[b][:, :], scores).then_inc(top_found, 1)
                dve.wait_ge(top_found, b + 1)
                nc.vector.max_index(at8[b][:, :], top8[b][:, :], scores).then_inc(at_found, 1)
                dve.wait_ge(at_found, b + 1)
                nc.vector.tensor_scalar(pick[b][:, :], at8[b][:, 0:1], b * CTX, None, ALU.add).then_inc(picked, 1)
            dve.wait_ge(mk_filled, 1)
            for b in range(B):
                nc.vector.tensor_tensor(mkz[:, b, :, :], per_row(psum[:, 6, b * P:(b + 1) * P], 4),
                                        per_elem(K_("headmask", 0, 4), P), ALU.mult).then_inc(mkz_ready, 1)
            for b in range(B):
                dve.wait_ge(la_filled, b + 1)
                logits = psum[:, 4 * b:4 * b + 4, :].rearrange("p j (i m) -> p (j i) m", i=4)
                link(dve, nc.vector.reduce_max(lm[:, b, :], logits, AX.X))
                nc.vector.tensor_tensor(la[:, b, :, :], logits, per_elem(lm[:, b, :], P), ALU.subtract).then_inc(la_shift, 1)
            for b in range(B):
                dve.wait_ge(la_exp, b + 1)
                link(dve, nc.vector.reduce_sum(ls[:, b, :], la[:, b, :, :], AX.X))
                link(dve, nc.vector.reciprocal(ls[:, b, :], ls[:, b, :]))
                nc.vector.tensor_tensor(la[:, b, :, :], la[:, b, :, :], per_elem(ls[:, b, :], P), ALU.mult).then_inc(la_ready, 1)
            dve.wait_ge(blk_used, BLK_X1 + 2)
            link(dve, nc.vector.tensor_tensor(x_res[:, :, :], x_res[:, :, :], psum[:, 2:4, :], ALU.add))

        lz = view(0, 3, C, T)
        le = view(3 * C * T, 2, C, T)
        lqk = view(5 * C * T, 2, C, T)
        lkv = view(7 * C * T, C * B, P)
        lden = view(8 * C * T, C * B, P)
        lvT = view(9 * C * T, C, T)
        ly = view(10 * C * T, B, D)
        lkvs = sb("lkvs", [P, C * B])
        lks = sb("lks", [P, C * B])

        lin_filled = sem("lin_filled")
        lmin_ready = sem("lmin_ready")
        lexp_ready = sem("lexp_ready")
        lv_ready = sem("lv_ready")
        ly_ready = sem("ly_ready")
        lgelu = sem("lgelu")

        def linear_pe(pe):
            norm_pe(pe, 4)
            for m in range(3):
                need(pe, BLK_LIN + m)
                for cc in range(C):
                    for c in range(C):
                        last = nc.tensor.matmul(psum[:, 2 + 2 * m + cc // 2, (cc % 2) * T:(cc % 2) * T + T],
                                                block(BLK_LIN + m)[:, c, cc * P:(cc + 1) * P], xnT[:, c, :],
                                                start=c == 0, stop=c == C - 1)
                    if cc % 2:
                        last.then_inc(lin_filled if cc == 1 else blk_used, 1)
            need(pe, BLK_LIN + 3)
            pe.wait_ge(lv_ready, 1)
            for b in range(B):
                for c in range(C):
                    last = nc.tensor.matmul(psum[:, b, :], lvT[:, c, b * P:(b + 1) * P], block(BLK_LIN + 3)[:, c, :],
                                            start=c == 0, stop=c == C - 1)
            last.then_inc(blk_used, 1)

        def linear_act(act):
            norm_act(act, 4)
            split_hi(act, 0)
            act.wait_ge(lmin_ready, 1)
            nc.scalar.activation(le, le, ACT.Exp).then_inc(lexp_ready, 1)
            act.wait_ge(ly_ready, 1)
            nc.scalar.activation(ly, ly, ACT.Gelu_apprx_tanh).then_inc(lgelu, 1)

        def linear_dve(dve):
            norm_dve(dve, 4)
            for m in range(3):
                for cc in range(C):
                    if cc == 0:
                        dve.wait_ge(lin_filled, m + 1)
                    if cc == 2:
                        dve.wait_ge(blk_used, BLK_LIN + m + 1)
                    ins = nc.vector.tensor_scalar(lz[:, m, cc, :], psum[:, 2 + 2 * m + cc // 2, (cc % 2) * T:(cc % 2) * T + T],
                                                  K_("lin_b", m * C + cc), None, ALU.add)
                if m == 1:
                    link(dve, ins)
                    nc.vector.tensor_scalar(le, lz[:, 0:2, :, :], 0.0, None, ALU.min).then_inc(lmin_ready, 1)
            dve.wait_ge(lexp_ready, 1)
            flat = lambda v: v.rearrange("p m c t -> p (m c t)")
            link(dve, nc.vector.scalar_tensor_tensor(flat(lqk), flat(lz[:, 0:2, :, :]), 0.0, flat(le), ALU.max, ALU.add))
            q8 = lqk[:, 0, :, :].rearrange("p c (b t) -> p (c b) t", b=B)
            k8 = lqk[:, 1, :, :].rearrange("p c (b t) -> p (c b) t", b=B)
            v8 = lz[:, 2, :, :].rearrange("p c (b t) -> p (c b) t", b=B)
            link(dve, nc.vector.tensor_tensor(lkv, k8, v8, ALU.mult))
            link(dve, nc.vector.reduce_sum(lkvs[:, :], lkv, AX.X))
            link(dve, nc.vector.reduce_sum(lks[:, :], k8, AX.X))
            link(dve, nc.vector.tensor_tensor(lden, q8, per_elem(lks[:, :], P), ALU.mult))
            link(dve, nc.vector.tensor_scalar(lden, lden, 1e-6, None, ALU.add))
            link(dve, nc.vector.reciprocal(lden, lden))
            link(dve, nc.vector.tensor_tensor(lkv, q8, per_elem(lkvs[:, :], P), ALU.mult))
            nc.vector.tensor_tensor(lvT.rearrange("p c (b t) -> p (c b) t", b=B), lkv, lden, ALU.mult).then_inc(lv_ready, 1)
            dve.wait_ge(blk_used, BLK_LIN + 4)
            nc.vector.tensor_tensor(ly, psum[:, 0:2, :], per_row(R_("lin_bo"), B), ALU.add).then_inc(ly_ready, 1)
            split_lo(dve, 0)
            dve.wait_ge(lgelu, 1)
            link(dve, nc.vector.tensor_tensor(x_res[:, :, :], x_res[:, :, :], ly, ALU.add))

        o = 0
        heven = [view(o + i * FC * T, FC, T, one_pass=True) for i in range(2)]
        o += 2 * FC * T
        hodd = [view(o + i * FC * T, FC, T, one_pass=True) for i in range(2)]
        o += 2 * FC * T
        fxT = [view(o + i * C * T, C, T, one_pass=True) for i in range(2)]
        o += 2 * C * T
        whi = [view(o + i * BLK, BLK, one_pass=True) for i in range(2)]
        o += 2 * BLK
        wlo = [view(o + i * BLK, BLK, one_pass=True) for i in range(2)]
        o += 2 * BLK
        fsilu = view(o, 4, T)
        o += 4 * T
        fhid = view(o, 4, T)
        o += 4 * T
        fy = view(o, B, D)
        NFFN = NBLK - BLK_W12
        w_hi = sem("w_hi")
        w_lo = sem("w_lo")
        fxT_hi = sem("fxT_hi")
        fxT_lo = sem("fxT_lo")
        ffn_filled = sem("ffn_filled")
        ffn_act = sem("ffn_act")
        ffn_hi = sem("ffn_hi")
        ffn_lo = sem("ffn_lo")

        def split_hi(act, j, reg=None):
            k = BLK_W12 + j
            if reg is None:
                act.wait_ge(blk_arrived[k % RING], 16 * (k // RING + 1))
                if j >= 2:
                    act.wait_ge(blk_used, k - 1)
            else:
                act.wait_ge(blk_arrived[k % RING], reg * 16 + 16 * (k // RING + 1))
                act.wait_ge(blk_used, reg * RING + (k - 1))
            nc.scalar.copy(whi[j % 2], ring[k % RING][:, :]).then_inc(w_hi, 1)

        def split_lo(dve, j, reg=None):
            dve.wait_ge(w_hi, j + 1 if reg is None else reg * RING + (j + 1))
            nc.vector.tensor_tensor(wlo[j % 2], ring[(BLK_W12 + j) % RING][:, :], whi[j % 2].bitcast(fp32),
                                    ALU.subtract).then_inc(w_lo, 1)

        def parts_ready(pe, j, reg=None):
            pe.wait_ge(w_hi, j + 1 if reg is None else reg * RING + (j + 1))
            pe.wait_ge(w_lo, j + 1 if reg is None else reg * RING + (j + 1))

        def ffn_pe(pe):
            for b in range(B):
                pe.wait_ge(xn_ready, 2 * 5 + b + 1)
                for c in range(C):
                    last = nc.tensor.transpose(psum[:, b, c * P:(c + 1) * P], xn[:, b, c * P:(c + 1) * P], C_("ident"))
                last.then_inc(xnT_filled, 1)
            pe.wait_ge(fxT_hi, B)
            pe.wait_ge(fxT_lo, B)
            for n in range(FC):
                j, f = n // 2, n % 4
                if n % 2 == 0:
                    parts_ready(pe, j)
                    w = [v[j % 2].rearrange("p (c i n) -> p c i n", c=C, i=2) for v in (whi, wlo)]
                if n >= 4:
                    pe.wait_ge(ffn_lo, n - 3)
                for i in range(2):
                    for c in range(C):
                        for wp, xp in PARTS:
                            last = nc.tensor.matmul(psum[:, f, i * T:(i + 1) * T], w[wp][:, c, i, (n % 2) * P:(n % 2 + 1) * P],
                                                    fxT[xp][:, c, :], start=c == wp == xp == 0, stop=c == C - 1 and wp == 1)
                last.then_inc(blk_used if n % 2 else ffn_filled, 1)
            for layer, src in enumerate((heven, hodd)):
                j0 = FC // 2 + layer * FC
                with pe.Fori(0, FC // RING) as it:
                    for s in range(RING):
                        j = j0 + s
                        parts_ready(pe, j, it)
                        w = [v[j % 2].rearrange("p (c n) -> p c n", c=FC) for v in (whi, wlo)]
                        pe.wait_ge(ffn_act, it * RING + (FC * (layer + 1) + s - 3))
                        for c in range(FC):
                            if c == 0:
                                pe.wait_ge(ffn_lo, FC * (layer + 1) - 1)
                            if c == FC - 1:
                                pe.wait_ge(ffn_lo, FC * (layer + 1))
                            for wp, xp in PARTS:
                                last = nc.tensor.matmul(psum[:, 4 + s, 0:T], w[wp][:, c, :], src[xp][:, c, :],
                                                        start=c == wp == xp == 0, stop=c == FC - 1 and wp == 1)
                        last.then_inc(blk_used, 1)
            for n in range(FC):
                j = NFFN - FQ + n // 4
                if n % 4 == 0:
                    parts_ready(pe, j)
                    w = [v[j % 2].rearrange("p (c n) -> p c n", c=4) for v in (whi, wlo)]
                if n in (0, FC - 1):
                    pe.wait_ge(ffn_lo, 3 * FC - (n == 0))
                for b in range(B):
                    for wp, xp in PARTS:
                        last = nc.tensor.matmul(psum[:, b, :], heven[xp][:, n, b * P:(b + 1) * P], w[wp][:, n % 4, :],
                                                start=n == wp == xp == 0, stop=n == FC - 1 and wp == 1)
                if n % 4 == 3:
                    last.then_inc(blk_used, 1)

        def ffn_scalar(act):
            norm_std_act(act, 5)
            split_hi(act, 1)
            for b in range(B):
                act.wait_ge(xnT_filled, 2 * 5 + b + 1)
                nc.scalar.copy(fxT[0][:, :, b * P:(b + 1) * P], psum[:, b, :].rearrange("p (c t) -> p c t", c=C)).then_inc(fxT_hi, 1)
            for n in range(FC):
                j, f = n // 2, n % 4
                if n % 2:
                    split_hi(act, j + 2)
                act.wait_ge(blk_used if n % 2 else ffn_filled, BLK_W12 + j + 1 if n % 2 else j + 1)
                nc.scalar.activation(fsilu[:, f, :], psum[:, f, 0:T], ACT.Silu, scale=K_("w1_s", n)).then_inc(ffn_act, 1)
            for layer, (dst, name) in enumerate(((hodd, "h1_s"), (heven, "h2_s"))):
                j0, done = FC // 2 + layer * FC, FC * (layer + 1)
                with act.Fori(0, FC // RING) as it:
                    for s in range(RING):
                        split_hi(act, j0 + s + 2, it)
                        act.wait_ge(ffn_lo, it * RING + (done + s - 3))
                        act.wait_ge(blk_used, it * RING + (BLK_W12 + j0 + s + 1))
                        nc.scalar.activation(fhid[:, s:s + 1, :], psum[:, 4 + s, 0:T].unsqueeze(1), ACT.Gelu,
                                             scale=col[:, ds(it * RING + (COLS[name][0] + s), 1)]).then_inc(ffn_act, 1)
                        act.wait_ge(ffn_act, it * RING + (done + s + 1))
                        nc.scalar.copy(dst[0][:, ds(it * RING + s, 1), :], fhid[:, s:s + 1, :]).then_inc(ffn_hi, 1)
            for j in (NFFN - 2, NFFN - 1):
                split_hi(act, j)

        def ffn_dve(dve):
            norm_stats_dve(dve, 5)
            split_lo(dve, 1)
            for b in range(B):
                dve.wait_ge(fxT_hi, b + 1)
                nc.vector.tensor_tensor(fxT[1][:, :, b * P:(b + 1) * P], psum[:, b, :].rearrange("p (c t) -> p c t", c=C),
                                        fxT[0][:, :, b * P:(b + 1) * P].bitcast(fp32), ALU.subtract).then_inc(fxT_lo, 1)
            for n in range(FC):
                f = n % 4
                if n % 2:
                    split_lo(dve, n // 2 + 2)
                dve.wait_ge(ffn_act, n + 1)
                link(dve, nc.vector.scalar_tensor_tensor(fhid[:, f, :], psum[:, f, T:2 * T], K_("w2_s", n), fsilu[:, f, :],
                                                         ALU.mult, ALU.mult))
                link(dve, nc.vector.tensor_copy(heven[0][:, n, :], fhid[:, f, :]))
                nc.vector.tensor_tensor(heven[1][:, n, :], fhid[:, f, :], heven[0][:, n, :].bitcast(fp32),
                                        ALU.subtract).then_inc(ffn_lo, 1)
            for layer, dst in enumerate((hodd, heven)):
                j0 = FC // 2 + layer * FC
                with dve.Fori(0, FC // RING) as it:
                    for s in range(RING):
                        split_lo(dve, j0 + s + 2, it)
                        dve.wait_ge(ffn_hi, it * RING + (layer * FC + s + 1))
                        nc.vector.tensor_tensor(dst[1][:, ds(it * RING + s, 1), :], fhid[:, s:s + 1, :],
                                                dst[0][:, ds(it * RING + s, 1), :].bitcast(fp32), ALU.subtract).then_inc(ffn_lo, 1)
            for j in (NFFN - 2, NFFN - 1):
                split_lo(dve, j)
            dve.wait_ge(blk_used, NBLK)
            link(dve, nc.vector.tensor_tensor(fy, psum[:, 0:2, :], per_row(R_("w3_s"), B), ALU.mult))
            nc.vector.tensor_tensor(x_res[:, :, :], x_res[:, :, :], fy, ALU.add).then_inc(x_final, 1)

        block_ = ctx.enter_context(nc.Block())

        @block_.sync
        def _(sp):
            def load_wk(hp):
                sp.dma_start(wk_in, wk[ds(hp, 1)].rearrange("a p (c n) -> p (a c) n", c=C)).then_inc(wk_arrived, 16)

            def load_wq(hp):
                sp.dma_start(wq_sb, wq[ds(hp, 1)].rearrange("a p (c n) -> p (a c) n", c=C)).then_inc(wq_arrived, 16)

            def load_wv(g):
                sp.dma_start(wv_in, wv[ds(g, 1)].rearrange("a p (c n) -> p (a c) n", c=C)).then_inc(wv_arrived, 16)

            def load_ctx(b, kb):
                k = slice(kb * 512, (kb + 1) * 512)
                sp.dma_start(cx_in[:, :, k], ctxT[b][:, :, k]).then_inc(ctx_arrived[kb], 16)

            def next_weights(n, hp, m=None, g=None, next_ctx=False):
                sp.wait_ge(kq_filled, n * 5 + 4)
                load_wk(hp)
                if m is not None:
                    sp.wait_ge(v_filled, m * 8 + 8)
                    if next_ctx:
                        load_ctx(1, 0)
                    load_wv(g)
                    if next_ctx:
                        for kb in range(1, KB):
                            load_ctx(1, kb)
                sp.wait_ge(kq_filled, n * 5 + 5)
                load_wq(hp)

            sp.dma_start(x_res[:, :, :], x).then_inc(x_loaded, 16)
            load_wk(0)
            load_ctx(0, 0)
            sp.dma_start(col[:, :], cols).then_inc(loaded, 16)
            sp.dma_start(cst[:, :], consts).then_inc(loaded, 16)
            load_ctx(0, 1)
            load_ctx(0, 2)
            load_ctx(0, 3)
            load_wq(0)
            load_wv(0)
            sp.dma_start(row[:, :], rows.partition_broadcast(P)).then_inc(loaded, 16)
            sp.dma_start(sml[:, :], small).then_inc(loaded, 16)
            next_weights(0, 1)
            dma_block(sp, 0, 0)
            dma_block(sp, 1, 1)
            for b in range(B):
                with sp.Fori(0, PAIRS // 2 - 1) as g:
                    j, m = g * 2 + PAIRS * b, g + PAIRS // 2 * b
                    next_weights(j + 1, g * 2 + 2, m, g + 1)
                    next_weights(j + 2, g * 2 + 3)
                if b == 0:
                    next_weights(PAIRS - 1, 0, PAIRS // 2 - 1, 0, next_ctx=True)
                    next_weights(PAIRS, 1)
            sp.wait_ge(pv_done, 2 * PAIRS)
            dma_block(sp, 2, 2)
            dma_block(sp, 3, 3)
            for k in range(RING, 7):
                dma_block(sp, k, k, used=k - RING + 1)
            with sp.Fori(0, E) as e:
                for i in range(3 * FQ):
                    dma_block(sp, ds(e * 12 + (BLK_MOE + i), 1), BLK_MOE + i, used=e * 12 + (BLK_MOE + i - RING + 1))
            turns = (NBLK - BLK_X1) // RING
            with sp.Fori(0, turns) as i:
                for s in range(RING):
                    dma_block(sp, ds(i * RING + (BLK_X1 + s), 1), BLK_X1 + s, used=i * RING + (BLK_X1 + s - RING + 1))
            for k in range(BLK_X1 + turns * RING, NBLK):
                dma_block(sp, k, k, used=k - RING + 1)
            sp.wait_ge(x_final, 1)
            sp.dma_start(out, x_res[:, :, :]).then_inc(stored, 16)
            sp.wait_ge(stored, 16)

        @block_.gpsimd
        def _(gp):
            gp.wait_ge(blk_used, BLK_MOE + 3 * FQ)
            for b in range(B):
                gp.dma_start(ctxT_sb[b], ctxT[b]).then_inc(ctx_back[b], 16)
            for b in range(B):
                gp.wait_ge(picked, b + 1)
                gp.indirect_dma_start(out=mem[:, b, :], out_offset=None, in_=ctx_rows,
                                      in_offset=bass.IndirectOffsetOnAxis(ap=pick[b][:, :], axis=0)).then_inc(mem_arrived[b], 16)

        @block_.scalar
        def _(act):
            cross0_act(act)
            mixer_act(act)
            experts_act(act)
            cross1_act(act)
            linear_act(act)
            ffn_scalar(act)

        @block_.vector
        def _(dve):
            cross0_dve(dve)
            mixer_dve(dve)
            experts_dve(dve)
            cross1_dve(dve)
            linear_dve(dve)
            ffn_dve(dve)

        @block_.tensor
        def _(pe):
            cross0_pe(pe)
            mixer_pe(pe)
            experts_pe(pe)
            cross1_pe(pe)
            linear_pe(pe)
            ffn_pe(pe)


def _rows_to_partitions(w):
    n = w.shape[0] // P
    return w.reshape(n, P, w.shape[1]).transpose(1, 0, 2).reshape(P, n * w.shape[1])


def _columns(v):
    return v.reshape(-1, P).T


def _stream_blocks(a):
    def quarters(w):
        return [w[:, q * 512:(q + 1) * 512] for q in range(w.shape[1] // 512)]

    def row_quarters(w):
        return [w[q * 512:(q + 1) * 512] for q in range(w.shape[0] // 512)]

    mats = row_quarters(a["L0_xattn_Wo"])
    mats += [a["L0_attn_" + n] for n in ("Wq", "Wk", "Wv", "Wg", "Wo")]
    for e in range(E):
        for w1, w3, w2 in zip(quarters(a["L0_ffn_w1"][e].T), quarters(a["L0_ffn_w3"][e].T),
                              row_quarters(a["L0_ffn_w2"][e].T)):
            mats += [w1, w3, w2]
    mats += [a["L1_xattn_Wq"].T, a["L1_xattn_Wc"].T]
    mats += [a["L1_attn_" + n] for n in ("Wq", "Wk", "Wv", "Wo")]
    w1, w2 = a["L1_ffn_w1_w"].T, a["L1_ffn_w2_w"].T
    mats += [np.concatenate([w1[:, f:f + 2 * P], w2[:, f:f + 2 * P]], axis=1) for f in range(0, F, 2 * P)]
    for n in ("h1", "h2"):
        w = a[f"L1_ffn_{n}_w"].T
        mats += [w[:, f * P:(f + 1) * P] for f in range(FC)]
    mats += row_quarters(a["L1_ffn_w3_w"].T)
    return np.stack([_rows_to_partitions(m) for m in mats])


def kernel(**inputs):
    import concourse.bacc as _bacc
    from concourse.bass_utils import run_bass_kernel_spmd as _run

    a = {k: np.asarray(v) for k, v in inputs.items()}
    f32 = np.float32
    wq, wk = [np.stack([_rows_to_partitions(a["L0_xattn_W" + m][:, hp * P:(hp + 1) * P]) for hp in range(PAIRS)])
              for m in "qk"]
    wv = np.stack([_rows_to_partitions(a["L0_xattn_Wv"][:, g * T:(g + 1) * T]) for g in range(PAIRS // 2)])
    convw = np.stack([a[f"L0_attn_conv_{m}_w"].reshape(C, P, TAPS) for m in "qkv"]).transpose(2, 0, 1, 3).reshape(P, -1)
    headmask = (np.arange(P)[:, None] // DK == np.arange(4)[None, :]).astype(f32)
    rank = np.broadcast_to(np.arange(E, 0, -1).astype(f32), (P, E))
    cols = np.concatenate([_columns(a["L0_xattn_bq"]), _columns(a["L0_xattn_bk"]), _columns(a["L0_xattn_bv"]), convw,
                           _columns(a["L1_attn_bq"]), _columns(a["L1_attn_bk"]), _columns(a["L1_attn_bv"])]
                          + [_columns(a[f"L1_ffn_{n}_s"]) for n in ("w1", "w2", "h1", "h2")] + [headmask, rank], axis=1)
    rows = np.concatenate([a[n] for n in ("L0_xattn_bo", "L0_xattn_ln_gamma", "L0_xattn_ln_beta", "L0_attn_dt_bias",
                                          "L0_attn_bb", "L0_attn_A_log", "L0_attn_gnorm_w", "L1_attn_bo",
                                          "L1_ffn_w3_s")])
    wkv = a["L1_xattn_Wkv"]
    small = np.concatenate([_rows_to_partitions(m) for m in (
        np.concatenate([a["L0_attn_Wgk"], a["L0_attn_Wb"]], axis=1), a["L0_ffn_gate_w"].T,
        np.concatenate([wkv[:DK].T] * 4, axis=1), wkv[DK:].T)], axis=1)
    ctx = a["ctx_1024"]
    arrays = {
        "x": a["x"].transpose(1, 0, 2),
        "ctxT": ctx.transpose(0, 2, 1).reshape(B, C, P, CTX).transpose(0, 2, 1, 3),
        "ctx_rows": ctx.reshape(B * CTX, D),
        "wq": wq, "wk": wk, "wv": wv, "stream": _stream_blocks(a), "small": small, "cols": cols, "rows": rows, "consts": constants(),
    }
    nc = _bacc.Bacc("TRN2", target_bir_lowering=False, num_devices=1)
    arrays = {f"in_{n}": np.ascontiguousarray(v) for n, v in arrays.items()}
    args = [nc.dram_tensor(n, v.shape, mybir.dt.from_np(v.dtype), kind="ExternalInput").ap() for n, v in arrays.items()]
    out = nc.dram_tensor("out", (P, B, D), mybir.dt.float32, kind="ExternalOutput").ap()
    build(nc, *args, out)
    r = _run(nc, [arrays], core_ids=[0])
    return r.results[0]["out"].transpose(1, 0, 2)
```

```python
from contextlib import ExitStack

import numpy as np

import concourse.bass as bass
from concourse import mybir

P = 128
B = 2
D = 512
C = D // P
T = B * P
CTX = 2048
KB = CTX // 512
KC = CTX // P
H = 16
PAIRS = H // 2
DK = D // H
TAPS = 4
E = 8
F = 2048
FQ = F // 512
FC = F // P
BLK = 2048
RING = 4
LEVELS = 7
JITTER = 0.01
EPS = 1e-5

BLK_MIX = 0
BLK_MOE = 5
BLK_X1 = BLK_MOE + E * FQ * 3
BLK_LIN = BLK_X1 + 2
BLK_W12 = BLK_LIN + 4
BLK_H1 = BLK_W12 + 2 * FQ
BLK_H2 = BLK_H1 + FC
BLK_W3 = BLK_H2 + FC
NBLK = BLK_W3 + FQ

CONST_NAMES = ["ident", "le", "gt", "low0", "low1", "low2", "low3", "low4", "low5", "low6", "up0",
               "ropec", "ropes", "partner", "group", "iota"]
CONST = {n: P * i for i, n in enumerate(CONST_NAMES)}
NCONST = P * len(CONST_NAMES)
ROWS = {"x0_bo": (0, D), "x0_gamma": (D, D), "x0_beta": (2 * D, D), "mix_dt": (3 * D, H),
        "mix_bb": (3 * D + H, H), "mix_alog": (3 * D + 2 * H, H), "mix_gnorm": (3 * D + 3 * H, DK),
        "lin_bo": (3 * D + 3 * H + DK, D), "w3_s": (4 * D + 3 * H + DK, D)}
NROWS = 5 * D + 3 * H + DK
COLS = {"x0_bq": (0, PAIRS), "x0_bk": (8, PAIRS), "x0_bv": (16, PAIRS), "convw": (24, 3 * C * TAPS),
        "lin_b": (72, 3 * C), "w1_s": (84, FC), "w2_s": (100, FC), "h1_s": (116, FC), "h2_s": (132, FC),
        "headmask": (148, 4), "rank": (152, E)}
NCOLS = 152 + E
SMALL = {"mix_gb": (0, 2 * H), "gate": (C * 2 * H, E), "x1_k": (C * (2 * H + E), P), "x1_v": (C * (2 * H + E + P), DK)}
NSMALL = C * (2 * H + E + P + DK)

ARENA = 32768
ARENA_R = 8192


def constants():
    r, c = np.indices((P, P))
    t = {"ident": r == c, "le": r <= c, "gt": r > c}
    for l in range(LEVELS):
        m = 1 << l
        pair = (r // (2 * m) == c // (2 * m)) & (r // m != c // m)
        t[f"low{l}"] = pair & (r > c)
        if l == 0:
            t["up0"] = pair & (r < c)
    half = DK // 4
    d = np.arange(P) % DK
    inv = (np.float32(10000.0) ** (-np.arange(half, dtype=np.float32) / np.float32(half))).astype(np.float32)
    ang = (np.arange(P, dtype=np.float32)[None, :] * inv[d % half][:, None]).astype(np.float32)
    rot = (d < 2 * half)[:, None]
    t["ropec"] = np.where(rot, np.cos(ang), 1.0)
    t["ropes"] = np.where(rot, np.sin(ang), 0.0)
    dm, dk = c % DK, r % DK
    t["partner"] = (r // DK == c // DK) * ((dm < half) * (dk == dm + half) * -1.0
                                           + ((dm >= half) & (dm < 2 * half)) * (dk == dm - half))
    t["group"] = r // DK == c // DK
    t["iota"] = c
    return np.concatenate([t[n].astype(np.float32) for n in CONST_NAMES], axis=1)


def build(nc, x, ctxT, ctx_rows, wq, wk, wv, wo, stream, small, cols, rows, consts, out):
    fp32, f32r, u32 = mybir.dt.float32, mybir.dt.float32r, mybir.dt.uint32
    ALU = mybir.AluOpType
    ACT = mybir.ActivationFunctionType
    AX = mybir.AxisListType
    ds = bass.ds

    with ExitStack() as ctx:
        def sb(name, shape, dt=fp32):
            return ctx.enter_context(nc.sbuf_tensor(name, shape, dt))

        def sem(name):
            return ctx.enter_context(nc.semaphore(name))

        x_res = sb("x_res", [P, B, D])
        xn = sb("xn", [P, B, D])
        xnT = sb("xnT", [P, C, T])
        cst = sb("cst", [P, NCONST])
        row = sb("row", [P, NROWS])
        col = sb("col", [P, NCOLS])
        sml = sb("sml", [P, NSMALL])
        ring, ring_r = [], []
        for i in range(RING):
            with nc.sbuf_tensor(f"ring{i}", [P, BLK], fp32) as ring_memory:
                ring.append(ring_memory)
            ring_r.append(sb(f"ring_r{i}", [P, BLK], f32r))
        with nc.sbuf_tensor("arena", [P, ARENA], fp32) as arena_memory:
            arena = arena_memory
        arena_r = [sb(f"arena_r{i}", [P, ARENA_R], f32r) for i in range(ARENA // ARENA_R)]
        stats = sb("stats", [P, B, 6])
        mv = sb("mv", [P, B, 2])
        std = sb("std", [P, B])
        rstd = sb("rstd", [P, B])
        epst = sb("epst", [P, 2])
        psum = ctx.enter_context(nc.psum_tensor("psum", [P, 8, 512], fp32))

        def C_(name, w=P):
            return cst[:, CONST[name]:CONST[name] + w]

        def R_(name):
            a, w = ROWS[name]
            return row[:, a:a + w]

        def K_(name, i=0, n=1):
            return col[:, COLS[name][0] + i:COLS[name][0] + i + n]

        def S_(name):
            a, w = SMALL[name]
            return sml[:, a:a + C * w].rearrange("p (c n) -> p c n", c=C)

        def view(at, *shape, one_pass=False):
            n = int(np.prod(shape))
            assert at + n <= ARENA, (at, shape)
            if one_pass:
                assert at // ARENA_R == (at + n - 1) // ARENA_R, (at, shape)
                v = arena_r[at // ARENA_R][:, at % ARENA_R:at % ARENA_R + n]
            else:
                v = arena[:, at:at + n]
            if len(shape) == 1:
                return v
            letters = "abcd"[:len(shape)]
            return v.rearrange(f"p ({' '.join(letters)}) -> p {' '.join(letters)}",
                               **dict(zip(letters[:-1], shape[:-1])))

        def block(k):
            return ring[k % RING][:, :].rearrange("p (c n) -> p c n", c=C)

        def per_row(ap, n):
            return ap.unsqueeze(1).to_broadcast([P, n, ap.shape[-1]])

        def per_elem(ap, n):
            return ap.unsqueeze(2).to_broadcast([P, ap.shape[-1], n])

        x_loaded = sem("x_loaded")
        cst_loaded = sem("cst_loaded")
        loaded = sem("loaded")
        wq_arrived = sem("wq_arrived")
        wk_arrived = sem("wk_arrived")
        wv_arrived = sem("wv_arrived")
        ctx_arrived = [sem(f"ctx_arrived{kb}") for kb in range(KB)]
        blk_arrived = [sem(f"blk_arrived{i}") for i in range(RING)]
        blk_used = sem("blk_used")
        x_final = sem("x_final")
        stored = sem("stored")
        v_chain = sem("v_chain")
        a_chain = sem("a_chain")

        ln_var = sem("ln_var")
        ln_std = sem("ln_std")
        xn_ready = sem("xn_ready")
        xnT_filled = sem("xnT_filled")
        xnT_v = sem("xnT_v")
        xnT_a = sem("xnT_a")

        NLOADS = 2

        def dma_block(sp, k_dram, k_static, used=None):
            if used is not None:
                sp.wait_ge(blk_used, used)
            sp.dma_start(ring[k_static % RING][:, :], stream[k_dram] if isinstance(k_dram, int) else stream[k_dram].rearrange("a p n -> (a p) n")).then_inc(blk_arrived[k_static % RING], 16)

        def need(pe, k, more_rounds=None):
            turn = 16 * (k // RING + 1)
            pe.wait_ge(blk_arrived[k % RING], turn if more_rounds is None else more_rounds * 16 + turn)

        def link(dve, ins, count=[0]):
            count[0] += 1
            ins.then_inc(v_chain, 1)
            dve.wait_ge(v_chain, count[0])

        def link_a(act, ins, count=[0]):
            count[0] += 1
            ins.then_inc(a_chain, 1)
            act.wait_ge(a_chain, count[0])

        def norm_stats_dve(dve, n):
            for b in range(B):
                ins = nc.vector.bn_stats(stats[:, b, :], x_res[:, b, :])
                if b == B - 1:
                    link(dve, ins)
            for b in range(B):
                nc.vector.bn_aggr(mv[:, b, :], stats[:, b, :]).then_inc(ln_var, 1)
            dve.wait_ge(ln_std, n + 1)
            link(dve, nc.vector.reciprocal(rstd[:, :], std[:, :]))
            for b in range(B):
                nc.vector.tensor_scalar(xn[:, b, :], x_res[:, b, :], mv[:, b, 0:1], rstd[:, b:b + 1],
                                        ALU.subtract, ALU.mult).then_inc(xn_ready, 1)

        def norm_dve(dve, n):
            norm_stats_dve(dve, n)
            norm_turned_dve(dve, n)

        def norm_turned_dve(dve, n):
            dve.wait_ge(xnT_filled, 2 * n + 1)
            nc.vector.tensor_copy(xnT[:, :, 0:P], psum[:, 0, :].rearrange("p (c t) -> p c t", c=C)).then_inc(xnT_v, 1)

        def norm_std_act(act, n):
            act.wait_ge(ln_var, 2 * n + 2)
            nc.scalar.activation(std[:, :], mv[:, :, 1], ACT.Sqrt, bias=epst[:, 0:1]).then_inc(ln_std, 1)

        def norm_act(act, n):
            norm_std_act(act, n)
            norm_turned_act(act, n)

        def norm_turned_act(act, n):
            act.wait_ge(xnT_filled, 2 * n + 2)
            nc.scalar.copy(xnT[:, :, P:T], psum[:, 1, :].rearrange("p (c t) -> p c t", c=C)).then_inc(xnT_a, 1)

        def norm_pe(pe, n):
            for b in range(B):
                pe.wait_ge(xn_ready, 2 * n + b + 1)
                for c in range(C):
                    last = nc.tensor.transpose(psum[:, b, c * P:(c + 1) * P], xn[:, b, c * P:(c + 1) * P], C_("ident"))
                last.then_inc(xnT_filled, 1)
            pe.wait_ge(xnT_v, n + 1)
            pe.wait_ge(xnT_a, n + 1)

        PARTS = ((0, 0), (0, 1), (1, 0))

        def lo_part(out, v, hi):
            return nc.vector.tensor_tensor(out, v, hi.bitcast(fp32), ALU.subtract)

        ctxT_sb = [view(b * C * CTX, C, CTX) for b in range(B)]
        cx = [view(i * C * CTX, C, CTX, one_pass=True) for i in range(2)]
        cx_in = view(C * CTX, C, CTX)
        o = B * C * CTX
        kT = [[view(o + i * CTX, CTX, one_pass=True) for i in range(2)],
              [ring_r[i][:, :] for i in range(2)]]
        o += 2 * CTX
        pbuf = view(o, CTX)
        o += CTX
        pT = [view(o + h * CTX, KC, P) for h in range(2)]
        o += 2 * CTX
        qz_lo = sb("qz_lo", [P, 2, 2, P], f32r)
        qz = [[view(o + i * 2 * P, 2, P, one_pass=True) for i in range(2)], [qz_lo[:, i, :, :] for i in range(2)]]
        o += 2 * 2 * P
        attnT = view(o, PAIRS, T)
        o += PAIRS * T
        wq_sb = view(o, C, P)
        o += C * P
        wk_sb = [view(o + i * C * P, C, P, one_pass=True) for i in range(2)]
        wk_in = view(o + C * P, C, P)
        o += 2 * C * P
        wv_sb = [view(o + i * C * T, C, T, one_pass=True) for i in range(2)]
        wv_in = view(o + C * T, C, T)
        x0_y = view(o, B, D)
        wo_sb = view(0, PAIRS, D)
        vv = [ring[2 + i][:, :].rearrange("p (k n) -> p k n", n=2 * P) for i in range(2)]
        nmax = sb("nmax", [P, 3])
        rsum = sb("rsum", [P, 1])
        rinv = sb("rinv", [P, 1])

        ctx_hi = sem("ctx_hi")
        ctx_lo = sem("ctx_lo")
        wk_hi = sem("wk_hi")
        wk_lo = sem("wk_lo")
        wv_hi = sem("wv_hi")
        wv_lo = sem("wv_lo")
        kq_filled = sem("kq_filled")
        kq_hi = sem("kq_hi")
        kq_evac = sem("kq_evac")
        wo_arrived = sem("wo_arrived")
        v_filled = sem("v_filled")
        v_evac = sem("v_evac")
        scores_ready = sem("scores_ready")
        nmax_ready = sem("nmax_ready")
        rinv_ready = sem("rinv_ready")
        exp_ready = sem("exp_ready")
        p_ready = sem("p_ready")
        pT_filled = sem("pT_filled")
        pT_v = sem("pT_v")
        pT_a = sem("pT_a")
        pv_done = sem("pv_done")
        head_done = sem("head_done")
        x0_filled = sem("x0_filled")
        x0_std = sem("x0_std")
        x0_var = sem("x0_var")

        FIRST = (("k0", "v0", "k1", "v1"), ("v2", "v3"), ("k2", "v4", "k3", "v5"), ("v6", "v7", "q"))
        SECOND = (("k0", "k1"), (), ("k2", "k3"), ("q",))
        NOTHING = ((), (), (), ())

        def project_k(pe, bn, n, kb, own_bank):
            bank = 4 if own_bank else 4 + kb % 2
            if not isinstance(n, int):
                pe.wait_ge(kq_evac, n * 5 + (kb if own_bank or kb == 0 else kb - 1))
            elif n * 5 + kb > 1:
                pe.wait_ge(kq_evac, n * 5 + (kb if own_bank or kb == 0 else kb - 1))
            if kb == 0:
                pe.wait_ge(wk_lo, n + 1)
            pe.wait_ge(ctx_hi, bn * KB + kb + 1)
            for wp, xp in ((0, 0), (1, 0), (0, 1)):
                if xp == 1:
                    pe.wait_ge(ctx_lo, bn * KB + kb + 1)
                for c in range(C):
                    last = nc.tensor.matmul(psum[:, bank, :], wk_sb[wp][:, c, :], cx[xp][:, c, kb * 512:(kb + 1) * 512],
                                            start=c == wp == xp == 0, stop=c == C - 1 and xp == 1)
            last.then_inc(kq_filled, 1)

        def project_v(pe, m, i):
            if i == 0:
                pe.wait_ge(wv_lo, m + 1)
                pe.wait_ge(nmax_ready, m * 8 + 2)
            if i >= 2:
                pe.wait_ge(v_evac, m * 8 + (i - 1))
            for q in range(2):
                kc = 2 * i + q
                for c in range(C):
                    for wp, xp in PARTS:
                        last = nc.tensor.matmul(psum[:, 7 - i % 2 * 2, q * T:(q + 1) * T], cx[xp][:, c, kc * P:(kc + 1) * P],
                                                wv_sb[wp][:, c, :], start=c == wp == xp == 0, stop=c == C - 1 and wp == 1)
            last.then_inc(v_filled, 1)

        def project_q(pe, bn, n):
            pe.wait_ge(kq_evac, n * 5 + 4)
            pe.wait_ge(wq_arrived, n * 16 + 16)
            for c in range(C):
                last = nc.tensor.matmul(psum[:, 4, 0:P], wq_sb[:, c, :], xnT[:, c, bn * P:(bn + 1) * P],
                                        start=c == 0, stop=c == C - 1)
            last.then_inc(kq_filled, 1)

        def project(pe, pause, bn, n, m, second):
            for item in pause:
                if item[0] == "k":
                    project_k(pe, bn, n, int(item[1]), own_bank=not second)
                elif item[0] == "v":
                    project_v(pe, m, int(item[1]))
                else:
                    project_q(pe, bn, n)

        def out_proj(pe, b, pairs):
            for hp in pairs:
                last = nc.tensor.matmul(psum[:, 4 + b, :], attnT[:, hp, b * P:(b + 1) * P],
                                        wo_sb[:, hp, :], start=hp == 0, stop=hp == PAIRS - 1)
            return last

        def unit_pe(pe, bn, j, m, second, pauses):
            n = j + 1
            pe.wait_ge(kq_evac, j * 5 + 5)
            for h in range(2):
                for kb in range(KB):
                    if h == 1:
                        pe.wait_ge(pT_v if kb < 2 else pT_a, j * 4 + (kb % 2 + 1))
                    for qp, kp in PARTS:
                        last = nc.tensor.matmul(psum[:, kb, :], qz[qp][second][:, h, :], kT[kp][second][:, kb * 512:(kb + 1) * 512],
                                                start=qp == kp == 0, stop=qp == 1)
                    if kb % 2:
                        last.then_inc(scores_ready, 1)
                if pauses is NOTHING:
                    if h == 0:
                        pe.wait_ge(head_done, 2 * H - 2)
                        pe.wait_ge(wo_arrived, 16)
                        out_proj(pe, 0, range(PAIRS)).then_inc(x0_filled, 1)
                    else:
                        out_proj(pe, 1, range(PAIRS - 1))
                project(pe, pauses[2 * h], bn, n, m, second)
                for kb in range(KB):
                    if kb % 2 == 0:
                        pe.wait_ge(p_ready, j * 4 + (2 * h + kb // 2 + 1))
                    for q in range(4):
                        kc = 4 * kb + q
                        last = nc.tensor.transpose(psum[:, kb, q * P:(q + 1) * P], pbuf[:, kc * P:(kc + 1) * P], C_("ident"))
                    last.then_inc(pT_filled, 1)
                project(pe, pauses[2 * h + 1], bn, n, m, second)
            for kc in range(KC):
                if kc == 0:
                    pe.wait_ge(pT_v, j * 4 + 4)
                if kc == KC // 2:
                    pe.wait_ge(pT_a, j * 4 + 4)
                if not second and kc in (0, 14):
                    pe.wait_ge(v_evac, m * 8 + 7 + kc // 14)
                for h in range(2):
                    last = nc.tensor.matmul(psum[64 * h:64 * h + 64, 6 + h, 0:P],
                                            vv[kc // 8][:, kc % 8, second * P + 64 * h:second * P + 64 * h + 64],
                                            pT[h][:, kc, :], start=kc == 0, stop=kc == KC - 1)
            last.then_inc(pv_done, 1)

        def cross0_pe(pe):
            for kb in range(KB):
                if kb == 2:
                    pe.wait_ge(cst_loaded, 16)
                    norm_pe(pe, 0)
                project_k(pe, 0, 0, kb, own_bank=False)
            project_q(pe, 0, 0)
            for b in range(B):
                with pe.Fori(0, PAIRS // 2 - 1) as g:
                    unit_pe(pe, b, g * 2 + PAIRS * b, g + PAIRS // 2 * b, 0, FIRST)
                    unit_pe(pe, b, g * 2 + (PAIRS * b + 1), g + PAIRS // 2 * b, 1, SECOND)
                j, m = PAIRS * (b + 1) - 2, PAIRS // 2 * (b + 1) - 1
                unit_pe(pe, b, j, m, 0, FIRST)
                unit_pe(pe, b + 1, j + 1, m, 1, SECOND if b == 0 else NOTHING)
            pe.wait_ge(head_done, 2 * H)
            out_proj(pe, 1, (PAIRS - 1,)).then_inc(x0_filled, 1)

        def split_wk_dve(dve, n):
            dve.wait_ge(wk_hi, n + 1)
            lo_part(wk_sb[1], wk_in, wk_sb[0]).then_inc(wk_lo, 1)

        def split_wv_dve(dve, m):
            dve.wait_ge(wv_hi, m + 1)
            lo_part(wv_sb[1], wv_in, wv_sb[0]).then_inc(wv_lo, 1)

        def split_ctx_dve(dve, b, kb):
            dve.wait_ge(ctx_hi, b * KB + kb + 1)
            k = slice(kb * 512, (kb + 1) * 512)
            lo_part(cx[1][:, :, k], cx_in[:, :, k], cx[0][:, :, k]).then_inc(ctx_lo, 1)

        def evac_k_dve(dve, n, hp, kb, place, own_bank):
            dve.wait_ge(kq_filled, n * 5 + (kb + 1))
            hi, lo = [v[place][:, kb * 512:(kb + 1) * 512] for v in kT]
            keys, bias = psum[:, 4 if own_bank else 4 + kb % 2, :], col[:, ds(hp + COLS["x0_bk"][0], 1)]
            nc.vector.tensor_scalar(hi, keys, bias, None, ALU.add).then_inc(kq_hi, 1)
            dve.wait_ge(kq_hi, n * 5 + (kb + 1))
            nc.vector.scalar_tensor_tensor(lo, keys, bias, hi.bitcast(fp32), ALU.add, ALU.subtract).then_inc(kq_evac, 1)

        def evac_q_dve(dve, n, hp, place):
            dve.wait_ge(kq_filled, n * 5 + 5)
            rows = [slice(64 * h, 64 * h + 64) for h in range(2)]
            biases = [col[r, ds(hp + COLS["x0_bq"][0], 1)] for r in rows]
            for h, r in enumerate(rows):
                ins = nc.vector.tensor_scalar(qz[0][place][r, h, :], psum[r, 4, 0:P], biases[h], None, ALU.add)
            ins.then_inc(kq_hi, 1)
            dve.wait_ge(kq_hi, n * 5 + 5)
            for h, r in enumerate(rows):
                ins = nc.vector.scalar_tensor_tensor(qz[1][place][r, h, :], psum[r, 4, 0:P], biases[h],
                                                     qz[0][place][r, h, :].bitcast(fp32), ALU.add, ALU.subtract)
            ins.then_inc(kq_evac, 1)

        def evac_dve(dve, items, n, hpn, second):
            for item in items:
                if item[0] == "k":
                    evac_k_dve(dve, n, hpn, int(item[1]), 1 - second, own_bank=not second)
                elif item == "q":
                    evac_q_dve(dve, n, hpn, 1 - second)

        def unit_dve(dve, b, j, hp, m, second, pauses, hpn, switch=False):
            n = j + 1
            if pauses is not NOTHING:
                split_wk_dve(dve, n)
            if not second:
                split_wv_dve(dve, m)
            if switch:
                split_ctx_dve(dve, 1, 0)
            for h in range(2):
                u = j * 2 + h
                keys = [item for item in pauses[2 * h] if item[0] == "k"]
                for i in range(2):
                    dve.wait_ge(scores_ready, u * 2 + (i + 1))
                    ins = nc.vector.reduce_max(nmax[:, i + 1:i + 2], psum[:, 2 * i:2 * i + 2, :].rearrange("p a n -> p (a n)"), AX.X)
                ins.then_inc(nmax_ready, 1)
                dve.wait_ge(nmax_ready, u * 2 + 1)
                nc.vector.tensor_scalar(nmax[:, 0:1], nmax[:, 1:2], nmax[:, 2:3], -0.125, ALU.max, ALU.mult).then_inc(nmax_ready, 1)
                if switch and h == 0:
                    split_ctx_dve(dve, 1, 1)
                evac_dve(dve, keys[:1], n, hpn, second)
                dve.wait_ge(exp_ready, u + 1)
                nc.vector.reciprocal(rinv[:, :], rsum[:, :]).then_inc(rinv_ready, 1)
                dve.wait_ge(rinv_ready, u + 1)
                for i in range(2):
                    half = pbuf[:, i * CTX // 2:(i + 1) * CTX // 2]
                    nc.vector.tensor_scalar(half, half, rinv[:, 0:1], None, ALU.mult).then_inc(p_ready, 1)
                evac_dve(dve, keys[1:], n, hpn, second)
                for kb in range(2):
                    dve.wait_ge(pT_filled, u * 4 + (kb + 1))
                    nc.vector.tensor_copy(pT[h][:, 4 * kb:4 * kb + 4, :], psum[:, kb, :].rearrange("p (q t) -> p q t", q=4)).then_inc(pT_v, 1)
                if switch and h == 0:
                    split_ctx_dve(dve, 1, 2)
                    split_ctx_dve(dve, 1, 3)
                evac_dve(dve, pauses[2 * h + 1], n, hpn, second)
            if pauses is NOTHING:
                dve.wait_ge(loaded, 16 * NLOADS)
                dve.wait_ge(x0_filled, 1)
                out_norm_dve(dve, 0)
            dve.wait_ge(pv_done, j + 1)
            for h in range(2):
                nc.vector.tensor_scalar(attnT[64 * h:64 * h + 64, ds(hp, 1), b * P:(b + 1) * P],
                                        psum[64 * h:64 * h + 64, 6 + h, 0:P].unsqueeze(1),
                                        col[64 * h:64 * h + 64, ds(hp + COLS["x0_bv"][0], 1)], None, ALU.add).then_inc(head_done, 1)

        def out_norm_dve(dve, b):
            y = x0_y[:, b, :]
            link(dve, nc.vector.tensor_tensor(y, psum[:, 4 + b, :], xn[:, b, :], ALU.add))
            link(dve, nc.vector.tensor_tensor(y, y, R_("x0_bo"), ALU.add))
            link(dve, nc.vector.bn_stats(stats[:, b, :], y))
            nc.vector.bn_aggr(mv[:, b, :], stats[:, b, :]).then_inc(x0_var, 1)
            dve.wait_ge(x0_std, b + 1)
            link(dve, nc.vector.reciprocal(rstd[:, b:b + 1], std[:, b:b + 1]))
            link(dve, nc.vector.tensor_scalar(y, y, mv[:, b, 0:1], rstd[:, b:b + 1], ALU.subtract, ALU.mult))
            link(dve, nc.vector.tensor_tensor(y, y, R_("x0_gamma"), ALU.mult))
            link(dve, nc.vector.tensor_tensor(y, y, R_("x0_beta"), ALU.add))
            link(dve, nc.vector.tensor_tensor(x_res[:, b, :], x_res[:, b, :], y, ALU.add))

        def out_std_act(act, b):
            act.wait_ge(x0_var, b + 1)
            nc.scalar.activation(std[:, b:b + 1], mv[:, b, 1:2], ACT.Sqrt, bias=epst[:, 0:1]).then_inc(x0_std, 1)

        def cross0_dve(dve):
            nc.vector.memset(epst[:, 0:1], EPS)
            nc.vector.memset(epst[:, 1:2], 1e-6)
            for i in range(2):
                for part in range(2):
                    link(dve, nc.vector.memset(qz[part][i].bitcast(fp32), 0.0))
            dve.wait_ge(x_loaded, 32)
            norm_stats_dve(dve, 0)
            split_wk_dve(dve, 0)
            split_ctx_dve(dve, 0, 0)
            for kb in range(KB):
                if kb < KB - 1:
                    split_ctx_dve(dve, 0, kb + 1)
                evac_k_dve(dve, 0, 0, kb, 0, own_bank=False)
                if kb == 1:
                    norm_turned_dve(dve, 0)
            evac_q_dve(dve, 0, 0, 0)
            for b in range(B):
                with dve.Fori(0, PAIRS // 2 - 1) as g:
                    j, m = g * 2 + PAIRS * b, g + PAIRS // 2 * b
                    unit_dve(dve, b, j, g * 2, m, 0, FIRST, g * 2 + 1)
                    unit_dve(dve, b, j + 1, g * 2 + 1, m, 1, SECOND, g * 2 + 2)
                j, m = PAIRS * (b + 1) - 2, PAIRS // 2 * (b + 1) - 1
                unit_dve(dve, b, j, PAIRS - 2, m, 0, FIRST, PAIRS - 1)
                unit_dve(dve, b, j + 1, PAIRS - 1, m, 1, SECOND if b == 0 else NOTHING, 0, switch=b == 0)
            dve.wait_ge(x0_filled, 2)
            out_norm_dve(dve, 1)

        def split_wk_act(act, n):
            act.wait_ge(wk_arrived, n * 16 + 16)
            nc.scalar.copy(wk_sb[0], wk_in).then_inc(wk_hi, 1)

        def split_wv_act(act, m):
            act.wait_ge(wv_arrived, m * 16 + 16)
            nc.scalar.copy(wv_sb[0], wv_in).then_inc(wv_hi, 1)

        def split_ctx_act(act, b, kb):
            act.wait_ge(ctx_arrived[kb], b * 16 + 16)
            k = slice(kb * 512, (kb + 1) * 512)
            nc.scalar.copy(cx[0][:, :, k], cx_in[:, :, k]).then_inc(ctx_hi, 1)

        def evac_v_act(act, items, m):
            for item in items:
                if item[0] == "v":
                    i = int(item[1])
                    act.wait_ge(v_filled, m * 8 + (i + 1))
                    nc.scalar.copy(vv[i // 4][:, i % 4 * 2:i % 4 * 2 + 2, :],
                                   psum[:, 7 - i % 2 * 2, :].rearrange("p (q n) -> p q n", q=2)).then_inc(v_evac, 1)

        def unit_act(act, j, m, second, pauses, switch=False):
            if pauses is not NOTHING:
                split_wk_act(act, j + 1)
            if not second:
                split_wv_act(act, m)
            if switch:
                split_ctx_act(act, 1, 0)
                split_ctx_act(act, 1, 1)
            for h in range(2):
                u = j * 2 + h
                act.wait_ge(nmax_ready, u * 2 + 2)
                nc.scalar.activation(pbuf, psum[:, 0:KB, :].rearrange("p a n -> p (a n)"), ACT.Exp, bias=nmax[:, 0:1],
                                     scale=0.125, accum_out=rsum[:, 0:1]).then_inc(exp_ready, 1)
                if switch and h == 0:
                    split_ctx_act(act, 1, 2)
                    split_ctx_act(act, 1, 3)
                evac_v_act(act, pauses[2 * h], m)
                for kb in range(2, 4):
                    act.wait_ge(pT_filled, u * 4 + (kb + 1))
                    nc.scalar.copy(pT[h][:, 4 * kb:4 * kb + 4, :], psum[:, kb, :].rearrange("p (q t) -> p q t", q=4)).then_inc(pT_a, 1)
                evac_v_act(act, pauses[2 * h + 1], m)

        def cross0_act(act):
            norm_std_act(act, 0)
            split_wk_act(act, 0)
            for kb in range(KB):
                split_ctx_act(act, 0, kb)
                if kb == 2:
                    norm_turned_act(act, 0)
            for b in range(B):
                with act.Fori(0, PAIRS // 2 - 1) as g:
                    j, m = g * 2 + PAIRS * b, g + PAIRS // 2 * b
                    unit_act(act, j, m, 0, FIRST)
                    unit_act(act, j + 1, m, 1, SECOND)
                j, m = PAIRS * (b + 1) - 2, PAIRS // 2 * (b + 1) - 1
                unit_act(act, j, m, 0, FIRST)
                unit_act(act, j + 1, m, 1, SECOND if b == 0 else NOTHING, switch=b == 0)
            for b in range(B):
                out_std_act(act, b)

        BH = B * H
        G8 = BH // 4
        dec = view(0, BH, P)
        etm = dec
        gm = view(4096, BH, P)
        um = gm
        m1 = gm
        pm = view(8192, BH, P)
        at = view(12288, BH, P)
        xi = view(16384, BH, P)
        xt = view(20480, BH, P)
        xpad = view(24576, 3 * C, B, P + TAPS - 1)
        yc = view(24576 + 3 * C * B * (P + TAPS - 1), 3 * C, B, P)
        yc_flat = view(24576 + 3 * C * B * (P + TAPS - 1), 3 * C * B * P)
        vtok = view(24576 + 3 * C * B * (P + TAPS - 1) + 3 * C * T, B, D)
        sq = view(0, 4, 512)
        rn = view(24576, 4, 512)
        turn = view(8192, 2 * C * B, P)
        qrot = view(12288, C, B, P)
        krot = view(24576 + 3 * C * B * (P + TAPS - 1) + 2 * C * T, C, B, P)
        kz = view(16384, B, C, 4, P)
        qzm = view(24576, B, C, 4, P)
        wmix = view(24576, B, D)
        osb = view(24576 + B * D, B, D)
        osq = view(24576 + 2 * B * D, B, D)
        oT = view(24576 + 3 * B * D, C, T)
        gs = xn
        z = sb("z", [P, B, 2 * H])
        za = sb("za", [P, B, H])
        zl = sb("zl", [P, B, H])
        gdec = sb("gdec", [P, B, H])
        beta = sb("beta", [P, B, H])
        alog = sb("alog", [P, H])
        oss = sb("oss", [P, BH])
        orn = sb("orn", [P, BH])

        mix_proj = sem("mix_proj")
        mix_evac = sem("mix_evac")
        mix_gb = sem("mix_gb")
        mix_z = sem("mix_z")
        mix_zl = sem("mix_zl")
        mix_beta = sem("mix_beta")
        mix_gs = sem("mix_gs")
        conv = sem("conv")
        pad_clear = sem("pad_clear")
        mix_silu = sem("mix_silu")
        sq_ready = sem("sq_ready")
        ss_filled = sem("ss_filled")
        ss_root = sem("ss_root")
        qkn_ready = sem("qkn_ready")
        turn_filled = sem("turn_filled")
        vtok_filled = sem("vtok_filled")
        vtok_ready = sem("vtok_ready")
        gm_ready = sem("gm_ready")
        dec_filled = sem("dec_filled")
        dec_exp = sem("dec_exp")
        masked_ready = sem("masked_ready")
        kk_filled = sem("kk_filled")
        u_ready = sem("u_ready")
        at_filled = sem("at_filled")
        at_ready = sem("at_ready")
        xi_upd = sem("xi_upd")
        xt_filled = sem("xt_filled")
        xt_upd = sem("xt_upd")
        xi_g = sem("xi_g")
        xi_v = sem("xi_v")
        g_chain = sem("g_chain")
        dec_beta = sem("dec_beta")
        kz_ready = sem("kz_ready")
        qk_ready = sem("qk_ready")
        qk_filled = sem("qk_filled")
        pm_ready = sem("pm_ready")
        pm_masked = sem("pm_masked")
        et_ready = sem("et_ready")
        m1_filled = sem("m1_filled")
        m1_ready = sem("m1_ready")
        xx_filled = sem("xx_filled")
        w_filled = sem("w_filled")
        w_ready = sem("w_ready")
        o_filled = sem("o_filled")
        oss_ready = sem("oss_ready")
        oss_root = sem("oss_root")
        on_ready = sem("on_ready")
        oT_filled = sem("oT_filled")
        oT_ready = sem("oT_ready")

        def four(ap, g):
            return ap[:, 4 * g:4 * g + 4, :]

        def bank4(i):
            return psum[:, i, :].rearrange("p (a t) -> p a t", a=4)

        DEC_BANK = (0, 1, 6, 7)

        def mixer_pool(gp):
            gp.wait_ge(mix_zl, 1)
            nc.gpsimd.tensor_scalar(gdec[:, :, :], z[:, :, 0:H], 0.0, None, ALU.max).then_inc(g_chain, 1)
            gp.wait_ge(g_chain, 1)
            nc.gpsimd.tensor_tensor(gdec[:, :, :], gdec[:, :, :], zl[:, :, :], ALU.add).then_inc(g_chain, 1)
            gp.wait_ge(g_chain, 2)
            nc.gpsimd.tensor_tensor(gdec[:, :, :], gdec[:, :, :], per_row(alog[:, :], B), ALU.mult).then_inc(g_chain, 1)
            gp.wait_ge(g_chain, 3)
            gflat = gdec[:, :, :].rearrange("p b h -> p (b h)")
            bflat = beta[:, :, :].rearrange("p b h -> p (b h)")
            for g in range(G8):
                nc.gpsimd.tensor_tensor(four(gm, g), per_row(C_("le"), 4), per_elem(gflat[:, 4 * g:4 * g + 4], P), ALU.mult).then_inc(gm_ready, 1)
            gp.wait_ge(mix_beta, 1)
            for g in range(G8):
                gp.wait_ge(dec_exp, g + 1)
                nc.gpsimd.tensor_tensor(four(dec, g), four(dec, g), per_elem(bflat[:, 4 * g:4 * g + 4], P), ALU.mult).then_inc(dec_beta, 1)
            for g in range(G8 // 2):
                gp.wait_ge(u_ready, g + 1)
                if g == 0:
                    gp.wait_ge(kk_filled, G8)
                nc.gpsimd.tensor_tensor(four(xi, g), four(um, g), per_row(C_("up0"), 4), ALU.mult).then_inc(g_chain, 1)
                gp.wait_ge(g_chain, g + 4)
                nc.gpsimd.tensor_tensor(four(xi, g), per_row(C_("ident"), 4), four(xi, g), ALU.subtract).then_inc(xi_g, 1)
            for g in range(G8):
                gp.wait_ge(pm_ready, g + 1)
                nc.gpsimd.tensor_tensor(four(pm, g), four(pm, g), per_row(C_("le"), 4), ALU.mult).then_inc(pm_masked, 1)
            gp.wait_ge(mix_gs, 1)
            g32 = gs[:, :, :].rearrange("p b (h d) -> p (b h) d", h=H)
            nc.gpsimd.tensor_tensor(g32, g32, per_row(R_("mix_gnorm"), BH), ALU.mult).then_inc(g_chain, 1)

        def mixer_pe(pe):
            norm_pe(pe, 1)
            for m in range(3):
                need(pe, BLK_MIX + m)
                for cc in range(C):
                    n = C * m + cc
                    for c in range(C):
                        last = nc.tensor.matmul(psum[:, 2 + n // 2, (n % 2) * T:(n % 2) * T + T],
                                                block(BLK_MIX + m)[:, c, cc * P:(cc + 1) * P], xnT[:, c, :],
                                                start=c == 0, stop=c == C - 1)
                    last.then_inc(blk_used if cc == C - 1 else mix_proj, 1)
            pe.wait_ge(mix_evac, 1)
            for b in range(B):
                for c in range(C):
                    last = nc.tensor.matmul(psum[:, 2, b * 2 * H:(b + 1) * 2 * H], xnT[:, c, b * P:(b + 1) * P],
                                            S_("mix_gb")[:, c, :], start=c == 0, stop=c == C - 1)
            last.then_inc(mix_gb, 1)
            need(pe, BLK_MIX + 3)
            for b in range(B):
                for c in range(C):
                    last = nc.tensor.matmul(psum[:, b, :], xnT[:, c, b * P:(b + 1) * P], block(BLK_MIX + 3)[:, c, :],
                                            start=c == 0, stop=c == C - 1)
            last.then_inc(blk_used, 1)
            pe.wait_ge(sq_ready, 1)
            for i in range(4):
                last = nc.tensor.matmul(psum[:, 2 + i, :], C_("group"), sq[:, i, :], start=True, stop=True)
            last.then_inc(ss_filled, 1)
            pe.wait_ge(mix_silu, 2)
            for b in range(B):
                for cc in range(C):
                    last = nc.tensor.transpose(psum[:, 6 + b, cc * P:(cc + 1) * P], yc[:, 2 * C + cc, b, :], C_("ident"))
                last.then_inc(vtok_filled, 1)
            pe.wait_ge(vtok_ready, 2)
            pe.wait_ge(mix_gs, 1)
            for g in range(G8):
                pe.wait_ge(gm_ready, g + 1)
                if g >= 4:
                    pe.wait_ge(dec_exp, g - 3)
                nc.tensor.matmul(psum[:, DEC_BANK[g % 4], :], C_("gt"), four(gm, g), start=True, stop=True).then_inc(dec_filled, 1)
            pe.wait_ge(qkn_ready, 1)
            for i in range(4):
                last = nc.tensor.matmul(psum[:, 2 + i, :], C_("partner"), yc_flat[:, i * 512:(i + 1) * 512],
                                        start=True, stop=True)
            last.then_inc(turn_filled, 1)
            pe.wait_ge(dec_exp, G8)
            pe.wait_ge(kz_ready, 4)
            for g in range(G8):
                nc.tensor.matmul(psum[:, g, :], krot[:, g % C, g // C, :], kz[:, g // C, g % C, :, :],
                                 start=True, stop=True).then_inc(kk_filled, 1)
            for g in range(G8):
                pe.wait_ge(u_ready, g + 1)
                for i in range(4):
                    last = nc.tensor.transpose(psum[:, g, i * P:(i + 1) * P], um[:, 4 * g + i, :], C_("ident"))
                last.then_inc(at_filled, 1)
            for g in range(G8):
                pe.wait_ge(xi_g if g < G8 // 2 else xi_v, g % (G8 // 2) + 1)
                pe.wait_ge(at_ready, g + 1)
                for i in range(4):
                    last = nc.tensor.transpose(psum[:, g, i * P:(i + 1) * P], xi[:, 4 * g + i, :], C_("ident"))
                last.then_inc(xt_filled, 1)
            pe.wait_ge(masked_ready, 2)
            for g in range(G8):
                pe.wait_ge(xt_upd, g + 1)
                nc.tensor.matmul(psum[:, g, :], krot[:, g % C, g // C, :], qzm[:, g // C, g % C, :, :],
                                 start=True, stop=True).then_inc(qk_filled, 1)
            with pe.Fori(0, LEVELS - 1) as l:
                def merge_first(g):
                    pe.wait_ge(et_ready, l * G8 + (g + 1))
                    if g >= 2:
                        pe.wait_ge(m1_ready, l * G8 + (g - 1))
                    for i in range(4):
                        last = nc.tensor.matmul(psum[:, g % 2, i * P:(i + 1) * P], etm[:, 4 * g + i, :],
                                                xi[:, 4 * g + i, :], start=True, stop=True)
                    last.then_inc(m1_filled, 1)

                def merge_second(g):
                    pe.wait_ge(m1_ready, l * G8 + (g + 1))
                    pe.wait_ge(xt_upd, l * G8 + (g + 1))
                    if g >= 2:
                        pe.wait_ge(xi_upd, l * G8 + (g - 1))
                    for i in range(4):
                        last = nc.tensor.matmul(psum[:, 2 + g % 2, i * P:(i + 1) * P], xt[:, 4 * g + i, :],
                                                m1[:, 4 * g + i, :], start=True, stop=True)
                    last.then_inc(xx_filled, 1)

                def turn_x(g):
                    pe.wait_ge(xi_upd, l * G8 + (g + 1))
                    pe.wait_ge(xt_upd, l * G8 + (G8 + g - 1))
                    for i in range(4):
                        last = nc.tensor.transpose(psum[:, 4 + g % 2, i * P:(i + 1) * P], xi[:, 4 * g + i, :], C_("ident"))
                    last.then_inc(xt_filled, 1)
                merge_first(0)
                merge_first(1)
                for g in range(G8):
                    merge_second(g)
                    if g + 2 < G8:
                        merge_first(g + 2)
                    if g >= 1:
                        turn_x(g - 1)
                turn_x(G8 - 1)
            for b in range(B):
                for h in range(H):
                    last = nc.tensor.matmul(psum[:, b, h * DK:(h + 1) * DK], xi[:, b * H + h, :],
                                            vtok[:, b, h * DK:(h + 1) * DK], start=True, stop=True)
                last.then_inc(w_filled, 1)
            pe.wait_ge(pm_masked, G8)
            for b in range(B):
                pe.wait_ge(w_ready, b + 1)
                for h in range(H):
                    last = nc.tensor.matmul(psum[:, 2 + b, h * DK:(h + 1) * DK], pm[:, b * H + h, :],
                                            wmix[:, b, h * DK:(h + 1) * DK], start=True, stop=True)
                last.then_inc(o_filled, 1)
            for b in range(B):
                pe.wait_ge(on_ready, b + 1)
                for c in range(C):
                    last = nc.tensor.transpose(psum[:, 4 + b, c * P:(c + 1) * P], osb[:, b, c * P:(c + 1) * P], C_("ident"))
                last.then_inc(oT_filled, 1)
            need(pe, BLK_MIX + 4)
            pe.wait_ge(oT_ready, 2)
            for b in range(B):
                for c in range(C):
                    last = nc.tensor.matmul(psum[:, 6 + b, :], oT[:, c, b * P:(b + 1) * P], block(BLK_MIX + 4)[:, c, :],
                                            start=c == 0, stop=c == C - 1)
            last.then_inc(blk_used, 1)

        def mixer_act(act):
            norm_act(act, 1)
            act.wait_ge(pad_clear, 1)
            for i in range(3 * C // 2):
                m = i // 2
                if i % 2:
                    act.wait_ge(blk_used, BLK_MIX + m + 1)
                else:
                    act.wait_ge(mix_proj, 3 * m + 2)
                nc.scalar.copy(xpad[:, 2 * i:2 * i + 2, :, TAPS - 1:].rearrange("p n b t -> p (n b) t"),
                               bank4(2 + i)).then_inc(mix_evac, 1)
            act.wait_ge(conv, 8 * C)
            nc.scalar.activation(yc_flat[:, 0:2 * C * T], yc_flat[:, 0:2 * C * T], ACT.Silu).then_inc(mix_silu, 1)
            act.wait_ge(conv, 12 * C)
            nc.scalar.activation(yc_flat[:, 2 * C * T:], yc_flat[:, 2 * C * T:], ACT.Silu).then_inc(mix_silu, 1)
            act.wait_ge(blk_used, BLK_MIX + 4)
            nc.scalar.activation(gs[:, :, :], psum[:, 0:2, :], ACT.Silu).then_inc(mix_gs, 1)
            act.wait_ge(ss_filled, 1)
            nc.scalar.activation(rn, psum[:, 2:6, :], ACT.Sqrt, bias=epst[:, 1:2]).then_inc(ss_root, 1)
            act.wait_ge(mix_z, 2)
            link_a(act, nc.scalar.activation(zl[:, :, :], za[:, :, :], ACT.Exp, scale=-1.0))
            link_a(act, nc.scalar.activation(alog[:, :], R_("mix_alog"), ACT.Exp))
            nc.scalar.activation(zl[:, :, :], zl[:, :, :], ACT.Ln, bias=1.0).then_inc(mix_zl, 1)
            nc.scalar.activation(beta[:, :, :], z[:, :, H:], ACT.Sigmoid).then_inc(mix_beta, 1)
            for b in range(B):
                act.wait_ge(vtok_filled, b + 1)
                nc.scalar.copy(vtok[:, b, :], psum[:, 6 + b, :]).then_inc(vtok_ready, 1)
            for g in range(G8):
                act.wait_ge(dec_filled, g + 1)
                nc.scalar.activation(four(dec, g), bank4(DEC_BANK[g % 4]), ACT.Exp, scale=-1.0).then_inc(dec_exp, 1)
            act.wait_ge(qk_ready, 1)
            for i in range(4):
                nc.scalar.activation(kz[:, :, :, i, :], krot.rearrange("p c b t -> p b c t"), ACT.Identity,
                                     scale=K_("headmask", i)).then_inc(kz_ready, 1)
            for g in range(G8):
                act.wait_ge(at_filled, g + 1)
                nc.scalar.copy(four(at, g), bank4(g)).then_inc(at_ready, 1)
            for g in range(G8):
                act.wait_ge(xt_filled, g + 1)
                nc.scalar.copy(four(xt, g), bank4(g)).then_inc(xt_upd, 1)
            with act.Fori(0, LEVELS - 1) as l:
                def copy_m1(g):
                    act.wait_ge(m1_filled, l * G8 + (g + 1))
                    nc.scalar.copy(four(m1, g), bank4(g % 2)).then_inc(m1_ready, 1)

                def copy_xt(g):
                    act.wait_ge(xt_filled, l * G8 + (G8 + g + 1))
                    nc.scalar.copy(four(xt, g), bank4(4 + g % 2)).then_inc(xt_upd, 1)
                copy_m1(0)
                copy_m1(1)
                for g in range(G8):
                    if g + 2 < G8:
                        copy_m1(g + 2)
                    if g >= 1:
                        copy_xt(g - 1)
                copy_xt(G8 - 1)
            for b in range(B):
                act.wait_ge(w_filled, b + 1)
                nc.scalar.copy(wmix[:, b, :], psum[:, b, :]).then_inc(w_ready, 1)
            for b in range(B):
                act.wait_ge(oss_ready, b + 1)
                nc.scalar.activation(orn[:, b * H:(b + 1) * H], oss[:, b * H:(b + 1) * H], ACT.Sqrt, bias=epst[:, 0:1],
                                     scale=1.0 / DK).then_inc(oss_root, 1)
            for b in range(B):
                act.wait_ge(oT_filled, b + 1)
                nc.scalar.copy(oT[:, :, b * P:(b + 1) * P], psum[:, 4 + b, :].rearrange("p (c t) -> p c t", c=C)).then_inc(oT_ready, 1)

        def mixer_dve(dve):
            norm_dve(dve, 1)
            nc.vector.memset(xpad[:, :, :, 0:TAPS - 1], 0.0).then_inc(pad_clear, 1)
            for i in range(3 * C // 2):
                dve.wait_ge(mix_evac, i + 1)
                for tap in range(TAPS):
                    for n in (2 * i, 2 * i + 1):
                        w = K_("convw", n * TAPS + tap)
                        src = xpad[:, n, :, tap:tap + P]
                        if tap == 0:
                            nc.vector.tensor_scalar(yc[:, n, :, :], src, w, None, ALU.mult).then_inc(conv, 1)
                        else:
                            dve.wait_ge(conv, i * 2 * TAPS + 2 * (tap - 1) + n % 2 + 1)
                            nc.vector.scalar_tensor_tensor(yc[:, n, :, :], src, w, yc[:, n, :, :], ALU.mult, ALU.add).then_inc(conv, 1)
            dve.wait_ge(mix_gb, 1)
            dtbb = row[:, ROWS["mix_dt"][0]:ROWS["mix_dt"][0] + 2 * H]
            nc.vector.tensor_tensor(z[:, :, :], psum[:, 2, 0:B * 2 * H].rearrange("p (b n) -> p b n", b=B),
                                    per_row(dtbb, B), ALU.add).then_inc(mix_z, 1)
            dve.wait_ge(mix_z, 1)
            nc.vector.scalar_tensor_tensor(za[:, :, :], z[:, :, 0:H], -1.0, z[:, :, 0:H], ALU.mult, ALU.max).then_inc(mix_z, 1)
            dve.wait_ge(mix_silu, 1)
            qkflat = yc_flat[:, 0:2 * C * T].rearrange("p (a n) -> p a n", a=4)
            nc.vector.tensor_tensor(sq, qkflat, qkflat, ALU.mult).then_inc(sq_ready, 1)
            dve.wait_ge(ss_root, 1)
            link(dve, nc.vector.reciprocal(rn, rn))
            nc.vector.tensor_tensor(qkflat, qkflat, rn, ALU.mult).then_inc(qkn_ready, 1)
            dve.wait_ge(qkn_ready, 1)
            halves = [v.rearrange("p n b t -> p (n b) t") for v in (krot, qrot)]
            yhalves = [yc_flat[:, i * C * T:(i + 1) * C * T].rearrange("p (a n) -> p a n", a=C * B) for i in (1, 0)]
            dve.wait_ge(vtok_filled, 2)
            nc.vector.tensor_tensor(halves[0], yhalves[0], per_row(C_("ropec"), C * B), ALU.mult)
            link(dve, nc.vector.tensor_tensor(halves[1], yhalves[1], per_row(C_("ropec"), C * B), ALU.mult))
            dve.wait_ge(turn_filled, 1)
            link(dve, nc.vector.tensor_tensor(turn.rearrange("p (a n) t -> p a n t", a=4), psum[:, 2:6, :].rearrange("p a (n t) -> p a n t", n=4),
                                              C_("ropes").unsqueeze(1).unsqueeze(1).to_broadcast([P, 4, 4, P]), ALU.mult))
            for i in range(2):
                nc.vector.tensor_tensor(halves[i], halves[i], turn[:, (1 - i) * C * B:(2 - i) * C * B, :], ALU.add).then_inc(qk_ready, 1)
            dve.wait_ge(qk_ready, 2)
            for b in range(B):
                nc.vector.tensor_tensor(qzm[:, b, :, :, :], qrot[:, :, b, :].unsqueeze(2).to_broadcast([P, C, 4, P]),
                                        K_("headmask", 0, 4).unsqueeze(1).unsqueeze(3).to_broadcast([P, C, 4, P]),
                                        ALU.mult).then_inc(masked_ready, 1)
            for g in range(G8):
                dve.wait_ge(dec_beta, g + 1)
                dve.wait_ge(kk_filled, g + 1)
                nc.vector.tensor_tensor(four(um, g), bank4(g), four(dec, g), ALU.mult).then_inc(u_ready, 1)
            for g in range(G8 // 2, G8):
                dve.wait_ge(u_ready, g + 1)
                link(dve, nc.vector.scalar_tensor_tensor(four(xi, g), four(um, g), -1.0, per_row(C_("up0"), 4), ALU.mult, ALU.mult))
                nc.vector.tensor_tensor(four(xi, g), four(xi, g), per_row(C_("ident"), 4), ALU.add).then_inc(xi_v, 1)
            for g in range(G8):
                dve.wait_ge(qk_filled, g + 1)
                nc.vector.tensor_tensor(four(pm, g), bank4(g), four(dec, g), ALU.mult).then_inc(pm_ready, 1)
            dve.wait_ge(at_ready, G8)
            dve.wait_ge(pm_ready, G8)
            for g in range(G8):
                nc.vector.tensor_tensor(four(etm, g), four(at, g), per_row(C_("low1"), 4), ALU.mult).then_inc(et_ready, 1)
            with dve.Fori(0, LEVELS - 1) as l:
                mask = cst[:, ds(l * P + CONST["low2"], P)]
                for g in range(G8):
                    dve.wait_ge(xx_filled, l * G8 + (g + 1))
                    nc.vector.tensor_tensor(four(xi, g), four(xi, g), bank4(2 + g % 2), ALU.subtract).then_inc(xi_upd, 1)
                    nc.vector.tensor_tensor(four(etm, g), four(at, g), per_row(mask, 4), ALU.mult).then_inc(et_ready, 1)
            heads = lambda v: v.rearrange("p (h d) -> p h d", h=H)
            for b in range(B):
                dve.wait_ge(o_filled, b + 1)
                link(dve, nc.vector.tensor_copy(osb[:, b, :], psum[:, 2 + b, :]))
                link(dve, nc.vector.tensor_tensor(osq[:, b, :], osb[:, b, :], osb[:, b, :], ALU.mult))
                nc.vector.reduce_sum(oss[:, b * H:(b + 1) * H], heads(osq[:, b, :]), AX.X).then_inc(oss_ready, 1)
            dve.wait_ge(g_chain, 8)
            for b in range(B):
                dve.wait_ge(oss_root, b + 1)
                r = orn[:, b * H:(b + 1) * H]
                link(dve, nc.vector.reciprocal(r, r))
                link(dve, nc.vector.tensor_tensor(heads(osb[:, b, :]), heads(osb[:, b, :]), per_elem(r, DK), ALU.mult))
                nc.vector.tensor_tensor(osb[:, b, :], osb[:, b, :], gs[:, b, :], ALU.mult).then_inc(on_ready, 1)
            dve.wait_ge(blk_used, BLK_MIX + 5)
            link(dve, nc.vector.tensor_tensor(x_res[:, :, :], x_res[:, :, :], psum[:, 6:8, :], ALU.add))

        hid = [view(16384 + i * C * T, C, T) for i in range(2)]
        hsilu = view(16384 + 2 * C * T, C, T)
        acc = view(16384 + 3 * C * T, B, D)
        sc = sb("sc", [P, B, E])
        gt = {n: sb("gt_" + n, [P, B, E]) for n in ("abs", "rank", "top1", "top2", "rest", "weight")}
        gdist = sb("gdist", [P, 2, B, E])
        gkeep = sb("gkeep", [P, 2, B, E])
        gexp = sb("gexp", [P, 2, B, E])
        gm1 = sb("gm1", [P, B])
        gm2 = sb("gm2", [P, B])
        grm = sb("grm", [P, B])
        gsum = sb("gsum", [P, 2, B])
        wcur = sb("wcur", [P, B])
        posm = sb("posm", [P, B, E])
        overfull = sb("overfull", [P, 1], mybir.dt.int32)
        sel = view(16384, B, E, P, one_pass=True)
        xn_parts = [view(29696 + i * B * D, B, D, one_pass=True) for i in range(2)]
        selw = view(18432, B, E, P)
        selT = view(20480, E, T)
        xgT = view(22528, C, E, P)
        shid = [view(26624 + i * C * P, C, P) for i in range(2)]
        ssilu = view(27648, C, P)
        yexp = view(28160, D)
        accT = view(28672, C, T)

        gate_filled = sem("gate_filled")
        gdist_ready = sem("gdist_ready")
        gexp_ready = sem("gexp_ready")
        up_filled = sem("up_filled")
        silu_ready = sem("silu_ready")
        hid_free = sem("hid_free")
        acc_upd = sem("acc_upd")
        wcur_ready = sem("wcur_ready")
        s_chain = sem("s_chain")
        chosen_ready = sem("chosen_ready")
        pos_filled = sem("pos_filled")
        overfull_known = sem("overfull_known")
        norm_hi = sem("norm_hi")
        norm_lo = sem("norm_lo")
        sel_ready = sem("sel_ready")
        xg_filled = sem("xg_filled")
        xg_ready = sem("xg_ready")
        selT_filled = sem("selT_filled")
        selT_ready = sem("selT_ready")
        scatter_filled = sem("scatter_filled")
        accT_filled = sem("accT_filled")
        moe_added = sem("moe_added")

        def experts_pe(pe):
            norm_pe(pe, 2)
            for b in range(B):
                for c in range(C):
                    last = nc.tensor.matmul(psum[:, 6, b * E:(b + 1) * E], xnT[:, c, b * P:(b + 1) * P],
                                            S_("gate")[:, c, :], start=c == 0, stop=c == C - 1)
            last.then_inc(gate_filled, 1)
            pe.wait_ge(chosen_ready, 1)
            chosen = gt["rest"]
            nc.tensor.matmul(psum[:, 7, 0:E], C_("le"), chosen[:, 0, :], start=True, stop=True)
            nc.tensor.matmul(psum[:, 7, E:2 * E], C_("le"), chosen[:, 1, :], start=True, stop=False)
            for o in (E, 2 * E):
                for i, w in enumerate(("le", "gt")):
                    last = nc.tensor.matmul(psum[:, 7, o:o + E], C_(w), chosen[:, 0, :],
                                            start=o == 2 * E and i == 0, stop=o == E and i == 1)
            for i, w in enumerate(("le", "gt")):
                last = nc.tensor.matmul(psum[:, 7, 2 * E:3 * E], C_(w), chosen[:, 1, :], start=False, stop=i == 1)
            last.then_inc(pos_filled, 1)
            pe.wait_ge(norm_lo, 1)
            pe.wait_ge(overfull_known, 1)
            most = pe.value_load(overfull[0:1, 0:1], min_val=0, max_val=T)
            with pe.If(most > P):
                dense_experts_pe(pe)
            with pe.Else():
                gathered_experts_pe(pe)

        def up_pe(pe, u, rounds, width, rhs, done):
            k = BLK_MOE + 3 * u
            for i in range(2):
                need(pe, k + i, rounds)
                for f in range(4):
                    if i == 0:
                        pe.wait_ge(hid_free, done + (4 * u + f + 1))
                    else:
                        pe.wait_ge(silu_ready, done + (4 * u + f + 1))
                    for c in range(C):
                        last = nc.tensor.matmul(psum[:, f, i * T:i * T + width], block(k + i)[:, c, f * P:(f + 1) * P],
                                                rhs(c), start=c == 0, stop=c == C - 1)
                    last.then_inc(up_filled if f < 3 else blk_used, 1)
            need(pe, k + 2, rounds)

        def up_ready(eng, e, u, i, f):
            if f < 3:
                eng.wait_ge(up_filled, e * (6 * FQ) + (6 * u + 3 * i + f + 1))
            else:
                eng.wait_ge(blk_used, e * (3 * FQ) + (BLK_MOE + 3 * u + i + 1))

        def dense_experts_pe(pe):
            with pe.Fori(0, E) as e:
                rounds = e * (3 * FQ // RING)
                for u in range(FQ):
                    up_pe(pe, u, rounds, T, lambda c: xnT[:, c, :], e * FC)
                    for f in range(4):
                        pe.wait_ge(hid_free, e * FC + (4 * u + f + 5))
                        if u == 0 and f == 0:
                            pe.wait_ge(acc_upd, e * B + 1)
                        for b in range(B):
                            last = nc.tensor.matmul(psum[:, 4 + b, :], hid[u % 2][:, f, b * P:(b + 1) * P],
                                                    block(BLK_MOE + 3 * u + 2)[:, f, :], start=u == 0 and f == 0,
                                                    stop=u == FQ - 1 and f == 3)
                    last.then_inc(blk_used, 1)

        def gathered_experts_pe(pe):
            pe.wait_ge(sel_ready, 1)
            for g in range(2):
                for c in range(C):
                    for b in range(B):
                        for i, xp in enumerate(xn_parts):
                            last = nc.tensor.matmul(psum[:, 4 * g + c, :], xp[:, b, c * P:(c + 1) * P],
                                                    sel[:, b, 4 * g:4 * g + 4, :], start=b == i == 0, stop=b == i == 1)
                    last.then_inc(xg_filled, 1)
            pe.wait_ge(sel_ready, 2)
            pe.wait_ge(xg_ready, 4)
            for e in range(E):
                for b in range(B):
                    o = (e % 2) * T + b * P
                    last = nc.tensor.transpose(psum[:, e // 2, o:o + P], selw[:, b, e, :], C_("ident"))
                if e % 2:
                    last.then_inc(selT_filled, 1)
            pe.wait_ge(xg_ready, 8)
            pe.wait_ge(selT_ready, 4)
            with pe.Fori(0, E) as e:
                rounds = e * (3 * FQ // RING)
                for u in range(FQ):
                    up_pe(pe, u, rounds, P, lambda c: xgT[:, c, ds(e, 1), :], e * FC)
                    for f in range(4):
                        pe.wait_ge(hid_free, e * FC + (4 * u + f + 5))
                        if u == 0 and f == 0:
                            pe.wait_ge(acc_upd, e * 2 + 1)
                        last = nc.tensor.matmul(psum[:, 4, :], shid[u % 2][:, f, :], block(BLK_MOE + 3 * u + 2)[:, f, :],
                                                start=u == 0 and f == 0, stop=u == FQ - 1 and f == 3)
                    last.then_inc(blk_used, 1)
                pe.wait_ge(acc_upd, e * 2 + 2)
                for c in range(C):
                    last = nc.tensor.matmul(psum[:, 6 + c // 2, (c % 2) * T:(c % 2) * T + T], yexp[:, c * P:(c + 1) * P],
                                            selT[:, ds(e, 1), :], start=True, stop=True)
                last.then_inc(scatter_filled, 1)
            pe.wait_ge(acc_upd, 2 * E + 1)
            for b in range(B):
                for c in range(C):
                    last = nc.tensor.transpose(psum[:, b, c * P:(c + 1) * P], accT[:, c, b * P:(b + 1) * P], C_("ident"))
            last.then_inc(accT_filled, 1)

        def experts_act(act):
            norm_act(act, 2)
            act.wait_ge(xn_ready, 2 * 2 + 2)
            nc.scalar.copy(xn_parts[0], xn[:, :, :]).then_inc(norm_hi, 1)
            act.wait_ge(gdist_ready, 1)
            nc.scalar.activation(gexp[:, :, :, :], gdist[:, :, :, :], ACT.Exp, scale=-1.0).then_inc(gexp_ready, 1)
            act.wait_ge(overfull_known, 1)
            most = act.value_load(overfull[0:1, 0:1], min_val=0, max_val=T)

            def silus(width, dst):
                with act.Fori(0, E) as e:
                    for u in range(FQ):
                        for f in range(4):
                            up_ready(act, e, u, 0, f)
                            nc.scalar.activation(dst[:, f, :], psum[:, f, 0:width], ACT.Silu).then_inc(silu_ready, 1)
            with act.If(most > P):
                silus(T, hsilu)
            with act.Else():
                for n in range(8):
                    act.wait_ge(xg_filled, n + 1)
                    nc.scalar.copy(xgT[:, n % 4, 4 * (n // 4):4 * (n // 4) + 4, :], bank4(n)).then_inc(xg_ready, 1)
                silus(P, ssilu)

        def gates_dve(dve):
            g = {k: v[:, :, :] for k, v in gt.items()}
            s = sc[:, :, :]
            tt = nc.vector.tensor_tensor
            stt = nc.vector.scalar_tensor_tensor
            rank = per_row(K_("rank", 0, E), B)
            dve.wait_ge(gate_filled, 1)
            link(dve, nc.vector.tensor_copy(s, psum[:, 6, 0:B * E].rearrange("p (b e) -> p b e", b=B)))
            link(dve, stt(g["abs"], s, -1.0, s, ALU.mult, ALU.max))
            m = (gm1[:, :], gm2[:, :])

            def choose(values, best, chosen):
                link(dve, nc.vector.reduce_max(best, values, AX.X))
                link(dve, tt(g["rank"], values, per_elem(best, E), ALU.is_equal))
                link(dve, tt(g["rank"], g["rank"], rank, ALU.mult))
                link(dve, nc.vector.reduce_max(grm[:, :], g["rank"], AX.X))
                link(dve, tt(chosen, g["rank"], per_elem(grm[:, :], E), ALU.is_equal))
            choose(s, m[0], g["top1"])
            link(dve, stt(g["rest"], g["top1"], -3.0e38, s, ALU.mult, ALU.add))
            choose(g["rest"], m[1], g["top2"])
            for i in range(2):
                link(dve, tt(gdist[:, i, :, :], per_elem(m[i], E), s, ALU.subtract))
                link(dve, tt(gkeep[:, i, :, :], per_elem(m[i], E), g["abs"], ALU.max))
                link(dve, stt(gkeep[:, i, :, :], gkeep[:, i, :, :], 2 * JITTER, gdist[:, i, :, :], ALU.mult, ALU.is_ge))
            link(dve, tt(g["rest"], gkeep[:, 1, :, :], g["top1"], ALU.mult))
            link(dve, tt(gkeep[:, 1, :, :], gkeep[:, 1, :, :], g["rest"], ALU.subtract))
            nc.vector.tensor_scalar(gdist[:, :, :, :], gdist[:, :, :, :], 0.0, None, ALU.max).then_inc(gdist_ready, 1)
            tt(g["rest"], g["top1"], g["top2"], ALU.add).then_inc(chosen_ready, 1)
            dve.wait_ge(gexp_ready, 1)
            link(dve, tt(gexp[:, :, :, :], gexp[:, :, :, :], gkeep[:, :, :, :], ALU.mult))
            link(dve, nc.vector.reduce_sum(gsum[:, :, :], gexp[:, :, :, :], AX.X))
            link(dve, nc.vector.reciprocal(gsum[:, :, :], gsum[:, :, :]))
            link(dve, tt(g["top1"], g["top1"], per_elem(gsum[:, 0, :], E), ALU.mult))
            link(dve, tt(g["top2"], g["top2"], per_elem(gsum[:, 1, :], E), ALU.mult))
            tt(g["weight"], g["top1"], g["top2"], ALU.add).then_inc(acc_upd, 1)
            dve.wait_ge(pos_filled, 1)
            link(dve, tt(posm[:, :, :], psum[:, 7, 0:2 * E].rearrange("p (b e) -> p b e", b=B), g["rest"], ALU.mult))
            link(dve, nc.vector.tensor_scalar(posm[:, :, :], posm[:, :, :], -1.0, None, ALU.add))
            nc.vector.reduce_max(overfull[:, :], psum[:, 7, 2 * E:3 * E], AX.X).then_inc(overfull_known, 1)

        def experts_dve(dve):
            norm_dve(dve, 2)
            for i in range(4):
                nc.vector.memset(acc[:, i // 2, (i % 2) * T:(i % 2) * T + T], 0.0).then_inc(hid_free, 1)
            gates_dve(dve)
            dve.wait_ge(overfull_known, 1)
            most = dve.value_load(overfull[0:1, 0:1], min_val=0, max_val=T)
            with dve.If(most > P):
                dense_experts_dve(dve)
            with dve.Else():
                gathered_experts_dve(dve)
            dve.wait_ge(moe_added, 1)

        def dense_experts_dve(dve):
            with dve.Fori(0, E) as e:
                dve.wait_ge(acc_upd, e * B + 1)
                nc.vector.tensor_copy(wcur[:, :].unsqueeze(2), gt["weight"][:, :, ds(e, 1)]).then_inc(wcur_ready, 1)
                for u in range(FQ):
                    for f in range(4):
                        dve.wait_ge(silu_ready, e * FC + (4 * u + f + 1))
                        up_ready(dve, e, u, 1, f)
                        nc.vector.tensor_tensor(hid[u % 2][:, f, :], hsilu[:, f, :], psum[:, f, T:2 * T], ALU.mult).then_inc(hid_free, 1)
                dve.wait_ge(wcur_ready, e + 1)
                dve.wait_ge(blk_used, e * 12 + (BLK_MOE + 12))
                for b in range(B):
                    nc.vector.scalar_tensor_tensor(acc[:, b, :], psum[:, 4 + b, :], wcur[:, b:b + 1], acc[:, b, :],
                                                   ALU.mult, ALU.add).then_inc(acc_upd, 1)
            dve.wait_ge(acc_upd, B * E + 1)
            nc.vector.tensor_tensor(x_res[:, :, :], x_res[:, :, :], acc, ALU.add).then_inc(moe_added, 1)

        def gathered_experts_dve(dve):
            flat = lambda v: v.rearrange("p b e s -> p (b e) s")
            nc.vector.tensor_tensor(flat(sel), per_row(C_("iota"), B * E),
                                    per_elem(posm[:, :, :].rearrange("p b e -> p (b e)"), P), ALU.is_equal).then_inc(sel_ready, 1)
            dve.wait_ge(sel_ready, 1)
            nc.vector.tensor_tensor(flat(selw), flat(sel).bitcast(fp32), per_elem(gt["weight"][:, :, :].rearrange("p b e -> p (b e)"), P),
                                    ALU.mult).then_inc(sel_ready, 1)
            nc.vector.memset(accT, 0.0).then_inc(s_chain, 1)
            for n in range(4):
                dve.wait_ge(selT_filled, n + 1)
                nc.vector.tensor_copy(selT[:, 2 * n:2 * n + 2, :], psum[:, n, :].rearrange("p (e t) -> p e t", e=2)).then_inc(selT_ready, 1)
            dve.wait_ge(s_chain, 1)
            with dve.Fori(0, E) as e:
                for u in range(FQ):
                    for f in range(4):
                        dve.wait_ge(silu_ready, e * FC + (4 * u + f + 1))
                        up_ready(dve, e, u, 1, f)
                        nc.vector.tensor_tensor(shid[u % 2][:, f, :], ssilu[:, f, :], psum[:, f, T:T + P], ALU.mult).then_inc(hid_free, 1)
                dve.wait_ge(blk_used, e * 12 + (BLK_MOE + 12))
                nc.vector.tensor_copy(yexp, psum[:, 4, :]).then_inc(acc_upd, 1)
                dve.wait_ge(scatter_filled, e + 1)
                dve.wait_ge(acc_upd, e * 2 + 1)
                nc.vector.tensor_tensor(accT.rearrange("p (a c) t -> p a (c t)", a=2), accT.rearrange("p (a c) t -> p a (c t)", a=2),
                                        psum[:, 6:8, :], ALU.add).then_inc(acc_upd, 1)
            dve.wait_ge(accT_filled, 1)
            nc.vector.tensor_tensor(x_res[:, :, :], x_res[:, :, :], psum[:, 0:2, :], ALU.add).then_inc(moe_added, 1)

        qpT = view(16384, C, T)
        mem = view(17408, B, D)
        memT = view(18432, C, T)
        mkz = view(19456, B, 4, P)
        la = view(20480, B, H, P)
        laT = view(24576, B, H, P)
        x1oT = view(28672, C, T)
        mvt = sb("mvt", [P, B, DK])
        top8 = [sb(f"top8_{b}", [P, 8]) for b in range(B)]
        at8 = [sb(f"at8_{b}", [P, 8], u32) for b in range(B)]
        pick = [sb(f"pick{b}", [P, 1], u32) for b in range(B)]
        lm = sb("lm", [P, B, H])
        ls = sb("ls", [P, B, H])

        ctx_back = [sem(f"ctx_back{b}") for b in range(B)]
        qp_filled = sem("qp_filled")
        qp_ready = sem("qp_ready")
        pick_scores = sem("pick_scores")
        top_found = sem("top_found")
        at_found = sem("at_found")
        picked = sem("picked")
        mem_arrived = [sem(f"mem_arrived{b}") for b in range(B)]
        memT_filled = sem("memT_filled")
        memT_ready = sem("memT_ready")
        mk_filled = sem("mk_filled")
        mkz_ready = sem("mkz_ready")
        mv_filled = sem("mv_filled")
        mv_ready = sem("mv_ready")
        la_filled = sem("la_filled")
        la_shift = sem("la_shift")
        la_exp = sem("la_exp")
        la_ready = sem("la_ready")
        laT_filled = sem("laT_filled")
        laT_ready = sem("laT_ready")
        x1o_filled = sem("x1o_filled")
        x1o_ready = sem("x1o_ready")

        def cross1_pe(pe):
            norm_pe(pe, 3)
            need(pe, BLK_X1)
            for ec in range(C):
                for c in range(C):
                    last = nc.tensor.matmul(psum[:, 2 + ec // 2, (ec % 2) * T:(ec % 2) * T + T],
                                            block(BLK_X1)[:, c, ec * P:(ec + 1) * P], xnT[:, c, :],
                                            start=c == 0, stop=c == C - 1)
                if ec % 2:
                    last.then_inc(qp_filled if ec == 1 else blk_used, 1)
            pe.wait_ge(qp_ready, 2)
            for b in range(B):
                pe.wait_ge(ctx_back[b], KB * 16)
                for kb in range(KB):
                    for c in range(C):
                        last = nc.tensor.matmul(psum[:, 4 - 4 * b + kb, :], qpT[:, c, b * P:(b + 1) * P],
                                                ctxT_sb[b][:, c, kb * 512:(kb + 1) * 512], start=c == 0, stop=c == C - 1)
                last.then_inc(pick_scores, 1)
            pe.wait_ge(at_found, 1)
            for b in range(B):
                pe.wait_ge(mem_arrived[b], 16)
                for c in range(C):
                    last = nc.tensor.transpose(psum[:, 4 + b, c * P:(c + 1) * P], mem[:, b, c * P:(c + 1) * P], C_("ident"))
                last.then_inc(memT_filled, 1)
            pe.wait_ge(memT_ready, 2)
            for c in range(C):
                last = nc.tensor.matmul(psum[:, 6, 0:T], S_("x1_k")[:, c, :], memT[:, c, :], start=c == 0, stop=c == C - 1)
            last.then_inc(mk_filled, 1)
            for b in range(B):
                for c in range(C):
                    last = nc.tensor.matmul(psum[:, 7, b * DK:(b + 1) * DK], memT[:, c, b * P:(b + 1) * P],
                                            S_("x1_v")[:, c, :], start=c == 0, stop=c == C - 1)
            last.then_inc(mv_filled, 1)
            pe.wait_ge(at_found, 2)
            for b in range(B):
                pe.wait_ge(mkz_ready, b + 1)
                if b == 1:
                    pe.wait_ge(mv_ready, 1)
                for j in range(C):
                    last = nc.tensor.matmul(psum[:, 4 * b + j, :], qpT[:, j, b * P:(b + 1) * P], mkz[:, b, :, :],
                                            start=True, stop=True)
                last.then_inc(la_filled, 1)
            for b in range(B):
                pe.wait_ge(la_ready, b + 1)
                for j in range(C):
                    for i in range(4):
                        last = nc.tensor.transpose(psum[:, 4 * b + j, i * P:(i + 1) * P], la[:, b, 4 * j + i, :], C_("ident"))
                    last.then_inc(laT_filled, 1)
            for b in range(B):
                pe.wait_ge(laT_ready, C * (b + 1))
                for i in range(4):
                    last = nc.tensor.matmul(psum[DK * i:DK * i + DK, b, :], mvt[:, b, :],
                                            laT[:, b, :, :].rearrange("p (j i) q -> p j i q", i=4)[:, :, i, :],
                                            start=True, stop=True)
                last.then_inc(x1o_filled, 1)
            need(pe, BLK_X1 + 1)
            for b in range(B):
                pe.wait_ge(x1o_ready, b + 1)
                for c in range(C):
                    last = nc.tensor.matmul(psum[:, 2 + b, :], x1oT[:, c, b * P:(b + 1) * P], block(BLK_X1 + 1)[:, c, :],
                                            start=c == 0, stop=c == C - 1)
            last.then_inc(blk_used, 1)

        def cross1_act(act):
            norm_act(act, 3)
            for i in range(2):
                if i == 0:
                    act.wait_ge(qp_filled, 1)
                else:
                    act.wait_ge(blk_used, BLK_X1 + 1)
                nc.scalar.copy(qpT[:, 2 * i:2 * i + 2, :], psum[:, 2 + i, :].rearrange("p (c t) -> p c t", c=2)).then_inc(qp_ready, 1)
            for b in range(B):
                act.wait_ge(memT_filled, b + 1)
                nc.scalar.copy(memT[:, :, b * P:(b + 1) * P], bank4(4 + b)).then_inc(memT_ready, 1)
            act.wait_ge(mv_filled, 1)
            nc.scalar.copy(mvt[:, :, :], psum[:, 7, 0:B * DK].rearrange("p (b d) -> p b d", b=B)).then_inc(mv_ready, 1)
            for b in range(B):
                act.wait_ge(la_shift, b + 1)
                nc.scalar.activation(la[:, b, :, :], la[:, b, :, :], ACT.Exp, scale=float(1.0 / np.sqrt(DK).astype(np.float32))).then_inc(la_exp, 1)
            for n in range(B * C):
                act.wait_ge(laT_filled, n + 1)
                nc.scalar.copy(laT[:, n // C, 4 * (n % C):4 * (n % C) + 4, :], bank4(n)).then_inc(laT_ready, 1)
            for b in range(B):
                act.wait_ge(x1o_filled, b + 1)
                nc.scalar.copy(x1oT[:, :, b * P:(b + 1) * P], bank4(b)).then_inc(x1o_ready, 1)

        def cross1_dve(dve):
            norm_dve(dve, 3)
            for b in range(B):
                dve.wait_ge(pick_scores, b + 1)
                scores = psum[:, 4 - 4 * b:8 - 4 * b, :].rearrange("p a n -> p (a n)")
                nc.vector.max(top8[b][:, :], scores).then_inc(top_found, 1)
                dve.wait_ge(top_found, b + 1)
                nc.vector.max_index(at8[b][:, :], top8[b][:, :], scores).then_inc(at_found, 1)
                dve.wait_ge(at_found, b + 1)
                nc.vector.tensor_scalar(pick[b][:, :], at8[b][:, 0:1], b * CTX, None, ALU.add).then_inc(picked, 1)
            dve.wait_ge(mk_filled, 1)
            for b in range(B):
                nc.vector.tensor_tensor(mkz[:, b, :, :], per_row(psum[:, 6, b * P:(b + 1) * P], 4),
                                        per_elem(K_("headmask", 0, 4), P), ALU.mult).then_inc(mkz_ready, 1)
            for b in range(B):
                dve.wait_ge(la_filled, b + 1)
                logits = psum[:, 4 * b:4 * b + 4, :].rearrange("p j (i m) -> p (j i) m", i=4)
                link(dve, nc.vector.reduce_max(lm[:, b, :], logits, AX.X))
                nc.vector.tensor_tensor(la[:, b, :, :], logits, per_elem(lm[:, b, :], P), ALU.subtract).then_inc(la_shift, 1)
            for b in range(B):
                dve.wait_ge(la_exp, b + 1)
                link(dve, nc.vector.reduce_sum(ls[:, b, :], la[:, b, :, :], AX.X))
                link(dve, nc.vector.reciprocal(ls[:, b, :], ls[:, b, :]))
                nc.vector.tensor_tensor(la[:, b, :, :], la[:, b, :, :], per_elem(ls[:, b, :], P), ALU.mult).then_inc(la_ready, 1)
            dve.wait_ge(blk_used, BLK_X1 + 2)
            link(dve, nc.vector.tensor_tensor(x_res[:, :, :], x_res[:, :, :], psum[:, 2:4, :], ALU.add))

        lz = view(0, 3, C, T)
        le = view(3 * C * T, 2, C, T)
        lqk = view(5 * C * T, 2, C, T)
        lkv = view(7 * C * T, C * B, P)
        lden = view(8 * C * T, C * B, P)
        lvT = view(9 * C * T, C, T)
        ly = view(10 * C * T, B, D)
        lkvs = sb("lkvs", [P, C * B])
        lks = sb("lks", [P, C * B])

        LIN_Q_BANK = (2, 3, 4, 5)
        lin_filled = sem("lin_filled")
        lmin_ready = sem("lmin_ready")
        lexp_ready = sem("lexp_ready")
        lv_ready = sem("lv_ready")
        ly_ready = sem("ly_ready")
        lgelu = sem("lgelu")

        def linear_pe(pe):
            norm_pe(pe, 4)
            for m in range(3):
                need(pe, BLK_LIN + m)
                for cc in range(C):
                    out = psum[:, LIN_Q_BANK[cc], 0:T] if m == 2 else psum[:, 4 + 2 * m + cc // 2, (cc % 2) * T:(cc % 2) * T + T]
                    if m == 2 and cc == 2:
                        pe.wait_ge(lexp_ready, 1)
                    for c in range(C):
                        last = nc.tensor.matmul(out, block(BLK_LIN + m)[:, c, cc * P:(cc + 1) * P], xnT[:, c, :],
                                                start=c == 0, stop=c == C - 1)
                    last.then_inc(lin_filled if cc < C - 1 else blk_used, 1)
            need(pe, BLK_LIN + 3)
            for c in range(C):
                pe.wait_ge(lv_ready, c + 1)
                for b in range(B):
                    last = nc.tensor.matmul(psum[:, b, :], lvT[:, c, b * P:(b + 1) * P], block(BLK_LIN + 3)[:, c, :],
                                            start=c == 0, stop=c == C - 1)
                    if c == C - 1:
                        last.then_inc(lin_filled if b == 0 else blk_used, 1)

        def linear_act(act):
            norm_act(act, 4)
            act.wait_ge(lmin_ready, 1)
            nc.scalar.activation(le[:, 0, :, :], le[:, 0, :, :], ACT.Exp).then_inc(lexp_ready, 1)
            for cc in range(C):
                act.wait_ge(lmin_ready, cc + 2)
                nc.scalar.activation(le[:, 1, cc, :], le[:, 1, cc, :], ACT.Exp).then_inc(lexp_ready, 1)
            split_hi(act, 0)
            for b in range(B):
                act.wait_ge(ly_ready, b + 1)
                nc.scalar.activation(ly[:, b, :], ly[:, b, :], ACT.Gelu_apprx_tanh).then_inc(lgelu, 1)

        def linear_dve(dve):
            norm_dve(dve, 4)
            for m in range(2):
                for cc in range(C):
                    if cc == 0:
                        dve.wait_ge(lin_filled, 3 * m + 2)
                    if cc == 2:
                        dve.wait_ge(blk_used, BLK_LIN + m + 1)
                    ins = nc.vector.tensor_scalar(lz[:, m, cc, :], psum[:, 4 + 2 * m + cc // 2, (cc % 2) * T:(cc % 2) * T + T],
                                                  K_("lin_b", m * C + cc), None, ALU.add)
                link(dve, ins)
                if m == 0:
                    nc.vector.tensor_scalar(le[:, 0, :, :], lz[:, 0, :, :], 0.0, None, ALU.min).then_inc(lmin_ready, 1)
                    dve.wait_ge(lexp_ready, 1)
                    link(dve, nc.vector.scalar_tensor_tensor(lqk[:, 0, :, :], lz[:, 0, :, :], 0.0, le[:, 0, :, :], ALU.max, ALU.add))
                    k8 = lqk[:, 0, :, :].rearrange("p c (b t) -> p (c b) t", b=B)
                    link(dve, nc.vector.reduce_sum(lks[:, :], k8, AX.X))
            v8 = lz[:, 1, :, :].rearrange("p c (b t) -> p (c b) t", b=B)
            link(dve, nc.vector.tensor_tensor(lkv, k8, v8, ALU.mult))
            link(dve, nc.vector.reduce_sum(lkvs[:, :], lkv, AX.X))

            def query_in(cc):
                if cc < C - 1:
                    dve.wait_ge(lin_filled, 6 + cc + 1)
                else:
                    dve.wait_ge(blk_used, BLK_LIN + 3)
                link(dve, nc.vector.tensor_scalar(lz[:, 2, cc, :], psum[:, LIN_Q_BANK[cc], 0:T], K_("lin_b", 2 * C + cc), None, ALU.add))
                nc.vector.tensor_scalar(le[:, 1, cc, :], lz[:, 2, cc, :], 0.0, None, ALU.min).then_inc(lmin_ready, 1)

            query_in(0)
            for cc in range(C):
                if cc + 1 < C:
                    query_in(cc + 1)
                dve.wait_ge(lexp_ready, cc + 2)
                q = lqk[:, 1, cc, :]
                link(dve, nc.vector.scalar_tensor_tensor(q, lz[:, 2, cc, :], 0.0, le[:, 1, cc, :], ALU.max, ALU.add))
                den = lden.rearrange("p (c b) t -> p c (b t)", c=C)[:, cc, :]
                for b in range(B):
                    i, t = cc * B + b, slice(b * P, (b + 1) * P)
                    ins = nc.vector.tensor_scalar(den[:, t], q[:, t], lks[:, i:i + 1], 1e-6, ALU.mult, ALU.add)
                link(dve, ins)
                link(dve, nc.vector.reciprocal(den, den))
                for b in range(B):
                    i, t = cc * B + b, slice(b * P, (b + 1) * P)
                    ins = nc.vector.scalar_tensor_tensor(lvT[:, cc, t], q[:, t], lkvs[:, i:i + 1], den[:, t], ALU.mult, ALU.mult)
                ins.then_inc(lv_ready, 1)
            for b in range(B):
                if b == 0:
                    dve.wait_ge(lin_filled, 10)
                else:
                    dve.wait_ge(blk_used, BLK_LIN + 4)
                nc.vector.tensor_tensor(ly[:, b, :], psum[:, b, :], R_("lin_bo"), ALU.add).then_inc(ly_ready, 1)
            split_lo(dve, 0)
            for b in range(B):
                dve.wait_ge(lgelu, b + 1)
                ins = nc.vector.tensor_tensor(x_res[:, b, :], x_res[:, b, :], ly[:, b, :], ALU.add)
            link(dve, ins)

        o = 0
        heven = [view(o + i * FC * T, FC, T, one_pass=True) for i in range(2)]
        o += 2 * FC * T
        hodd = [view(o + i * FC * T, FC, T, one_pass=True) for i in range(2)]
        o += 2 * FC * T
        fxT = [view(o + i * C * T, C, T, one_pass=True) for i in range(2)]
        o += 2 * C * T
        whi = [view(o + i * BLK, BLK, one_pass=True) for i in range(2)]
        o += 2 * BLK
        wlo = [view(o + i * BLK, BLK, one_pass=True) for i in range(2)]
        o += 2 * BLK
        fsilu = view(o, 4, T)
        o += 4 * T
        fhid = view(o, 4, T)
        o += 4 * T
        fy = view(o, B, D)
        NFFN = NBLK - BLK_W12
        w_hi = sem("w_hi")
        w_lo = sem("w_lo")
        ffn_filled = sem("ffn_filled")
        ffn_act = sem("ffn_act")
        ffn_hi = sem("ffn_hi")
        ffn_lo = sem("ffn_lo")

        def split_hi(act, j, reg=None):
            k = BLK_W12 + j
            if reg is None:
                act.wait_ge(blk_arrived[k % RING], 16 * (k // RING + 1))
                if j >= 2:
                    act.wait_ge(blk_used, k - 1)
            else:
                act.wait_ge(blk_arrived[k % RING], reg * 16 + 16 * (k // RING + 1))
                act.wait_ge(blk_used, reg * RING + (k - 1))
            nc.scalar.copy(whi[j % 2], ring[k % RING][:, :]).then_inc(w_hi, 1)

        def split_lo(dve, j, reg=None):
            dve.wait_ge(w_hi, j + 1 if reg is None else reg * RING + (j + 1))
            nc.vector.tensor_tensor(wlo[j % 2], ring[(BLK_W12 + j) % RING][:, :], whi[j % 2].bitcast(fp32),
                                    ALU.subtract).then_inc(w_lo, 1)

        def parts_ready(pe, j, reg=None):
            pe.wait_ge(w_hi, j + 1 if reg is None else reg * RING + (j + 1))
            pe.wait_ge(w_lo, j + 1 if reg is None else reg * RING + (j + 1))

        def ffn_pe(pe):
            for b in range(B):
                pe.wait_ge(xn_ready, 2 * 5 + b + 1)
                for c in range(C):
                    last = nc.tensor.transpose(psum[:, b, c * P:(c + 1) * P], xn[:, b, c * P:(c + 1) * P], C_("ident"))
                last.then_inc(xnT_filled, 1)
            pe.wait_ge(norm_hi, B + 1)
            pe.wait_ge(norm_lo, B + 1)
            for n in range(FC):
                j, f = n // 2, n % 4
                if n % 2 == 0:
                    parts_ready(pe, j)
                    w = [v[j % 2].rearrange("p (c i n) -> p c i n", c=C, i=2) for v in (whi, wlo)]
                if n >= 4:
                    pe.wait_ge(ffn_lo, n - 3)
                for i in range(2):
                    for c in range(C):
                        for wp, xp in PARTS:
                            last = nc.tensor.matmul(psum[:, f, i * T:(i + 1) * T], w[wp][:, c, i, (n % 2) * P:(n % 2 + 1) * P],
                                                    fxT[xp][:, c, :], start=c == wp == xp == 0, stop=c == C - 1 and wp == 1)
                last.then_inc(blk_used if n % 2 else ffn_filled, 1)
            for layer, src in enumerate((heven, hodd)):
                j0 = FC // 2 + layer * FC
                with pe.Fori(0, FC // RING) as it:
                    for s in range(RING):
                        j = j0 + s
                        parts_ready(pe, j, it)
                        w = [v[j % 2].rearrange("p (c n) -> p c n", c=FC) for v in (whi, wlo)]
                        pe.wait_ge(ffn_act, it * RING + (FC * (layer + 1) + s - 3))
                        for c in range(FC):
                            if c == 0:
                                pe.wait_ge(ffn_lo, FC * (layer + 1) - 1)
                            if c == FC - 1:
                                pe.wait_ge(ffn_lo, FC * (layer + 1))
                            for wp, xp in PARTS:
                                last = nc.tensor.matmul(psum[:, 4 + s, 0:T], w[wp][:, c, :], src[xp][:, c, :],
                                                        start=c == wp == xp == 0, stop=c == FC - 1 and wp == 1)
                        last.then_inc(blk_used, 1)
            for n in range(FC):
                j = NFFN - FQ + n // 4
                if n % 4 == 0:
                    parts_ready(pe, j)
                    w = [v[j % 2].rearrange("p (c n) -> p c n", c=4) for v in (whi, wlo)]
                if n in (0, FC - 1):
                    pe.wait_ge(ffn_lo, 3 * FC - (n == 0))
                for b in range(B):
                    for wp, xp in PARTS:
                        last = nc.tensor.matmul(psum[:, b, :], heven[xp][:, n, b * P:(b + 1) * P], w[wp][:, n % 4, :],
                                                start=n == wp == xp == 0, stop=n == FC - 1 and wp == 1)
                if n % 4 == 3:
                    last.then_inc(blk_used, 1)

        def ffn_scalar(act):
            norm_std_act(act, 5)
            split_hi(act, 1)
            for b in range(B):
                act.wait_ge(xnT_filled, 2 * 5 + b + 1)
                nc.scalar.copy(fxT[0][:, :, b * P:(b + 1) * P], psum[:, b, :].rearrange("p (c t) -> p c t", c=C)).then_inc(norm_hi, 1)
            for n in range(FC):
                j, f = n // 2, n % 4
                if n % 2:
                    split_hi(act, j + 2)
                act.wait_ge(blk_used if n % 2 else ffn_filled, BLK_W12 + j + 1 if n % 2 else j + 1)
                nc.scalar.activation(fsilu[:, f, :], psum[:, f, 0:T], ACT.Silu, scale=K_("w1_s", n)).then_inc(ffn_act, 1)
            for layer, (dst, name) in enumerate(((hodd, "h1_s"), (heven, "h2_s"))):
                j0, done = FC // 2 + layer * FC, FC * (layer + 1)
                with act.Fori(0, FC // RING) as it:
                    for s in range(RING):
                        split_hi(act, j0 + s + 2, it)
                        act.wait_ge(ffn_lo, it * RING + (done + s - 3))
                        act.wait_ge(blk_used, it * RING + (BLK_W12 + j0 + s + 1))
                        nc.scalar.activation(fhid[:, s:s + 1, :], psum[:, 4 + s, 0:T].unsqueeze(1), ACT.Gelu,
                                             scale=col[:, ds(it * RING + (COLS[name][0] + s), 1)]).then_inc(ffn_act, 1)
                        act.wait_ge(ffn_act, it * RING + (done + s + 1))
                        nc.scalar.copy(dst[0][:, ds(it * RING + s, 1), :], fhid[:, s:s + 1, :]).then_inc(ffn_hi, 1)
            for j in (NFFN - 2, NFFN - 1):
                split_hi(act, j)

        def ffn_dve(dve):
            norm_stats_dve(dve, 5)
            split_lo(dve, 1)
            for b in range(B):
                dve.wait_ge(norm_hi, b + 2)
                nc.vector.tensor_tensor(fxT[1][:, :, b * P:(b + 1) * P], psum[:, b, :].rearrange("p (c t) -> p c t", c=C),
                                        fxT[0][:, :, b * P:(b + 1) * P].bitcast(fp32), ALU.subtract).then_inc(norm_lo, 1)
            for n in range(FC):
                f = n % 4
                if n % 2:
                    split_lo(dve, n // 2 + 2)
                dve.wait_ge(ffn_act, n + 1)
                link(dve, nc.vector.scalar_tensor_tensor(fhid[:, f, :], psum[:, f, T:2 * T], K_("w2_s", n), fsilu[:, f, :],
                                                         ALU.mult, ALU.mult))
                link(dve, nc.vector.tensor_copy(heven[0][:, n, :], fhid[:, f, :]))
                nc.vector.tensor_tensor(heven[1][:, n, :], fhid[:, f, :], heven[0][:, n, :].bitcast(fp32),
                                        ALU.subtract).then_inc(ffn_lo, 1)
            for layer, dst in enumerate((hodd, heven)):
                j0 = FC // 2 + layer * FC
                with dve.Fori(0, FC // RING) as it:
                    for s in range(RING):
                        split_lo(dve, j0 + s + 2, it)
                        dve.wait_ge(ffn_hi, it * RING + (layer * FC + s + 1))
                        nc.vector.tensor_tensor(dst[1][:, ds(it * RING + s, 1), :], fhid[:, s:s + 1, :],
                                                dst[0][:, ds(it * RING + s, 1), :].bitcast(fp32), ALU.subtract).then_inc(ffn_lo, 1)
            for j in (NFFN - 2, NFFN - 1):
                split_lo(dve, j)
            dve.wait_ge(blk_used, NBLK)
            link(dve, nc.vector.tensor_tensor(fy, psum[:, 0:2, :], per_row(R_("w3_s"), B), ALU.mult))
            nc.vector.tensor_tensor(x_res[:, :, :], x_res[:, :, :], fy, ALU.add).then_inc(x_final, 1)

        block_ = ctx.enter_context(nc.Block())

        @block_.sync
        def _(sp):
            def load_wk(hp):
                sp.dma_start(wk_in, wk[ds(hp, 1)].rearrange("a p (c n) -> p (a c) n", c=C)).then_inc(wk_arrived, 16)

            def load_wq(hp):
                sp.dma_start(wq_sb, wq[ds(hp, 1)].rearrange("a p (c n) -> p (a c) n", c=C)).then_inc(wq_arrived, 16)

            def load_wv(g):
                sp.dma_start(wv_in, wv[ds(g, 1)].rearrange("a p (c n) -> p (a c) n", c=C)).then_inc(wv_arrived, 16)

            def load_ctx(b, kb):
                k = slice(kb * 512, (kb + 1) * 512)
                sp.dma_start(cx_in[:, :, k], ctxT[b][:, :, k]).then_inc(ctx_arrived[kb], 16)

            def next_weights(n, hp, m=None, g=None, next_ctx=False):
                sp.wait_ge(kq_filled, n * 5 + 4)
                load_wk(hp)
                if m is not None:
                    sp.wait_ge(v_filled, m * 8 + 8)
                    if next_ctx:
                        load_ctx(1, 0)
                    load_wv(g)
                    if next_ctx:
                        for kb in range(1, KB):
                            load_ctx(1, kb)
                sp.wait_ge(kq_filled, n * 5 + 5)
                load_wq(hp)

            sp.dma_start(x_res[:, :, :], x).then_inc(x_loaded, 16)
            sp.dma_start(col[:, :], cols).then_inc(x_loaded, 16)
            load_wk(0)
            load_ctx(0, 0)
            load_ctx(0, 1)
            sp.dma_start(cst[:, :], consts).then_inc(cst_loaded, 16)
            load_ctx(0, 2)
            load_ctx(0, 3)
            load_wq(0)
            load_wv(0)
            sp.dma_start(row[:, :], rows.partition_broadcast(P)).then_inc(loaded, 16)
            sp.dma_start(sml[:, :], small).then_inc(loaded, 16)
            next_weights(0, 1)
            for b in range(B):
                with sp.Fori(0, PAIRS // 2 - 1) as g:
                    j, m = g * 2 + PAIRS * b, g + PAIRS // 2 * b
                    next_weights(j + 1, g * 2 + 2, m, g + 1)
                    next_weights(j + 2, g * 2 + 3)
                if b == 0:
                    next_weights(PAIRS - 1, 0, PAIRS // 2 - 1, 0, next_ctx=True)
                    next_weights(PAIRS, 1)
            sp.wait_ge(v_filled, 8 * PAIRS)
            sp.wait_ge(kq_filled, 5 * 2 * PAIRS)
            sp.dma_start(wo_sb, wo.rearrange("p (c n) -> p c n", c=PAIRS)).then_inc(wo_arrived, 16)
            sp.wait_ge(scores_ready, 8 * PAIRS)
            dma_block(sp, 0, 0)
            dma_block(sp, 1, 1)
            sp.wait_ge(pv_done, 2 * PAIRS)
            dma_block(sp, 2, 2)
            dma_block(sp, 3, 3)
            for k in range(RING, BLK_MOE):
                dma_block(sp, k, k, used=k - RING + 1)
            with sp.Fori(0, E) as e:
                for i in range(3 * FQ):
                    dma_block(sp, ds(e * 12 + (BLK_MOE + i), 1), BLK_MOE + i, used=e * 12 + (BLK_MOE + i - RING + 1))
            turns = (NBLK - BLK_X1) // RING
            with sp.Fori(0, turns) as i:
                for s in range(RING):
                    dma_block(sp, ds(i * RING + (BLK_X1 + s), 1), BLK_X1 + s, used=i * RING + (BLK_X1 + s - RING + 1))
            for k in range(BLK_X1 + turns * RING, NBLK):
                dma_block(sp, k, k, used=k - RING + 1)
            sp.wait_ge(x_final, 1)
            sp.dma_start(out, x_res[:, :, :]).then_inc(stored, 16)
            sp.wait_ge(stored, 16)

        @block_.gpsimd
        def _(gp):
            mixer_pool(gp)
            gp.wait_ge(norm_hi, 1)
            nc.gpsimd.tensor_tensor(xn_parts[1], xn[:, :, :], xn_parts[0].bitcast(fp32), ALU.subtract).then_inc(norm_lo, 1)
            for b in range(B):
                for kb in range(KB):
                    gp.wait_ge(blk_used, BLK_MOE + 3 * FQ + 9 * (b * KB + kb))
                    k = slice(kb * 512, (kb + 1) * 512)
                    gp.dma_start(ctxT_sb[b][:, :, k], ctxT[b][:, :, k]).then_inc(ctx_back[b], 16)
            for b in range(B):
                gp.wait_ge(picked, b + 1)
                gp.indirect_dma_start(out=mem[:, b, :], out_offset=None, in_=ctx_rows,
                                      in_offset=bass.IndirectOffsetOnAxis(ap=pick[b][:, :], axis=0)).then_inc(mem_arrived[b], 16)

        @block_.scalar
        def _(act):
            cross0_act(act)
            mixer_act(act)
            experts_act(act)
            cross1_act(act)
            linear_act(act)
            ffn_scalar(act)

        @block_.vector
        def _(dve):
            cross0_dve(dve)
            mixer_dve(dve)
            experts_dve(dve)
            cross1_dve(dve)
            linear_dve(dve)
            ffn_dve(dve)

        @block_.tensor
        def _(pe):
            cross0_pe(pe)
            mixer_pe(pe)
            experts_pe(pe)
            cross1_pe(pe)
            linear_pe(pe)
            ffn_pe(pe)


def _rows_to_partitions(w):
    n = w.shape[0] // P
    return w.reshape(n, P, w.shape[1]).transpose(1, 0, 2).reshape(P, n * w.shape[1])


def _columns(v):
    return v.reshape(-1, P).T


def _stream_blocks(a):
    def quarters(w):
        return [w[:, q * 512:(q + 1) * 512] for q in range(w.shape[1] // 512)]

    def row_quarters(w):
        return [w[q * 512:(q + 1) * 512] for q in range(w.shape[0] // 512)]

    mats = [a["L0_attn_" + n] for n in ("Wq", "Wk", "Wv", "Wg", "Wo")]
    for e in range(E):
        for w1, w3, w2 in zip(quarters(a["L0_ffn_w1"][e].T), quarters(a["L0_ffn_w3"][e].T),
                              row_quarters(a["L0_ffn_w2"][e].T)):
            mats += [w1, w3, w2]
    mats += [a["L1_xattn_Wq"].T, a["L1_xattn_Wc"].T]
    mats += [a["L1_attn_" + n] for n in ("Wk", "Wv", "Wq", "Wo")]
    w1, w2 = a["L1_ffn_w1_w"].T, a["L1_ffn_w2_w"].T
    mats += [np.concatenate([w1[:, f:f + 2 * P], w2[:, f:f + 2 * P]], axis=1) for f in range(0, F, 2 * P)]
    for n in ("h1", "h2"):
        w = a[f"L1_ffn_{n}_w"].T
        mats += [w[:, f * P:(f + 1) * P] for f in range(FC)]
    mats += row_quarters(a["L1_ffn_w3_w"].T)
    return np.stack([_rows_to_partitions(m) for m in mats])


def kernel(**inputs):
    import concourse.bacc as _bacc
    from concourse.bass_utils import run_bass_kernel_spmd as _run

    a = {k: np.asarray(v) for k, v in inputs.items()}
    f32 = np.float32
    wq, wk = [np.stack([_rows_to_partitions(a["L0_xattn_W" + m][:, hp * P:(hp + 1) * P]) for hp in range(PAIRS)])
              for m in "qk"]
    wv = np.stack([_rows_to_partitions(a["L0_xattn_Wv"][:, g * T:(g + 1) * T]) for g in range(PAIRS // 2)])
    convw = np.stack([a[f"L0_attn_conv_{m}_w"].reshape(C, P, TAPS) for m in "qkv"]).transpose(2, 0, 1, 3).reshape(P, -1)
    headmask = (np.arange(P)[:, None] // DK == np.arange(4)[None, :]).astype(f32)
    rank = np.broadcast_to(np.arange(E, 0, -1).astype(f32), (P, E))
    cols = np.concatenate([_columns(a["L0_xattn_bq"]), _columns(a["L0_xattn_bk"]), _columns(a["L0_xattn_bv"]), convw,
                           _columns(a["L1_attn_bk"]), _columns(a["L1_attn_bv"]), _columns(a["L1_attn_bq"])]
                          + [_columns(a[f"L1_ffn_{n}_s"]) for n in ("w1", "w2", "h1", "h2")] + [headmask, rank], axis=1)
    rows = np.concatenate([a[n] for n in ("L0_xattn_bo", "L0_xattn_ln_gamma", "L0_xattn_ln_beta", "L0_attn_dt_bias",
                                          "L0_attn_bb", "L0_attn_A_log", "L0_attn_gnorm_w", "L1_attn_bo",
                                          "L1_ffn_w3_s")])
    wkv = a["L1_xattn_Wkv"]
    small = np.concatenate([_rows_to_partitions(m) for m in (
        np.concatenate([a["L0_attn_Wgk"], a["L0_attn_Wb"]], axis=1), a["L0_ffn_gate_w"].T,
        np.concatenate([wkv[:DK].T] * 4, axis=1), wkv[DK:].T)], axis=1)
    ctx = a["ctx_1024"]
    arrays = {
        "x": a["x"].transpose(1, 0, 2),
        "ctxT": ctx.transpose(0, 2, 1).reshape(B, C, P, CTX).transpose(0, 2, 1, 3),
        "ctx_rows": ctx.reshape(B * CTX, D),
        "wq": wq, "wk": wk, "wv": wv, "wo": _rows_to_partitions(a["L0_xattn_Wo"]), "stream": _stream_blocks(a), "small": small, "cols": cols, "rows": rows, "consts": constants(),
    }
    nc = _bacc.Bacc("TRN2", target_bir_lowering=False, num_devices=1)
    arrays = {f"in_{n}": np.ascontiguousarray(v) for n, v in arrays.items()}
    args = [nc.dram_tensor(n, v.shape, mybir.dt.from_np(v.dtype), kind="ExternalInput").ap() for n, v in arrays.items()]
    out = nc.dram_tensor("out", (P, B, D), mybir.dt.float32, kind="ExternalOutput").ap()
    build(nc, *args, out)
    r = _run(nc, [arrays], core_ids=[0])
    return r.results[0]["out"].transpose(1, 0, 2)
```
